# Optimizing a Trainium2 kernel written in Bass

```python
import numpy as np
import jax
import jax.numpy as jnp

def _softmax(x, axis=-1):
    return jax.nn.softmax(x, axis=axis)

def _gelu(x):
    return jax.nn.gelu(x, approximate=True)

def _silu(x):
    return jax.nn.silu(x)

def _sigmoid(x):
    return jax.nn.sigmoid(x)

def _layernorm(x, axis=-1, eps=1e-05):
    m = jnp.mean(x, axis=axis, keepdims=True)
    v = jnp.var(x, axis=axis, keepdims=True)
    return (x - m) / jnp.sqrt(v + eps)

def _scatter_add(tgt, idx, src, axis=0):
    return tgt.at[idx].add(src)

def _segment_sum(src, seg, n):
    return jax.ops.segment_sum(src, seg, n)
kernel_name = 'mk_gps_d1_gnn_r8_5d84ed'

def setup_inputs(seed: int=0):
    np.random.seed(seed)
    _w = jnp.asarray

    def _rec_inputs():
        import jax
        import jax.numpy as jnp
        _gk = jax.random.key(seed)
        x = -0.0003713 + 1 * jax.random.normal(jax.random.fold_in(_gk, 1), (6250, 256), jnp.float32)
        _s = jax.random.randint(jax.random.fold_in(_gk, 2), (100000,), 0, 6250, jnp.int32)
        _d = jax.random.randint(jax.random.fold_in(_gk, 3), (100000,), 0, 6250, jnp.int32)
        _loop = jnp.arange(6250, dtype=jnp.int32)
        src = jnp.concatenate([_s, _d, _loop])
        dst = jnp.concatenate([_d, _s, _loop])
        _o = jnp.argsort(dst, stable=True)
        src = src[_o]
        dst = dst[_o]
        edge_weight = jax.random.uniform(jax.random.fold_in(_gk, 12), (206250,), jnp.float32, 0.0, 0.999998)
        return (x, src, dst, edge_weight)
    x, src, dst, edge_weight = _rec_inputs()

    def _L0_gnn_setup():
        import jax, jax.numpy as jnp
        import numpy as np
        EPS = 1e-05

        def _bn(x, gamma, beta):
            m = jnp.mean(x, axis=0)
            v = jnp.mean((x - m) ** 2, axis=0)
            return gamma * (x - m) * jax.lax.rsqrt(v + EPS) + beta

        def _hconv(x, src, dst, ew, w1, b1, w2, b2, g, b):
            h = jax.nn.relu(x @ w1 + b1)
            msg = ew[:, None] * h[src]
            agg = jax.ops.segment_sum(msg, dst, num_segments=x.shape[0])
            h = agg @ w2 + b2
            return jax.nn.relu(_bn(h, g, b))
        N, C, E = (6250, 256, 37500)
        key = jax.random.key(seed)
        ks = jax.random.split(key, 16)
        s = 1.0 / np.sqrt(C)
        inp = {'x': jax.random.normal(ks[0], (N, C), dtype=jnp.float32), 'hyperedge_index': jax.random.randint(ks[1], (2, E), 0, N, dtype=jnp.int32), 'hyperedge_weight': jax.random.uniform(ks[2], (E,), dtype=jnp.float32), 'c1_w1': jax.random.normal(ks[3], (C, C), dtype=jnp.float32) * s, 'c1_b1': jnp.zeros((C,), jnp.float32), 'c1_w2': jax.random.normal(ks[4], (C, C), dtype=jnp.float32) * s, 'c1_b2': jnp.zeros((C,), jnp.float32), 'c1_g': jnp.ones((C,), jnp.float32), 'c1_b': jnp.zeros((C,), jnp.float32), 'bn1_g': jnp.ones((C,), jnp.float32), 'bn1_b': jnp.zeros((C,), jnp.float32), 'c2_w1': jax.random.normal(ks[5], (C, C), dtype=jnp.float32) * s, 'c2_b1': jnp.zeros((C,), jnp.float32), 'c2_w2': jax.random.normal(ks[6], (C, C), dtype=jnp.float32) * s, 'c2_b2': jnp.zeros((C,), jnp.float32), 'c2_g': jnp.ones((C,), jnp.float32), 'c2_b': jnp.zeros((C,), jnp.float32), 'bn2_g': jnp.ones((C,), jnp.float32), 'bn2_b': jnp.zeros((C,), jnp.float32)}
        return inp
    _L0_gnn_all = _L0_gnn_setup()
    _L0_gnn_in = {k: v for k, v in _L0_gnn_all.items() if k in ('c1_w1', 'c1_b1', 'c1_w2', 'c1_b2', 'c1_g', 'c1_b', 'bn1_g', 'bn1_b', 'c2_w1', 'c2_b1', 'c2_w2', 'c2_b2', 'c2_g', 'c2_b', 'bn2_g', 'bn2_b')}
    del _L0_gnn_all

    def _L0_mix_setup():
        import jax, jax.numpy as jnp
        import numpy as np
        HEADS = 8
        DIM_HEAD = 64
        EPS = 1e-05

        def _inst_norm(t):
            mu = jnp.mean(t, axis=-1, keepdims=True)
            var = jnp.var(t, axis=-1, keepdims=True)
            return (t - mu) / jnp.sqrt(var + EPS)
        key = jax.random.key(seed)
        k1, k2, k3, k4 = jax.random.split(key, 4)
        b, n, dim = (4, 1024, 256)
        inner = HEADS * DIM_HEAD
        x = jax.random.normal(k1, (b, n, dim), dtype=jnp.float32)
        w_qkv = jax.random.normal(k2, (dim, 3 * inner), dtype=jnp.float32) * (1.0 / DIM_HEAD)
        w_out = jax.random.normal(k3, (inner, dim), dtype=jnp.float32) * dim ** (-0.5)
        b_out = jax.random.normal(k4, (dim,), dtype=jnp.float32) * 0.01
        return {'x': x, 'w_qkv': w_qkv, 'w_out': w_out, 'b_out': b_out}
    _L0_mix_all = _L0_mix_setup()
    _L0_mix_in = {k: v for k, v in _L0_mix_all.items() if k in ('w_qkv', 'w_out', 'b_out')}
    del _L0_mix_all

    def _L0_ffn_setup():
        import jax, jax.numpy as jnp
        import numpy as np
        TOP_K = 2
        LN_EPS = 1e-05
        key = jax.random.key(seed)
        ks = jax.random.split(key, 8)
        B, S, D, E, H = (16, 1024, 256, 8, 1024)
        x = jax.random.normal(ks[0], (B, S, D), dtype=jnp.float32)
        Wr = jax.random.normal(ks[1], (D, E), dtype=jnp.float32) * 0.1
        br = jnp.zeros((E,), dtype=jnp.float32)
        ln_g = jnp.ones((E, D), dtype=jnp.float32)
        ln_b = jnp.zeros((E, D), dtype=jnp.float32)
        W1 = jax.random.normal(ks[2], (E, D, H), dtype=jnp.float32) * (1.0 / np.sqrt(D))
        b1 = jnp.zeros((E, H), dtype=jnp.float32)
        W2 = jax.random.normal(ks[3], (E, H, D), dtype=jnp.float32) * (1.0 / np.sqrt(H))
        b2 = jnp.zeros((E, D), dtype=jnp.float32)
        return {'x': x, 'Wr': Wr, 'br': br, 'ln_g': ln_g, 'ln_b': ln_b, 'W1': W1, 'b1': b1, 'W2': W2, 'b2': b2}
    _L0_ffn_all = _L0_ffn_setup()
    _L0_ffn_in = {k: v for k, v in _L0_ffn_all.items() if k in ('Wr', 'br', 'ln_g', 'ln_b', 'W1', 'b1', 'W2', 'b2')}
    del _L0_ffn_all
    return {'x': x, 'src': src, 'dst': dst, 'edge_weight': edge_weight, 'L0_gnn_c1_w1': _L0_gnn_in['c1_w1'], 'L0_gnn_c1_b1': _L0_gnn_in['c1_b1'], 'L0_gnn_c1_w2': _L0_gnn_in['c1_w2'], 'L0_gnn_c1_b2': _L0_gnn_in['c1_b2'], 'L0_gnn_c1_g': _L0_gnn_in['c1_g'], 'L0_gnn_c1_b': _L0_gnn_in['c1_b'], 'L0_gnn_bn1_g': _L0_gnn_in['bn1_g'], 'L0_gnn_bn1_b': _L0_gnn_in['bn1_b'], 'L0_gnn_c2_w1': _L0_gnn_in['c2_w1'], 'L0_gnn_c2_b1': _L0_gnn_in['c2_b1'], 'L0_gnn_c2_w2': _L0_gnn_in['c2_w2'], 'L0_gnn_c2_b2': _L0_gnn_in['c2_b2'], 'L0_gnn_c2_g': _L0_gnn_in['c2_g'], 'L0_gnn_c2_b': _L0_gnn_in['c2_b'], 'L0_gnn_bn2_g': _L0_gnn_in['bn2_g'], 'L0_gnn_bn2_b': _L0_gnn_in['bn2_b'], 'L0_mix_w_qkv': _L0_mix_in['w_qkv'], 'L0_mix_w_out': _L0_mix_in['w_out'], 'L0_mix_b_out': _L0_mix_in['b_out'], 'L0_ffn_Wr': _L0_ffn_in['Wr'], 'L0_ffn_br': _L0_ffn_in['br'], 'L0_ffn_ln_g': _L0_ffn_in['ln_g'], 'L0_ffn_ln_b': _L0_ffn_in['ln_b'], 'L0_ffn_W1': _L0_ffn_in['W1'], 'L0_ffn_b1': _L0_ffn_in['b1'], 'L0_ffn_W2': _L0_ffn_in['W2'], 'L0_ffn_b2': _L0_ffn_in['b2']}

def reference(x, src, dst, edge_weight, L0_gnn_c1_w1, L0_gnn_c1_b1, L0_gnn_c1_w2, L0_gnn_c1_b2, L0_gnn_c1_g, L0_gnn_c1_b, L0_gnn_bn1_g, L0_gnn_bn1_b, L0_gnn_c2_w1, L0_gnn_c2_b1, L0_gnn_c2_w2, L0_gnn_c2_b2, L0_gnn_c2_g, L0_gnn_c2_b, L0_gnn_bn2_g, L0_gnn_bn2_b, L0_mix_w_qkv, L0_mix_w_out, L0_mix_b_out, L0_ffn_Wr, L0_ffn_br, L0_ffn_ln_g, L0_ffn_ln_b, L0_ffn_W1, L0_ffn_b1, L0_ffn_W2, L0_ffn_b2):
    import jax
    import jax.numpy as jnp

    def _L0_gnn_ref(x, hyperedge_index, hyperedge_weight, c1_w1, c1_b1, c1_w2, c1_b2, c1_g, c1_b, bn1_g, bn1_b, c2_w1, c2_b1, c2_w2, c2_b2, c2_g, c2_b, bn2_g, bn2_b):
        import jax, jax.numpy as jnp
        import numpy as np
        EPS = 1e-05

        def _bn(x, gamma, beta):
            m = jnp.mean(x, axis=0)
            v = jnp.mean((x - m) ** 2, axis=0)
            return gamma * (x - m) * jax.lax.rsqrt(v + EPS) + beta

        def _hconv(x, src, dst, ew, w1, b1, w2, b2, g, b):
            h = jax.nn.relu(x @ w1 + b1)
            msg = ew[:, None] * h[src]
            agg = jax.ops.segment_sum(msg, dst, num_segments=x.shape[0])
            h = agg @ w2 + b2
            return jax.nn.relu(_bn(h, g, b))
        src, dst = (hyperedge_index[0], hyperedge_index[1])
        residual = x
        h = _hconv(x, src, dst, hyperedge_weight, c1_w1, c1_b1, c1_w2, c1_b2, c1_g, c1_b)
        h = jax.nn.relu(_bn(h, bn1_g, bn1_b))
        h = _hconv(h, src, dst, hyperedge_weight, c2_w1, c2_b1, c2_w2, c2_b2, c2_g, c2_b)
        h = _bn(h, bn2_g, bn2_b)
        return jax.nn.relu(h + residual)

    def _L0_mix_ref(x, w_qkv, w_out, b_out):
        import jax, jax.numpy as jnp
        import numpy as np
        HEADS = 8
        DIM_HEAD = 64
        EPS = 1e-05

        def _inst_norm(t):
            mu = jnp.mean(t, axis=-1, keepdims=True)
            var = jnp.var(t, axis=-1, keepdims=True)
            return (t - mu) / jnp.sqrt(var + EPS)
        b, n, dim = x.shape
        qkv = x @ w_qkv
        q, k, v = jnp.split(qkv, 3, axis=-1)
        to_heads = lambda t: t.reshape(b, n, HEADS, DIM_HEAD).transpose(0, 2, 1, 3)
        q, k, v = (to_heads(q), to_heads(k), to_heads(v))
        k = _inst_norm(k)
        v = _inst_norm(v)
        dots = jnp.einsum('bhnd,bhne->bhde', k, v)
        out = jnp.einsum('bhnd,bhde->bhne', q, dots) * (1.0 / n)
        out = out.transpose(0, 2, 1, 3).reshape(b, n, HEADS * DIM_HEAD)
        return out @ w_out + b_out

    def _L0_ffn_ref(x, Wr, br, ln_g, ln_b, W1, b1, W2, b2):
        import jax, jax.numpy as jnp
        import numpy as np
        TOP_K = 2
        LN_EPS = 1e-05
        B, S, D = x.shape
        N = B * S
        xt = x.reshape(N, D)
        logits = xt @ Wr + br
        probs = jax.nn.softmax(logits, axis=-1)
        top_p, top_idx = jax.lax.top_k(probs, TOP_K)
        weights = top_p / top_p.sum(axis=-1, keepdims=True)
        mu = xt.mean(axis=-1, keepdims=True)
        var = ((xt - mu) ** 2).mean(axis=-1, keepdims=True)
        xn = (xt - mu) * jax.lax.rsqrt(var + LN_EPS)
        xe = xn[None, :, :] * ln_g[:, None, :] + ln_b[:, None, :]
        h = jax.nn.gelu(jnp.einsum('end,edh->enh', xe, W1) + b1[:, None, :], approximate=False)
        y = jnp.einsum('enh,ehd->end', h, W2) + b2[:, None, :]
        y_tok = jnp.transpose(y, (1, 0, 2))
        sel = jnp.take_along_axis(y_tok, top_idx[:, :, None], axis=1)
        out = (weights[:, :, None] * sel).sum(axis=1)
        return out.reshape(B, S, D)
    edge_index = jnp.stack([src, dst])
    xn = _layernorm(x, axis=-1)
    x = x + _L0_gnn_ref(xn, edge_index, edge_weight, L0_gnn_c1_w1, L0_gnn_c1_b1, L0_gnn_c1_w2, L0_gnn_c1_b2, L0_gnn_c1_g, L0_gnn_c1_b, L0_gnn_bn1_g, L0_gnn_bn1_b, L0_gnn_c2_w1, L0_gnn_c2_b1, L0_gnn_c2_w2, L0_gnn_c2_b2, L0_gnn_c2_g, L0_gnn_c2_b, L0_gnn_bn2_g, L0_gnn_bn2_b) + _L0_mix_ref(xn[None], L0_mix_w_qkv, L0_mix_w_out, L0_mix_b_out)[0]
    x = x + _L0_ffn_ref(_layernorm(x, axis=-1)[None], L0_ffn_Wr, L0_ffn_br, L0_ffn_ln_g, L0_ffn_ln_b, L0_ffn_W1, L0_ffn_b1, L0_ffn_W2, L0_ffn_b2)[0]
    return x

_drawn_inputs = setup_inputs


def setup_inputs(seed=0):
    import zlib

    import numpy as np

    out = dict(_drawn_inputs(seed))
    spreads = {'L0_gnn_c1_b1': (0.0, 0.1),
     'L0_gnn_c1_b2': (0.0, 0.8),
     'L0_gnn_c1_g': (1.0, 0.6),
     'L0_gnn_c1_b': (0.0, 0.1),
     'L0_gnn_bn1_g': (1.0, 0.2),
     'L0_gnn_bn1_b': (0.0, 0.1),
     'L0_gnn_c2_b1': (0.0, 0.1),
     'L0_gnn_c2_b2': (0.0, 0.8),
     'L0_gnn_c2_g': (1.0, 0.6),
     'L0_gnn_c2_b': (0.0, 0.1),
     'L0_gnn_bn2_g': (1.0, 0.2),
     'L0_gnn_bn2_b': (0.0, 0.1),
     'L0_ffn_br': (0.0, 0.1),
     'L0_ffn_ln_g': (1.0, 0.2),
     'L0_ffn_ln_b': (0.0, 0.277),
     'L0_ffn_b1': (0.0, 0.274),
     'L0_ffn_b2': (0.0, 0.1)}
    factors = {'L0_mix_b_out': 5.233}
    for name, (base, spread) in spreads.items():
        noise = np.random.default_rng([zlib.crc32(name.encode()), seed]).standard_normal(out[name].shape)
        drawn = base * np.exp(spread * noise) if base else spread * noise
        out[name] = jnp.asarray(drawn.astype(out[name].dtype))
    for name, factor in factors.items():
        out[name] = (out[name] * factor).astype(out[name].dtype)
    return out
```

```python
import numpy as np
from contextlib import ExitStack

import concourse.bass as bass
from concourse import mybir

F32, BF16, I32, U32 = mybir.dt.float32, mybir.dt.bfloat16, mybir.dt.int32, mybir.dt.uint32
ALU = mybir.AluOpType
ACT = mybir.ActivationFunctionType
AX = mybir.AxisListType.X

P = 128
N, C = 6250, 256
CB = C // P
NT = -(-N // P)
NP = NT * P
TAIL = N - (NT - 1) * P
EPS = 1e-5

E = 206250
GC = 4
GE = GC * P
NG = -(-E // GE)
NGP = -(-NG // 4) * 4
NCH = NGP * GC
SLOTS = 4
W = 64
AGW = -(-(N + W) // P) * P

HEADS, DH = 8, 64
INNER = HEADS * DH
NX = 8
HID = 1024
HB = HID // P
TOK = 256
MAX_TILES = 2 * N // TOK + NX
ROWS = (MAX_TILES + 1) * TOK
ZEROS = 6 * C
HPB = 512 // TOK
NODE_CHUNK = 512
NODE_CHUNKS = [(a, min(NODE_CHUNK, N - a)) for a in range(0, N, NODE_CHUNK)]
FULL_CHUNKS = N // NODE_CHUNK
BNS = 6


class Named:
    pass


def make_tools(nc, ctx, stage=""):
    def sb(name, shape, dt=F32):
        return ctx.enter_context(nc.sbuf_tensor(f"sb_{stage}{name}", shape, dt))

    def ps(name, shape, dt=F32):
        return ctx.enter_context(nc.psum_tensor(f"ps_{stage}{name}", shape, dt))

    def sem(name):
        return ctx.enter_context(nc.semaphore(f"{stage}{name}"))

    return sb, ps, sem


class Steps:

    def __init__(self, eng, sem):
        self.eng, self.sem, self.n = eng, sem, 0

    def __call__(self, instruction):
        instruction.then_inc(self.sem, 1)
        self.n += 1
        self.eng.wait_ge(self.sem, self.n)


def tiles(eng, body, peel=False):
    if peel:
        body(0, 0)
        body(1, 1)
    with eng.Fori(1 if peel else 0, NT // 2) as i:
        body(i * 2, 0)
        body(i * 2 + 1, 1)
    if NT % 2:
        body(NT - 1, 0)


def is_last(t):
    return isinstance(t, int) and t == NT - 1


def is_first(t):
    return isinstance(t, int) and t < 2


def load_stage(nc, d, m):
    with ExitStack() as ctx:
        sb, ps, sem = make_tools(nc, ctx)
        dst_rows = sb("dst_rows", [NGP // 4, 4, GE], I32)
        span = sb("span", [NGP // 4, 2, 4], F32)
        span_i = sb("span_i", [NGP // 4, 2, 4], I32)
        base_bc = sb("base_bc", [P, NGP], I32)
        base_f = sb("base_f", [P, NGP])
        dst_cols = sb("dst_cols", [P, NCH], I32)
        lasts = sb("lasts", [1, NGP], I32)
        extra_f = sb("extra_f", [1, NGP])
        zeros = sb("zeros", [1, NGP])
        stats = sb("stats", [P, NT, BNS])
        tmp = sb("tmp", [P, NT, 4])
        head_mean = sb("head_mean", [P, CB * 2 * HEADS])
        x_loaded, dst_loaded, const_loaded = sem("x_loaded"), sem("dst_loaded"), sem("const_loaded")
        tables_back, span_stored, span_ready = sem("tables_back"), sem("span_stored"), sem("span_ready")
        x_cleared, dve_done, stats_done, root_done = sem("x_cleared"), sem("dve_done"), sem("stats_done"), sem("root_done")
        ident_step = sem("ident_step")
        var_ready, root_step = sem("var_ready"), sem("root_step")
        block = ctx.enter_context(nc.Block())

        @block.sync
        def _(sp):
            sp.wait_ge(x_cleared, 1)
            sp.dma_start(m.x[:, 0:NT - 1, :], d.x[0:(NT - 1) * P, :].rearrange("(t p) c -> p t c", p=P)).then_inc(x_loaded, 16)
            sp.dma_start(m.x[0:TAIL, NT - 1, :], d.x[(NT - 1) * P:N, :]).then_inc(x_loaded, 16)
            sp.wait_ge(span_ready, 1)
            sp.dma_start(d.spans[:, :].rearrange("k (p g) -> p k g", g=4), span_i[:, :, :]).then_inc(span_stored, 16)
            sp.wait_ge(span_stored, 16)
            sp.dma_start(base_bc[:, :], d.spans[0:1, :].to_broadcast([P, NGP])).then_inc(tables_back, 16)
            sp.dma_start(m.base[:, :], d.spans[0:1, :]).then_inc(tables_back, 16)
            sp.dma_start(lasts[:, :], d.spans[1:2, :]).then_inc(tables_back, 16)

        @block.scalar
        def _(act):
            act.dma_start(dst_rows[:, :, :], d.dst_rows).then_inc(dst_loaded, 16)
            act.dma_start(dst_cols[:, :], d.dst_cols).then_inc(const_loaded, 16)
            act.dma_start(m.src[:, :], d.src_cols).then_inc(const_loaded, 16)
            act.dma_start(m.ew[:, :], d.ew_cols).then_inc(const_loaded, 16)
            for to, frm in m.weight_loads:
                act.dma_start(to, frm).then_inc(const_loaded, 16)
            act.wait_ge(const_loaded, 16 * (3 + len(m.weight_loads)))
            act.wait_ge(var_ready, 1)
            act.activation(tmp[:, :, 3], tmp[:, :, 2], ACT.Sqrt).then_inc(root_done, 1)

        @block.gpsimd
        def _(pool):
            step = Steps(pool, ident_step)
            step(pool.memset(m.ident[:, :], 0.0))
            step(pool.affine_select(out=m.ident[:, :], in_=m.ident[:, :], compare_op=ALU.not_equal, fill=1.0,
                                    base=0, pattern=[[-1, P]], channel_multiplier=1))
            step(pool.iota(m.iota_i[:, :], [[1, W]], base=0, channel_multiplier=0))
            step(pool.tensor_copy(m.iota[:, :], m.iota_i[:, :]))
            step(pool.iota(m.offsets_i[:, :], [[W, N // W + 2]], base=0, channel_multiplier=0))
            step(pool.tensor_copy(m.offsets[:, :], m.offsets_i[:, :]))
            step(pool.memset(m.ones[:, :], 1.0))

        @block.vector
        def _(dve):
            nc.vector.memset(m.x[:, NT - 1, :], 0.0).then_inc(x_cleared, 1)
            step = Steps(dve, dve_done)
            dve.wait_ge(dst_loaded, 16)
            step(nc.vector.tensor_reduce(span[:, 0, :], dst_rows[:, :, :], AX, ALU.min))
            step(nc.vector.tensor_reduce(span[:, 1, :], dst_rows[:, :, :], AX, ALU.max))
            nc.vector.tensor_copy(span_i[:, :, :], span[:, :, :]).then_inc(span_ready, 1)
            dve.wait_ge(x_loaded, 32)
            with dve.Fori(0, NT) as t:
                nc.vector.bn_stats(stats[:, bass.ds(t, 1), :].squeeze(1), m.x[:, bass.ds(t, 1), :].squeeze(1)).then_inc(stats_done, 1)
            dve.wait_ge(stats_done, NT)
            merge_stats(nc, step, stats, tmp, m.mean[:, :])
            step(nc.vector.tensor_scalar(tmp[:, :, 2], tmp[:, :, 2], EPS, None, ALU.add))
            step(nc.vector.memset(zeros[:, :], 0.0))
            dve.sem_inc(var_ready, 1)
            dve.wait_ge(tables_back, 48)
            step(nc.vector.tensor_tensor(lasts[:, :], lasts[:, :], m.base[:, :], ALU.subtract))
            step(nc.vector.tensor_scalar(m.extra[:, :], lasts[:, :], W.bit_length() - 1, None, ALU.logical_shift_right))
            step(nc.vector.tensor_copy(extra_f[:, :], m.extra[:, :]))
            step(nc.vector.tensor_tensor_scan(m.extra_sum_f[:, 1:NGP + 1], extra_f[:, :], zeros[:, :], 0.0, ALU.add, ALU.add))
            step(nc.vector.memset(m.extra_sum_f[:, 0:1], 0.0))
            step(nc.vector.tensor_copy(m.extra_sum[:, :], m.extra_sum_f[:, :]))
            step(nc.vector.tensor_copy(base_f[:, :], base_bc[:, :]))
            dve.wait_ge(const_loaded, 16 * (3 + len(m.weight_loads)))
            step(nc.vector.tensor_copy(m.dst[:, :], dst_cols[:, :]))
            heads = m.w_kv[:, :, :].rearrange("p c (h e) -> p (c h) e", e=DH)
            step(nc.vector.tensor_reduce(head_mean[:, :], heads, AX, ALU.add))
            step(nc.vector.tensor_scalar(head_mean[:, :], head_mean[:, :], 1.0 / DH, None, ALU.mult))
            step(nc.vector.tensor_tensor(heads, heads, head_mean[:, :].unsqueeze(2).to_broadcast([P, CB * 2 * HEADS, DH]), ALU.subtract))
            by_group = m.dst[:, :].rearrange("p (g k) -> p g k", k=GC)
            step(nc.vector.tensor_tensor(by_group, by_group, base_f[:, :].unsqueeze(2).to_broadcast([P, NGP, GC]), ALU.subtract))
            dve.wait_ge(root_done, 1)
            step(nc.vector.reciprocal(m.rstd[:, :], tmp[:, :, 3]))


def merge_stats(nc, step, stats, tmp, mean):
    me, mo = stats[:, :, 1], stats[:, :, 4]
    step(nc.vector.tensor_tensor(tmp[:, :, 0], me, mo, ALU.add))
    step(nc.vector.tensor_scalar(mean, tmp[:, :, 0], 0.5, None, ALU.mult))
    step(nc.vector.tensor_tensor(tmp[:, :, 0], me, mo, ALU.subtract))
    step(nc.vector.tensor_tensor(tmp[:, :, 0], tmp[:, :, 0], tmp[:, :, 0], ALU.mult))
    step(nc.vector.tensor_tensor(tmp[:, :, 1], stats[:, :, 2], stats[:, :, 5], ALU.add))
    step(nc.vector.tensor_scalar(tmp[:, :, 1], tmp[:, :, 1], 1.0 / C, None, ALU.mult))
    step(nc.vector.scalar_tensor_tensor(tmp[:, :, 2], tmp[:, :, 0], 0.25, tmp[:, :, 1], ALU.mult, ALU.add))


def norm_stage(nc, m):
    with ExitStack() as ctx:
        sb, ps, sem = make_tools(nc, ctx)
        xn = sb("xn", [P, 2, C])
        turned = ps("turned", [P, 2, NODE_CHUNK])
        normed, turned_ready, turned_used = sem("normed"), sem("turned_ready"), sem("turned_used")
        block = ctx.enter_context(nc.Block())

        @block.vector
        def _(dve):
            dve.sem_inc(turned_ready, 2)

            def body(t, s):
                dve.wait_ge(turned_ready, t + 1)
                nc.vector.tensor_scalar(xn[:, s, :], m.x[:, bass.ds(t, 1), :].squeeze(1), m.mean[:, bass.ds(t, 1)],
                                        m.rstd[:, bass.ds(t, 1)], ALU.subtract, ALU.mult).then_inc(normed, 1)
            tiles(dve, body)

        @block.tensor
        def _(pe):
            def body(t, s):
                pe.wait_ge(normed, t + 1)
                pe.wait_ge(turned_used, t + 1)
                for c in range(CB):
                    last = nc.tensor.transpose(turned[:, s, c * P:(c + 1) * P], xn[:, s, c * P:(c + 1) * P], m.ident[:, :])
                last.then_inc(turned_ready, 1)
            tiles(pe, body)

        @block.scalar
        def _(act):
            act.sem_inc(turned_used, 2)

            def body(t, s):
                act.wait_ge(turned_ready, t + 3)
                act.activation(m.xT[:, :, bass.ds(t * P, P)], turned[:, s, 0:C].rearrange("p (c n) -> p c n", c=CB),
                               ACT.Copy).then_inc(turned_used, 1)
            tiles(act, body)


def hidden_stage(nc, d, m, layer, srcT, w, b):
    with ExitStack() as ctx:
        sb, ps, sem = make_tools(nc, ctx, f"hidden{layer}_")
        a_tile = sb("a_tile", [P, 2, CB, P])
        h_tile = sb("h_tile", [P, 2, C])
        acc = ps("acc", [P, 2, NODE_CHUNK])
        staged, product, relued = sem("staged"), sem("product"), sem("relued")
        stored = [sem("stored_0"), sem("stored_1")]
        block = ctx.enter_context(nc.Block())

        @block.scalar
        def _(act):
            act.sem_inc(product, 2)

            def body(t, s):
                act.wait_ge(product, t + 1)
                act.activation(a_tile[:, s, :, :], srcT[:, :, bass.ds(t * P, P)], ACT.Copy).then_inc(staged, 1)
            tiles(act, body)

        @block.tensor
        def _(pe):
            def body(t, s):
                pe.wait_ge(staged, t + 1)
                pe.wait_ge(relued, t + 1)
                nc.tensor.matmul(acc[:, s, 0:C], m.ones[0:1, :], b, start=True, stop=False)
                for c in range(CB):
                    last = nc.tensor.matmul(acc[:, s, 0:C], a_tile[:, s, c, :], w[:, c, :], start=False, stop=c == CB - 1)
                last.then_inc(product, 1)
            tiles(pe, body)

        @block.vector
        def _(dve):
            dve.sem_inc(relued, 2)

            def body(t, s):
                dve.wait_ge(product, t + 3)
                if not is_first(t):
                    dve.wait_ge(stored[s], 8 * (t - s))
                nc.vector.tensor_scalar(h_tile[:, s, :], acc[:, s, 0:C], 0.0, None, ALU.max).then_inc(relued, 1)
            tiles(dve, body, peel=True)

        @block.sync
        def _(sp):
            def body(t, s):
                sp.wait_ge(relued, t + 3)
                sp.dma_start(d.h[bass.ds(t * P, P), :], h_tile[:, s, :]).then_inc(stored[s], 16)
            tiles(sp, body)
            for s in range(2):
                sp.wait_ge(stored[s], 16 * ((NT + 1 - s) // 2))


def gather_stage(nc, d, m, mix):
    with ExitStack() as ctx:
        sb, ps, sem = make_tools(nc, ctx, "gather_mix_" if mix else "gather_")
        rows = sb("rows", [P, SLOTS, GC, C])
        idx = sb("idx", [P, SLOTS, GC], U32)
        sel = sb("sel", [P, 2, GC, W])
        hit_x = sb("hit_x", [P, GC, W])
        sel_x = sb("sel_x", [P, GC, W])
        parts = [ps(f"part{i}", [P, NODE_CHUNK]) for i in range(3)]
        part = [x[:, 0:CB * W].rearrange("p (b w) -> p b w", b=CB) for x in parts]
        part_x = part[2]
        gathered = [sem(f"gathered{i}") for i in range(SLOTS)]
        idx_ready, sel_ready, summed, added = sem("idx_ready"), sem("sel_ready"), sem("summed"), sem("added")
        cleared = sem("cleared")
        x_hit, x_sel, x_summed, x_added = sem("x_hit"), sem("x_sel"), sem("x_summed"), sem("x_added")
        k = mixer_parts(sb, ps, sem) if mix else None
        if not mix:
            zeros, blanked = sb("zeros", [P, ZEROS]), sem("blanked")
        block = ctx.enter_context(nc.Block())

        first = PER_MIX * NT if mix else 0
        turns = (NG - first) // SLOTS
        rest = first + turns * SLOTS

        def groups(group, eng, hooks=()):
            if mix:
                def some(t, s):
                    for j in range(PER_MIX):
                        group(t * PER_MIX + j, j % SLOTS)
                        if j in hooks:
                            hooks[j](t, s)
                tiles(eng, some)
            with eng.Fori(0, turns) as i:
                for j in range(SLOTS):
                    group(i * SLOTS + (first + j), j)
            for g in range(rest, NG):
                group(g, g % SLOTS)

        if not mix:
            @block.sync
            def _(sp):
                sp.wait_ge(cleared, 1)
                blank = zeros[:, :].unsqueeze(1).to_broadcast([P, ROWS * C // P // ZEROS, ZEROS])
                for to in (d.routed, d.expert_out):
                    sp.dma_start(to.rearrange("(p a) c -> p (a c)", p=P).rearrange("p (b z) -> p b z", z=ZEROS), blank).then_inc(blanked, 16)
                sp.wait_ge(blanked, 32)

        @block.gpsimd
        def _(pool):
            def group(g, s):
                pool.wait_ge(idx_ready, g + 1)
                pool.nop(nofuse=True)
                for c in range(GC):
                    pool.indirect_dma_start(rows[:, s, c, :], None, d.h[:, :],
                                            bass.IndirectOffsetOnAxis(ap=idx[:, s, c:c + 1], axis=0)).then_inc(gathered[s], 16)
            groups(group, pool)

        @block.scalar
        def _(act):
            act.sem_inc(added, SLOTS)
            act.sem_inc(x_added, 1)

            def group(g, s):
                act.wait_ge(added, g + 1)
                nc.scalar.activation(idx[:, s, :], m.src[:, bass.ds(g * GC, GC)], ACT.Copy).then_inc(idx_ready, 1)

            def stage_tile(t, s):
                act.wait_ge(k.dots_done, t + 1)
                nc.scalar.activation(k.x_tile[:, s, :, :], m.xT[:, :, bass.ds(t * P, P)], ACT.Copy).then_inc(k.staged, 1)

            def square(t, s):
                act.wait_ge(k.kv_ready, t + 1)
                kv_psum = k.kv_psum[:, :, :].rearrange("p a n -> p (a n)")
                nc.scalar.activation(k.kv[:, s, :], kv_psum, ACT.Copy).then_inc(k.kv_out, 1)
                act.wait_ge(k.var_out, t + 1)
                act.wait_ge(k.kv_out, t + 2)
                nc.scalar.activation(k.squares[:, :], k.kv[:, s, :], ACT.Square).then_inc(k.squared, 1)

            def root(t, s):
                act.wait_ge(k.var_out, t + 2)
                nc.scalar.activation(k.root[:, s, :], k.var[:, s, :], ACT.Sqrt).then_inc(k.rooted, 1)
            if mix:
                act.sem_inc(k.dots_done, 2)
                act.sem_inc(k.kv_out, 1)
                act.sem_inc(k.var_out, 1)
            groups(group, act, {0: stage_tile, 5: square, 7: root})

        @block.tensor
        def _(pe):
            def group(g, s):
                extra = pe.value_load(m.extra[0:1, bass.ds(g, 1)], min_val=0, max_val=N // W)
                pe.wait_ge(gathered[s], (g - s) * (16 * GC // SLOTS) + 16 * GC)
                pe.wait_ge(sel_ready, g + 1)
                pe.wait_ge(added, g + SLOTS - 1)
                for b in range(CB):
                    for c in range(GC):
                        last = nc.tensor.matmul(part[s % 2][:, b, :], rows[:, s, c, b * P:(b + 1) * P], sel[:, s % 2, c, :],
                                                start=c == 0, stop=c == GC - 1)
                last.then_inc(summed, 1)
                with pe.If(extra > 0):
                    before = pe.value_load(m.extra_sum[0:1, bass.ds(g, 1)], min_val=0, max_val=NG * (N // W))
                    with pe.Fori(0, extra) as j:
                        pe.wait_ge(x_sel, before + j + 1)
                        pe.wait_ge(x_added, before + j + 1)
                        for b in range(CB):
                            for c in range(GC):
                                last = nc.tensor.matmul(part_x[:, b, :], rows[:, s, c, b * P:(b + 1) * P], sel_x[:, c, :],
                                                        start=c == 0, stop=c == GC - 1)
                        last.then_inc(x_summed, 1)
                    pe.nop(nofuse=True)
                with pe.Else():
                    pe.nop(nofuse=True)

            def keys_values(t, s):
                pe.wait_ge(k.staged, t + 1)
                pe.wait_ge(k.kv_out, t + 1)
                for half in range(2):
                    for c in range(CB):
                        last = nc.tensor.matmul(k.kv_psum[:, half, :], k.x_tile[:, s, c, :],
                                                m.w_kv[:, c, half * INNER:(half + 1) * INNER], start=c == 0, stop=c == CB - 1)
                last.then_inc(k.kv_ready, 1)

            def dots(t, s):
                pe.wait_ge(k.scaled, t + 1)
                ends = is_last(t)
                for b in range(INNER // P):
                    last = nc.tensor.matmul(k.dots[:, b * P:(b + 1) * P], k.kv[:, s, INNER + b * P:INNER + (b + 1) * P],
                                            k.kv[:, s, b * P:(b + 1) * P], start=False, stop=ends, skip_group_check=True)
                last.then_inc(k.dots_done, 1)
            if mix:
                pe.wait_ge(cleared, 1)
                nc.tensor.matmul(k.dots[:, :], m.ident[:, :], m.agg[:, 0, 0:INNER], start=True, stop=False, skip_group_check=True)\
                    .then_inc(k.zeroed, 1)
            groups(group, pe, {0: keys_values, 7: dots})

        @block.vector
        def _(dve):
            if not mix:
                nc.vector.memset(zeros[:, :], 0.0)
            nc.vector.memset(m.agg[:, :, :], 0.0).then_inc(cleared, 1)
            dve.wait_ge(cleared, 1)
            if mix:
                dve.wait_ge(k.zeroed, 1)

            def select(g, s):
                for c in range(GC):
                    at = bass.ds(g * GC + c, 1)
                    last = nc.vector.tensor_scalar(sel[:, s % 2, c, :], m.iota[:, :], m.dst[:, at], m.ew[:, at],
                                                   ALU.is_equal, ALU.mult)
                last.then_inc(sel_ready, 1)

            def group(g, s):
                select(g + 1, (s + 1) % SLOTS)
                base = dve.value_load(m.base[0:1, bass.ds(g, 1)], min_val=0, max_val=N - 1)
                extra = dve.value_load(m.extra[0:1, bass.ds(g, 1)], min_val=0, max_val=N // W)
                with dve.If(extra > 0):
                    before = dve.value_load(m.extra_sum[0:1, bass.ds(g, 1)], min_val=0, max_val=NG * (N // W))
                    with dve.Fori(0, extra) as j:
                        for c in range(GC):
                            last = nc.vector.tensor_scalar(hit_x[:, c, :], m.iota[:, :], m.offsets[:, bass.ds(j + 1, 1)],
                                                           m.dst[:, bass.ds(g * GC + c, 1)], ALU.add, ALU.is_equal)
                        last.then_inc(x_hit, 1)
                        dve.wait_ge(x_hit, before + j + 1)
                        for c in range(GC):
                            last = nc.vector.tensor_scalar(sel_x[:, c, :], hit_x[:, c, :], m.ew[:, bass.ds(g * GC + c, 1)],
                                                           None, ALU.mult)
                        last.then_inc(x_sel, 1)
                        dve.wait_ge(x_summed, before + j + 1)
                        dve.wait_ge(added, g + SLOTS)
                        start = nc.s_assert_within(base + (j + 1) * W, 0, N - 1,
                                                   skip_runtime_bounds_check_because="the windows end with the last destination")
                        to = m.agg[:, :, bass.ds(start, W)]
                        nc.vector.tensor_tensor(to, part_x[:, :, :], to, ALU.add).then_inc(x_added, 1)
                    dve.wait_ge(x_added, before + extra + 1)
                    dve.nop(nofuse=True)
                with dve.Else():
                    dve.nop(nofuse=True)
                dve.wait_ge(summed, g + 1)
                dve.wait_ge(added, g + SLOTS)
                to = m.agg[:, :, bass.ds(base, W)]
                nc.vector.tensor_tensor(to, part[s % 2][:, :, :], to, ALU.add).then_inc(added, 1)

            def variance(t, s):
                dve.wait_ge(k.squared, t + 1)
                nc.vector.tensor_reduce(k.sums[:, :], k.squares[:, :].rearrange("p (h e) -> p h e", e=DH), AX, ALU.add).then_inc(k.sum_out, 1)
                dve.wait_ge(k.sum_out, t + 1)
                nc.vector.tensor_scalar(k.var[:, s, :], k.sums[:, :], 1.0 / DH, EPS, ALU.mult, ALU.add).then_inc(k.var_out, 1)

            def scale(t, s):
                dve.wait_ge(k.rooted, t + 1)
                nc.vector.tensor_tensor(k.both[:, :], k.root[:, s, 0:HEADS], k.root[:, s, HEADS:2 * HEADS], ALU.mult).then_inc(k.both_out, 1)
                dve.wait_ge(k.both_out, t + 1)
                nc.vector.reciprocal(k.rstd[:, :], k.both[:, :]).then_inc(k.rstd_out, 1)
                dve.wait_ge(k.rstd_out, t + 1)
                keys = k.kv[:, s, 0:INNER].rearrange("p (h e) -> p h e", e=DH)
                nc.vector.tensor_tensor(keys, keys, k.rstd[:, :].unsqueeze(2).to_broadcast([P, HEADS, DH]), ALU.mult).then_inc(k.scaled, 1)
            select(0, 0)
            groups(group, dve, {3: variance, 5: scale})
            if mix:
                dve.wait_ge(k.dots_done, NT + 2)
                nc.vector.memset(m.dots[:, :, :], 0.0).then_inc(k.final, 1)
                dve.wait_ge(k.final, 1)
                dots = k.dots[:, :].rearrange("p (b n) -> p b n", n=P)
                for a in (0, DH):
                    nc.vector.tensor_copy(m.dots[a:a + DH, :, a:a + DH], dots[a:a + DH, :, a:a + DH]).then_inc(k.final, 1)


PER_MIX = 8


def mixer_parts(sb, ps, sem):
    k = Named()
    k.x_tile = sb("mx_x", [P, 2, CB, P])
    k.kv = sb("mx_kv", [P, 2, 2 * INNER])
    k.squares = sb("mx_squares", [P, 2 * INNER])
    k.sums = sb("mx_sums", [P, 2 * HEADS])
    k.var = sb("mx_var", [P, 2, 2 * HEADS])
    k.root = sb("mx_root", [P, 2, 2 * HEADS])
    k.both = sb("mx_both", [P, HEADS])
    k.rstd = sb("mx_rstd", [P, HEADS])
    k.kv_psum = ps("mx_kv_psum", [P, 2, INNER])
    k.dots = ps("mx_dots", [P, INNER])
    k.staged, k.kv_ready, k.kv_out, k.squared = sem("mx_staged"), sem("mx_kv_ready"), sem("mx_kv_out"), sem("mx_squared")
    k.sum_out, k.var_out, k.rooted, k.both_out = sem("mx_sum_out"), sem("mx_var_out"), sem("mx_rooted"), sem("mx_both_out")
    k.rstd_out, k.scaled, k.dots_done = sem("mx_rstd_out"), sem("mx_scaled"), sem("mx_dots_done")
    k.zeroed, k.final = sem("mx_zeroed"), sem("mx_final")
    return k


def batch_norm_stage(nc, d, m, layer, last_layer):
    with ExitStack() as ctx:
        sb, ps, sem = make_tools(nc, ctx, f"norm{layer}_")
        stats = sb("bn_stats", [P, CB, len(NODE_CHUNKS), BNS])
        mv = sb("bn_mv", [P, CB, 2])
        root = sb("bn_root", [P, CB])
        scale = sb("bn_scale", [P, CB])
        shift = sb("bn_shift", [P, CB])
        acc = ps("bn_acc", [P, 2, CB, NODE_CHUNK])
        product, biased, steps, var_ready, rooted, scaled, applied, counted, part_done = (
            sem("bn_" + x) for x in "product biased steps var_ready rooted scaled applied counted part_done".split())
        mixing = layer == 0
        if mixing:
            mid_psum = ps("mid_psum", [P, 2, NODE_CHUNK])
            mid = sb("mid", [P, INNER // P, C])
            mid_ready, mid_out, mix_ready, mix_out = (sem(x) for x in "mid_ready mid_out mix_ready mix_out".split())
        block = ctx.enter_context(nc.Block())
        w2, b2 = m.w2[layer], m.b2[layer]
        gains = m.gains[layer]
        nchunk = len(NODE_CHUNKS)

        def chunks(eng, body):
            with eng.Fori(0, FULL_CHUNKS // 2) as i:
                body(i * 2, 0, bass.ds(i * (2 * NODE_CHUNK), NODE_CHUNK), NODE_CHUNK)
                body(i * 2 + 1, 1, bass.ds(i * (2 * NODE_CHUNK) + NODE_CHUNK, NODE_CHUNK), NODE_CHUNK)
            for i in range(FULL_CHUNKS // 2 * 2, nchunk):
                a, n = NODE_CHUNKS[i]
                body(i, i % 2, slice(a, a + n), n)

        @block.tensor
        def _(pe):
            def body(i, s, cols, n):
                pe.wait_ge(biased, i + 1)
                for b in range(CB):
                    for c in range(CB):
                        last = nc.tensor.matmul(acc[:, s, b, 0:n], w2[:, c, b * P:(b + 1) * P], m.agg[:, c, cols],
                                                start=c == 0, stop=c == CB - 1)
                last.then_inc(product, 1)
            chunks(pe, body)
            if mixing:
                for b in range(INNER // P):
                    if b >= 2:
                        pe.wait_ge(mid_out, b - 1)
                    nc.tensor.matmul(mid_psum[:, b % 2, 0:C], m.dots[:, b, :], m.w_out[:, b, :], start=True, stop=True).then_inc(mid_ready, 1)
                pe.wait_ge(mid_out, INNER // P)
                for c in range(CB):
                    for b in range(INNER // P):
                        last = nc.tensor.matmul(mid_psum[:, c, 0:C], m.w_q[:, b, c * P:(c + 1) * P], mid[:, b, :],
                                                start=b == 0, stop=b == INNER // P - 1)
                    last.then_inc(mix_ready, 1)

        @block.scalar
        def _(act):
            act.sem_inc(biased, 2)

            def body(i, s, cols, n):
                act.wait_ge(product, i + 1)
                for b in range(CB):
                    ins = nc.scalar.activation(m.agg[:, b, cols], acc[:, s, b, 0:n], ACT.Identity, bias=b2[:, b:b + 1])
                ins.then_inc(biased, 1)
            chunks(act, body)
            if mixing:
                for b in range(INNER // P):
                    act.wait_ge(mid_ready, b + 1)
                    nc.scalar.activation(mid[:, b, :], mid_psum[:, b % 2, 0:C], ACT.Copy).then_inc(mid_out, 1)
                for c in range(CB):
                    act.wait_ge(mix_ready, c + 1)
                    nc.scalar.activation(m.w_mix[:, c, :], mid_psum[:, c, 0:C], ACT.Copy, scale=1.0 / N).then_inc(mix_out, 1)
            for norm in range(2):
                act.wait_ge(var_ready, norm + 1)
                nc.scalar.activation(root[:, :], mv[:, :, 1], ACT.Sqrt).then_inc(rooted, 1)
                act.wait_ge(scaled, norm + 1)
                ends = norm == 1 and last_layer

                def apply(i, s, cols, n):
                    if ends:
                        act.wait_ge(part_done, i + 1)
                        for b in range(CB):
                            ins = nc.scalar.activation(m.agg[:, b, cols], m.agg[:, b, cols], ACT.Relu, bias=shift[:, b:b + 1])
                    else:
                        for b in range(CB):
                            ins = nc.scalar.activation(m.agg[:, b, cols], m.agg[:, b, cols], ACT.Relu, bias=shift[:, b:b + 1],
                                                       scale=scale[:, b:b + 1])
                    ins.then_inc(applied, 1)
                chunks(act, apply)

        @block.vector
        def _(dve):
            step = Steps(dve, steps)
            for norm in range(2):
                def count(i, s, cols, n):
                    if norm:
                        dve.wait_ge(applied, i + 1)
                    else:
                        dve.wait_ge(biased, i + 3)
                    at = bass.ds(i, 1)
                    for b in range(CB):
                        ins = nc.vector.bn_stats(stats[:, b, at, :].squeeze(1), m.agg[:, b, cols])
                    ins.then_inc(counted, 1)
                chunks(dve, count)
                dve.wait_ge(counted, nchunk * (norm + 1))
                for b in range(CB):
                    step(nc.vector.bn_aggr(mv[:, b, :], stats[:, b, :, :].rearrange("p a b -> p (a b)")))
                step(nc.vector.tensor_scalar(mv[:, :, 1], mv[:, :, 1], EPS, None, ALU.add))
                dve.sem_inc(var_ready, 1)
                dve.wait_ge(rooted, norm + 1)
                step(nc.vector.reciprocal(scale[:, :], root[:, :]))
                step(nc.vector.tensor_tensor(scale[:, :], scale[:, :], gains[norm][0], ALU.mult))
                step(nc.vector.tensor_tensor(shift[:, :], scale[:, :], mv[:, :, 0], ALU.mult))
                step(nc.vector.tensor_tensor(shift[:, :], gains[norm][1], shift[:, :], ALU.subtract))
                dve.sem_inc(scaled, 1)
            if last_layer:
                def residual(i, s, cols, n):
                    for b in range(CB):
                        ins = nc.vector.scalar_tensor_tensor(m.agg[:, b, cols], m.agg[:, b, cols], scale[:, b:b + 1],
                                                             m.xT[:, b, cols], ALU.mult, ALU.add)
                    ins.then_inc(part_done, 1)
                chunks(dve, residual)
            dve.wait_ge(applied, nchunk * 2)


def join_stage(nc, d, m):
    with ExitStack() as ctx:
        sb, ps, sem = make_tools(nc, ctx)
        x_tile = sb("jn_x", [P, 2, C])
        xT_tile = sb("jn_xT", [P, 2, CB, P])
        gT_tile = sb("jn_gT", [P, 2, CB, P])
        stats = sb("jn_stats", [P, NT, BNS])
        tmp = sb("jn_tmp", [P, NT, 4])
        acc = ps("jn_acc", [P, 2, NODE_CHUNK])
        staged, product, joined, counted, steps, var_ready, rooted, cleared = (
            sem("jn_" + x) for x in "staged product joined counted steps var_ready rooted cleared".split())
        loaded = [sem("jn_loaded0"), sem("jn_loaded1")]
        stored = sem("jn_stored")
        block = ctx.enter_context(nc.Block())

        @block.sync
        def _(sp):
            sp.wait_ge(cleared, 1)

            def body(t, s):
                sp.wait_ge(joined, t + 1)
                if is_last(t):
                    sp.dma_start(x_tile[0:TAIL, s, :], d.x[(NT - 1) * P:N, :]).then_inc(loaded[s], 16)
                else:
                    sp.dma_start(x_tile[:, s, :], d.x[bass.ds(t * P, P), :]).then_inc(loaded[s], 16)
            tiles(sp, body)
            sp.wait_ge(joined, NT + 2)
            sp.dma_start(d.x2[0:N - TAIL, :].rearrange("(t p) c -> p t c", p=P), m.tok[:, 0:NT - 1, :]).then_inc(stored, 16)
            sp.dma_start(d.x2[N - TAIL:N, :], m.tok[0:TAIL, NT - 1, :]).then_inc(stored, 16)
            sp.wait_ge(stored, 32)

        @block.scalar
        def _(act):
            act.sem_inc(product, 2)

            def body(t, s):
                act.wait_ge(product, t + 1)
                at = bass.ds(t * P, P)
                nc.scalar.activation(xT_tile[:, s, :, :], m.xT[:, :, at], ACT.Copy)
                nc.scalar.activation(gT_tile[:, s, :, :], m.agg[:, :, at], ACT.Copy).then_inc(staged, 1)
            tiles(act, body)
            act.wait_ge(var_ready, 1)
            nc.scalar.activation(tmp[:, :, 3], tmp[:, :, 2], ACT.Sqrt).then_inc(rooted, 1)

        @block.tensor
        def _(pe):
            def body(t, s):
                pe.wait_ge(staged, t + 1)
                pe.wait_ge(joined, t + 1)
                nc.tensor.matmul(acc[:, s, 0:C], m.ones[0:1, :], m.b_out[0:1, :], start=True, stop=False)
                for c in range(CB):
                    nc.tensor.matmul(acc[:, s, c * P:(c + 1) * P], gT_tile[:, s, c, :], m.ident[:, :], start=False, stop=False,
                                     skip_group_check=True)
                for c in range(CB):
                    last = nc.tensor.matmul(acc[:, s, 0:C], xT_tile[:, s, c, :], m.w_mix[:, c, :], start=False, stop=c == CB - 1)
                last.then_inc(product, 1)
            tiles(pe, body)

        @block.vector
        def _(dve):
            dve.sem_inc(joined, 2)
            step = Steps(dve, steps)
            step(nc.vector.memset(x_tile[:, :, :], 0.0))
            dve.sem_inc(cleared, 1)

            def body(t, s):
                dve.wait_ge(product, t + 3)
                dve.wait_ge(loaded[s], 8 * (t - s) + 16)
                at = bass.ds(t, 1)
                nc.vector.tensor_tensor(m.tok[:, at, :].squeeze(1), acc[:, s, 0:C], x_tile[:, s, :], ALU.add).then_inc(joined, 1)
                dve.wait_ge(joined, t + 3)
                nc.vector.bn_stats(stats[:, at, :].squeeze(1), m.tok[:, at, :].squeeze(1)).then_inc(counted, 1)
            tiles(dve, body)
            dve.wait_ge(counted, NT)
            merge_stats(nc, step, stats, tmp, m.mean[:, :])
            step(nc.vector.tensor_scalar(tmp[:, :, 2], tmp[:, :, 2], EPS, None, ALU.add))
            dve.sem_inc(var_ready, 1)
            dve.wait_ge(rooted, 1)
            step(nc.vector.reciprocal(m.rstd[:, :], tmp[:, :, 3]))


def router_stage(nc, d, m):
    with ExitStack() as ctx:
        sb, ps, sem = make_tools(nc, ctx)
        turned_tile = sb("rt_turned", [P, 2, CB, P])
        stats = sb("rt_stats", [P, NT, BNS])
        tmp = sb("rt_tmp", [P, NT, 4])
        big = {n: sb("rt_" + n, [P, NT, NX]) for n in "p eq where oh1 oh2 place a".split()}
        one = {n: sb("rt_" + n, [P, NT]) for n in "max1 max2 id1 id2 sum".split()}
        valid, node = sb("rt_valid", [P, NT]), sb("rt_node", [P, NT], I32)
        expert, expert_i = sb("rt_expert", [P, NX]), sb("rt_expert_i", [P, NX], I32)
        picked = sb("rt_picked", [P, NT * NX], BF16)
        earlier, all_ones = sb("rt_earlier", [P, P], BF16), sb("rt_all_ones", [P, P], BF16)
        zeros = sb("rt_zeros", [P, NT])
        tiles_f, tiles_i = sb("rt_tiles_f", [P, 2, NX]), sb("rt_tiles_i", [P, NX], I32)
        turned = ps("rt_turned_psum", [P, 2, NODE_CHUNK])
        logits = ps("rt_logits", [P, NODE_CHUNK])
        counts = ps("rt_counts", [P, 2, NODE_CHUNK])
        normed, turned_ready, turned_used, logit_ready, counted, steps, var_ready, rooted, pool_steps, shifted, exped, pick_ready, count_ready = (
            sem("rt_" + x) for x in ("normed turned_ready turned_used logit_ready counted steps var_ready rooted pool_steps "
                                     "shifted exped pick_ready count_ready").split())
        block = ctx.enter_context(nc.Block())

        @block.gpsimd
        def _(pool):
            step = Steps(pool, pool_steps)
            step(pool.iota(node[:, :], [[P, NT]], base=0, channel_multiplier=1))
            step(pool.tensor_copy(valid[:, :], node[:, :]))
            step(pool.tensor_scalar(valid[:, :], valid[:, :], float(N), None, ALU.is_lt))
            step(pool.iota(expert_i[:, :], [[1, NX]], base=0, channel_multiplier=0))
            step(pool.tensor_copy(expert[:, :], expert_i[:, :]))
            step(pool.memset(all_ones[:, :], 1.0))
            step(pool.affine_select(out=earlier[:, :], in_=all_ones[:, :], compare_op=ALU.is_gt, fill=0.0,
                                    base=0, pattern=[[1, P]], channel_multiplier=-1))

        @block.tensor
        def _(pe):
            def body(t, s):
                pe.wait_ge(normed, t + 1)
                pe.wait_ge(turned_used, t + 1)
                for c in range(CB):
                    last = nc.tensor.transpose(turned[:, s, c * P:(c + 1) * P], m.tok_tile[:, s, c * P:(c + 1) * P], m.ident[:, :])
                last.then_inc(turned_ready, 1)
                pe.wait_ge(turned_used, t + 3)
                out = logits[:, bass.ds(t * NX, NX)]
                nc.tensor.matmul(out, m.ones[0:1, :], m.br[0:1, :], start=True, stop=False)
                for c in range(CB):
                    last = nc.tensor.matmul(out, turned_tile[:, s, c, :], m.wr[:, c, :], start=False, stop=c == CB - 1)
                last.then_inc(logit_ready, 1)
            tiles(pe, body)
            pe.wait_ge(pick_ready, 1)
            pe.wait_ge(pool_steps, 7)
            nc.tensor.matmul(counts[:, 0, 0:NT * NX], earlier[:, :], picked[:, :], start=True, stop=True)
            nc.tensor.matmul(counts[:, 1, 0:NT * NX], all_ones[:, :], picked[:, :], start=True, stop=True).then_inc(count_ready, 1)

        @block.scalar
        def _(act):
            act.sem_inc(turned_used, 2)

            def body(t, s):
                act.wait_ge(turned_ready, t + 3)
                nc.scalar.activation(turned_tile[:, s, :, :], turned[:, s, 0:C].rearrange("p (c n) -> p c n", c=CB),
                                     ACT.Copy).then_inc(turned_used, 1)
            tiles(act, body)
            act.wait_ge(var_ready, 1)
            nc.scalar.activation(tmp[:, :, 3], tmp[:, :, 2], ACT.Sqrt).then_inc(rooted, 1)
            act.wait_ge(shifted, 1)
            nc.scalar.activation(big["p"][:, :, :], big["p"][:, :, :], ACT.Exp).then_inc(exped, 1)

        @block.vector
        def _(dve):
            dve.sem_inc(turned_ready, 2)
            step = Steps(dve, steps)

            def body(t, s):
                dve.wait_ge(turned_ready, t + 1)
                at = bass.ds(t, 1)
                nc.vector.tensor_scalar(m.tok_tile[:, s, :], m.tok[:, at, :].squeeze(1), m.mean[:, at], m.rstd[:, at],
                                        ALU.subtract, ALU.mult).then_inc(normed, 1)
                dve.wait_ge(normed, t + 1)
                nc.vector.bn_stats(stats[:, at, :].squeeze(1), m.tok_tile[:, s, :])
                nc.vector.tensor_copy(m.tok[:, at, :].squeeze(1), m.tok_tile[:, s, :]).then_inc(counted, 1)
            tiles(dve, body)
            dve.wait_ge(counted, NT)
            merge_stats(nc, step, stats, tmp, m.mean[:, :])
            step(nc.vector.tensor_scalar(tmp[:, :, 2], tmp[:, :, 2], EPS, None, ALU.add))
            dve.sem_inc(var_ready, 1)
            dve.wait_ge(rooted, 1)
            step(nc.vector.reciprocal(m.rstd[:, :], tmp[:, :, 3]))

            def bc(x):
                return x.unsqueeze(2).to_broadcast([P, NT, NX])
            tt, ts = nc.vector.tensor_tensor, nc.vector.tensor_scalar
            p, eq, where, oh1, oh2, place, a = (big[n][:, :, :] for n in "p eq where oh1 oh2 place a".split())
            max1, max2, id1, id2, total = (one[n][:, :] for n in "max1 max2 id1 id2 sum".split())
            dve.wait_ge(logit_ready, NT)
            lg = logits[:, 0:NT * NX].rearrange("p (t e) -> p t e", e=NX)
            step(nc.vector.tensor_reduce(max1, lg, AX, ALU.max))
            step(tt(p, lg, bc(max1), ALU.subtract))
            dve.sem_inc(shifted, 1)
            dve.wait_ge(exped, 1)
            step(nc.vector.tensor_reduce(total, p, AX, ALU.add))
            step(nc.vector.reciprocal(total, total))
            step(tt(p, p, bc(total), ALU.mult))
            dve.wait_ge(pool_steps, 7)
            e_bc = expert[:, :].unsqueeze(1).to_broadcast([P, NT, NX])
            for oh, mx, ident in ((oh1, max1, id1), (oh2, max2, id2)):
                step(nc.vector.tensor_reduce(mx, p, AX, ALU.max))
                step(tt(eq, p, bc(mx), ALU.is_equal))
                step(nc.vector.scalar_tensor_tensor(where, eq, -float(NX), e_bc, ALU.mult, ALU.add))
                step(nc.vector.tensor_reduce(ident, where, AX, ALU.min))
                step(tt(oh, where, bc(ident), ALU.is_equal))
                step(nc.vector.scalar_tensor_tensor(p, oh, -2.0, p, ALU.mult, ALU.add))
            step(tt(total, max1, max2, ALU.add))
            step(nc.vector.reciprocal(total, total))
            step(tt(m.weight[:, 0, :], max1, total, ALU.mult))
            step(tt(m.weight[:, 1, :], max2, total, ALU.mult))
            step(tt(a, oh1, oh2, ALU.add))
            step(tt(picked[:, :].rearrange("p (t e) -> p t e", e=NX), a, bc(valid[:, :]), ALU.mult))
            dve.sem_inc(pick_ready, 1)
            step(nc.vector.memset(zeros[:, :], 0.0))
            dve.wait_ge(count_ready, 1)
            step(nc.vector.tensor_copy(a, counts[:, 1, 0:NT * NX].rearrange("p (t e) -> p t e", e=NX)))
            for e in range(NX):
                step(nc.vector.tensor_tensor_scan(where[:, :, e], a[:, :, e], zeros[:, :], 0.0, ALU.add, ALU.add))
            step(tt(place, where, a, ALU.subtract))
            step(tt(place, place, counts[:, 0, 0:NT * NX].rearrange("p (t e) -> p t e", e=NX), ALU.add))
            total_e = where[:, NT - 1, :]
            step(ts(tiles_f[:, 0, :], total_e, float(TOK - 1), None, ALU.add))
            step(nc.vector.tensor_copy(tiles_i[:, :], tiles_f[:, 0, :]))
            step(ts(tiles_i[:, :], tiles_i[:, :], TOK.bit_length() - 1, None, ALU.logical_shift_right))
            step(nc.vector.tensor_copy(tiles_f[:, 0, :], tiles_i[:, :]))
            step(ts(tiles_f[:, 0, :], tiles_f[:, 0, :], 1.0, None, ALU.max))
            step(nc.vector.tensor_tensor_scan(tiles_f[:, 1, :], tiles_f[:, 0, :], zeros[:, 0:NX], 0.0, ALU.add, ALU.add))
            step(tt(tiles_f[:, 1, :], tiles_f[:, 1, :], tiles_f[:, 0, :], ALU.subtract))
            step(nc.vector.tensor_copy(m.expert_i[:, :, :], tiles_f[0:1, :, :]))
            step(ts(expert[:, :], tiles_f[:, 1, :], float(TOK), None, ALU.mult))
            step(tt(place, place, e_bc, ALU.add))
            for i, oh in enumerate((oh1, oh2)):
                step(tt(eq, oh, place, ALU.mult))
                step(nc.vector.tensor_reduce(max1, eq, AX, ALU.add))
                step(nc.vector.tensor_copy(m.row[:, i, :], max1))


def scatter_stage(nc, d, m):
    with ExitStack() as ctx:
        sb, ps, sem = make_tools(nc, ctx)
        idx = sb("sc_idx", [P, 2, 2], U32)
        ready, idx_ready = sem("sc_ready"), sem("sc_idx_ready")
        sent = [sem("sc_sent0"), sem("sc_sent1")]
        block = ctx.enter_context(nc.Block())

        @block.vector
        def _(dve):
            def body(t, s):
                if not is_first(t):
                    dve.wait_ge(sent[s], 16 * (t - s))
                    dve.nop(nofuse=True)
                at = bass.ds(t, 1)
                nc.vector.tensor_copy(idx[:, s, :].unsqueeze(2), m.row[:, :, at]).then_inc(idx_ready, 1)
                nc.vector.tensor_scalar(m.tok_tile[:, s, :], m.tok[:, at, :].squeeze(1), m.mean[:, at], m.rstd[:, at],
                                        ALU.subtract, ALU.mult).then_inc(ready, 1)
            tiles(dve, body, peel=True)

        @block.gpsimd
        def _(pool):
            def body(t, s):
                pool.wait_ge(idx_ready, t + 1)
                pool.wait_ge(ready, t + 1)
                pool.nop(nofuse=True)
                n = TAIL if is_last(t) else P
                for i in range(2):
                    pool.indirect_dma_start(d.routed[:, :], bass.IndirectOffsetOnAxis(ap=idx[0:n, s, i:i + 1], axis=0),
                                            m.tok_tile[0:n, s, :], None).then_inc(sent[s], 16)
            tiles(pool, body)

        @block.sync
        def _(sp):
            for s in range(2):
                sp.wait_ge(sent[s], 32 * ((NT + 1 - s) // 2))


def expert_stage(nc, d, m):
    with ExitStack() as ctx:
        sb, ps, sem = make_tools(nc, ctx)
        w1 = sb("ex_w1", [P, 2, CB, HID])
        w2 = sb("ex_w2", [P, 2, HB, C])
        x = sb("ex_x", [P, TOK // P, C])
        xT = sb("ex_xT", [P, CB, TOK])
        hT = sb("ex_hT", [P, HB, TOK])
        y = sb("ex_y", [P, TOK // P, C])
        turned = ps("ex_turned", [P, CB, TOK])
        hidden = ps("ex_hidden", [P, HB, TOK])
        out = ps("ex_out", [P, TOK // P, C])
        x_loaded, turned_ready, x_ready, h_ready, h_out, y_ready, y_out, y_stored, y_free, expert_done = (
            sem("ex_" + n) for n in "x_loaded turned_ready x_ready h_ready h_out y_ready y_out y_stored y_free expert_done".split())
        w_loaded = [sem("ex_w_loaded0"), sem("ex_w_loaded1")]
        block = ctx.enter_context(nc.Block())

        def experts(eng, body):
            with eng.Fori(0, NX // 2) as i:
                for s in range(2):
                    e = i * 2 + s
                    n = eng.value_load(m.expert_i[0:1, 0:1, bass.ds(e, 1)].squeeze(1), min_val=1, max_val=-(-N // TOK))
                    before = eng.value_load(m.expert_i[0:1, 1:2, bass.ds(e, 1)].squeeze(1), min_val=0, max_val=MAX_TILES)
                    body(i, e, s, n, before)

        @block.gpsimd
        def _(pool):
            pool.sem_inc(expert_done, 2)
            with pool.Fori(0, NX // 2) as i:
                for s in range(2):
                    e = i * 2 + s
                    pool.wait_ge(expert_done, e + 1)
                    pool.dma_start(w1[:, s, :, :], d.W1[bass.ds(e, 1), :, :].squeeze(0).rearrange("(c p) h -> p c h", p=P)).then_inc(w_loaded[s], 16)
                    pool.dma_start(w2[:, s, :, :], d.W2[bass.ds(e, 1), :, :].squeeze(0).rearrange("(k p) c -> p k c", p=P)).then_inc(w_loaded[s], 16)

        @block.sync
        def _(sp):
            def row(tile):
                return nc.s_assert_within(tile * TOK, 0, ROWS - TOK,
                                          skip_runtime_bounds_check_because="the experts' tiles are at most MAX_TILES")

            def body(i, e, s, n, before):
                def load(j):
                    sp.wait_ge(turned_ready, before + e + j + 1)
                    sp.dma_start(x[:, :, :], d.routed[bass.ds(row(before + j), TOK), :].rearrange("(a p) c -> p a c", p=P))\
                        .then_inc(x_loaded, 16)
                load(0)
                with sp.Fori(0, n) as j:
                    load(j + 1)
                    sp.wait_ge(y_out, before + j + 2)
                    sp.dma_start(d.expert_out[bass.ds(row(before + j), TOK), :].rearrange("(a p) c -> p a c", p=P), y[:, :, :])\
                        .then_inc(y_stored, 16)
                    sp.wait_ge(y_stored, (before + j) * 16 + 16)
                    sp.sem_inc(y_free, 1)
            sp.sem_inc(y_free, 1)
            experts(sp, body)

        @block.tensor
        def _(pe):
            def body(i, e, s, n, before):
                def turn(j):
                    pe.wait_ge(x_loaded, (before + e + j) * 16 + 16)
                    pe.wait_ge(x_ready, before + e + j + 1)
                    for c in range(CB):
                        for a in range(TOK // P):
                            last = nc.tensor.transpose(turned[:, c, a * P:(a + 1) * P], x[:, a, c * P:(c + 1) * P], m.ident[:, :])
                    last.then_inc(turned_ready, 1)
                turn(0)
                pe.wait_ge(w_loaded[s], i * 32 + 32)
                pe.nop(nofuse=True)
                with pe.Fori(0, n) as j:
                    pe.wait_ge(x_ready, before + e + j + 2)
                    for h in range(HB):
                        for c in range(CB):
                            last = nc.tensor.matmul(hidden[:, h, :], w1[:, s, c, h * P:(h + 1) * P], xT[:, c, :],
                                                    start=c == 0, stop=c == CB - 1)
                        if h % HPB == HPB - 1:
                            last.then_inc(h_ready, 1)
                    turn(j + 1)
                    pe.wait_ge(y_out, before + j + 1)
                    for a in range(TOK // P):
                        for h in range(HB):
                            if a == 0:
                                pe.wait_ge(h_out, (before + j) * HB + (h + 1))
                            last = nc.tensor.matmul(out[:, a, :], hT[:, h, a * P:(a + 1) * P], w2[:, s, h, :],
                                                    start=h == 0, stop=h == HB - 1)
                    last.then_inc(y_ready, 1)
                pe.wait_ge(y_out, before + n + 1)
                pe.sem_inc(expert_done, 1)
            pe.sem_inc(turned_ready, 1)
            experts(pe, body)

        @block.scalar
        def _(act):
            def body(i, e, s, n, before):
                with act.Fori(0, n) as j:
                    for h in range(HB):
                        if h % HPB == 0:
                            act.wait_ge(h_ready, (before + j) * (HB // HPB) + (h // HPB + 1))
                        nc.scalar.activation(hT[:, h, :], hidden[:, h, :], ACT.Gelu,
                                             bias=m.b1[:, h:h + 1, bass.ds(e, 1)].squeeze(1)).then_inc(h_out, 1)
            experts(act, body)

        @block.vector
        def _(dve):
            def body(i, e, s, n, before):
                def gain(j):
                    dve.wait_ge(turned_ready, before + e + j + 2)
                    for c in range(CB):
                        last = nc.vector.tensor_scalar(xT[:, c, :], turned[:, c, :], m.ln_g[:, c:c + 1, bass.ds(e, 1)].squeeze(1),
                                                       m.ln_b[:, c:c + 1, bass.ds(e, 1)].squeeze(1), ALU.mult, ALU.add)
                    last.then_inc(x_ready, 1)
                gain(0)
                with dve.Fori(0, n) as j:
                    gain(j + 1)
                    dve.wait_ge(y_ready, before + j + 1)
                    dve.wait_ge(y_free, before + j + 1)
                    nc.vector.tensor_tensor(y[:, :, :], out[:, :, :], m.b2_all[:, bass.ds(e, 1), :].to_broadcast([P, TOK // P, C]),
                                            ALU.add).then_inc(y_out, 1)
            dve.sem_inc(x_ready, 1)
            dve.sem_inc(y_out, 1)
            experts(dve, body)


def combine_stage(nc, d, m):
    with ExitStack() as ctx:
        sb, ps, sem = make_tools(nc, ctx)
        idx = sb("cb_idx", [P, 2, 2], U32)
        rows = sb("cb_rows", [P, 2, 2, C])
        x2 = sb("cb_x2", [P, 2, C])
        res = sb("cb_res", [P, 2, C])
        idx_ready, half, done = sem("cb_idx_ready"), sem("cb_half"), sem("cb_done")
        got = [sem("cb_got0"), sem("cb_got1")]
        x2_loaded = [sem("cb_x2_loaded0"), sem("cb_x2_loaded1")]
        stored = [sem("cb_stored0"), sem("cb_stored1")]
        block = ctx.enter_context(nc.Block())

        @block.scalar
        def _(act):
            act.sem_inc(done, 2)

            def body(t, s):
                act.wait_ge(done, t + 1)
                nc.scalar.activation(idx[:, s, :].unsqueeze(2), m.row[:, :, bass.ds(t, 1)], ACT.Copy).then_inc(idx_ready, 1)
            tiles(act, body)

        @block.gpsimd
        def _(pool):
            def body(t, s):
                pool.wait_ge(idx_ready, t + 1)
                pool.nop(nofuse=True)
                n = TAIL if is_last(t) else P
                for i in range(2):
                    pool.indirect_dma_start(rows[0:n, s, i, :], None, d.expert_out[:, :],
                                            bass.IndirectOffsetOnAxis(ap=idx[0:n, s, i:i + 1], axis=0)).then_inc(got[s], 16)
            tiles(pool, body)

        @block.vector
        def _(dve):

            def body(t, s):
                n = TAIL if is_last(t) else P
                dve.wait_ge(got[s], 16 * (t - s) + 32)
                dve.wait_ge(x2_loaded[s], 8 * (t - s) + 16)
                if not is_first(t):
                    dve.wait_ge(stored[s], 8 * (t - s))
                at = bass.ds(t, 1)
                nc.vector.scalar_tensor_tensor(res[0:n, s, :], rows[0:n, s, 0, :], m.weight[0:n, 0, at], x2[0:n, s, :],
                                               ALU.mult, ALU.add).then_inc(half, 1)
                dve.wait_ge(half, t + 1)
                nc.vector.scalar_tensor_tensor(res[0:n, s, :], rows[0:n, s, 1, :], m.weight[0:n, 1, at], res[0:n, s, :],
                                               ALU.mult, ALU.add).then_inc(done, 1)
            tiles(dve, body, peel=True)

        @block.sync
        def _(sp):
            def load(t, s):
                if is_last(t):
                    sp.dma_start(x2[0:TAIL, s, :], d.x2[(NT - 1) * P:N, :]).then_inc(x2_loaded[s], 16)
                else:
                    sp.dma_start(x2[:, s, :], d.x2[bass.ds(t * P, P), :]).then_inc(x2_loaded[s], 16)

            def body(t, s):
                sp.wait_ge(done, t + 1)
                load(t, s)
                sp.wait_ge(done, t + 3)
                if is_last(t):
                    sp.dma_start(d.out[(NT - 1) * P:N, :], res[0:TAIL, s, :]).then_inc(stored[s], 16)
                else:
                    sp.dma_start(d.out[bass.ds(t * P, P), :], res[:, s, :]).then_inc(stored[s], 16)
            tiles(sp, body)
            for s in range(2):
                sp.wait_ge(stored[s], 16 * ((NT + 1 - s) // 2))


def build(nc, d):
    with ExitStack() as ctx:
        sb, ps, sem = make_tools(nc, ctx)
        m = Named()
        m.ident = sb("ident", [P, P])
        m.iota_i, m.iota = sb("iota_i", [P, W], I32), sb("iota", [P, W])
        m.offsets_i, m.offsets = sb("offsets_i", [P, N // W + 2], I32), sb("offsets", [P, N // W + 2])
        m.ones = sb("ones", [1, P])
        m.mean, m.rstd = sb("mean", [P, NT]), sb("rstd", [P, NT])
        m.weight = sb("weight", [P, 2, NT])
        m.row = sb("row", [P, 2, NT], U32)
        m.expert_i = sb("expert_i", [1, 2, NX], I32)
        m.w_mix = sb("w_mix", [P, CB, C])
        m.wr, m.br = sb("wr", [P, CB, NX]), sb("br", [1, NX])
        m.ln_g, m.ln_b = sb("ln_g", [P, CB, NX]), sb("ln_b", [P, CB, NX])
        m.b1 = sb("b1", [P, HB, NX])
        m.b_out = sb("b_out", [1, C])
        loads = [(m.wr[:, :, :], d.Wr.rearrange("(c p) e -> p c e", p=P)), (m.br[:, :], d.br),
                 (m.ln_g[:, :, :], d.ln_g), (m.ln_b[:, :, :], d.ln_b), (m.b1[:, :, :], d.b1), (m.b_out[:, :], d.b_out)]
        with ExitStack() as early:
            esb, _, _ = make_tools(nc, early)
            m.xT = esb("xT", [P, CB, NP])
            m.agg = esb("agg", [P, CB, AGW])
            with ExitStack() as convs:
                csb, _, _ = make_tools(nc, convs)
                m.src = csb("src", [P, NCH], U32)
                m.dst, m.ew = csb("dst", [P, NCH]), csb("ew", [P, NCH])
                m.base, m.extra = csb("base", [1, NGP], I32), csb("extra", [1, NGP], I32)
                m.extra_sum_f, m.extra_sum = csb("extra_sum_f", [1, NGP + 1]), csb("extra_sum", [1, NGP + 1], I32)
                m.w_kv = csb("w_kv", [P, CB, 2 * INNER])
                m.w_q = csb("w_q", [P, INNER // P, C])
                m.w_out = csb("w_out", [P, INNER // P, C])
                m.dots = csb("dots", [P, INNER // P, P])
                m.w1 = [csb(f"w1_{i}", [P, CB, C]) for i in range(2)]
                m.b1c = [csb(f"b1_{i}", [1, C]) for i in range(2)]
                m.w2 = [csb(f"w2_{i}", [P, CB, C]) for i in range(2)]
                vecs = csb("vecs", [P, 2, 5, CB])
                m.b2 = [vecs[:, i, 0, :] for i in range(2)]
                m.gains = [[(vecs[:, i, 1 + 2 * n, :], vecs[:, i, 2 + 2 * n, :]) for n in range(2)] for i in range(2)]
                m.x = m.agg[:, :, :].rearrange("p b n -> p (b n)")[:, 0:NT * C].rearrange("p (t c) -> p t c", c=C)
                m.weight_loads = loads + [
                    (m.w_kv[:, :, :], d.w_qkv[:, INNER:3 * INNER].rearrange("(c p) n -> p c n", p=P)),
                    (m.w_q[:, :, :], d.w_qT.rearrange("(b p) c -> p b c", p=P)),
                    (m.w_out[:, :, :], d.w_out.rearrange("(b p) c -> p b c", p=P))]
                for i in range(2):
                    m.weight_loads += [(m.w1[i][:, :, :], d.cw1[i].rearrange("(c p) n -> p c n", p=P)), (m.b1c[i][:, :], d.cb1[i]),
                                       (m.w2[i][:, :, :], d.cw2[i].rearrange("(c p) n -> p c n", p=P))]
                    for n, v in enumerate(d.cvecs[i]):
                        m.weight_loads.append((vecs[:, i, n, :], v))
                load_stage(nc, d, m)
                norm_stage(nc, m)
                for layer in range(2):
                    hidden_stage(nc, d, m, layer, m.agg if layer else m.xT, m.w1[layer], m.b1c[layer][0:1, :])
                    gather_stage(nc, d, m, mix=layer == 0)
                    batch_norm_stage(nc, d, m, layer, layer == 1)
            m.tok = esb("tok", [P, NT, C])
            m.tok_tile = esb("tok_tile", [P, 2, C])
            join_stage(nc, d, m)
            router_stage(nc, d, m)
            scatter_stage(nc, d, m)
        with ExitStack() as late:
            lsb, _, _ = make_tools(nc, late)
            m.b2_all = lsb("b2_all", [P, NX, C])
            b2_loaded = late.enter_context(nc.semaphore("b2_loaded"))
            with nc.Block() as block:
                @block.sync
                def _(sp):
                    sp.dma_start(m.b2_all[:, :, :], d.b2.unsqueeze(0).to_broadcast([P, NX, C])).then_inc(b2_loaded, 16)
                    sp.wait_ge(b2_loaded, 16)
            expert_stage(nc, d, m)
            combine_stage(nc, d, m)


def kernel(**inputs):
    from concourse import bacc
    from concourse.bass_utils import run_bass_kernel_spmd

    nc = bacc.Bacc("TRN2", target_bir_lowering=False, num_devices=1)
    g = "L0_gnn_"
    arrays = {}
    d = Named()

    def give(name, array):
        array = np.ascontiguousarray(array)
        arrays[name] = array
        return nc.dram_tensor(name, array.shape, mybir.dt.from_np(array.dtype), kind="ExternalInput").ap()

    def raw(name):
        return np.asarray(inputs[name])

    def edges(name, mode):
        return np.pad(raw(name), (0, NCH * P - E), mode=mode)

    def channels(array):
        return np.moveaxis(array.reshape(array.shape[:-1] + (array.shape[-1] // P, P)), -1, 0)

    d.x = give("x", raw("x"))
    dst = edges("dst", "edge")
    d.dst_rows = give("dst_rows", dst.reshape(NGP // 4, 4, GE))
    d.dst_cols = give("dst_cols", dst.reshape(NCH, P).T)
    d.src_cols = give("src_cols", edges("src", "edge").reshape(NCH, P).T.view(np.uint32))
    d.ew_cols = give("ew_cols", edges("edge_weight", "constant").reshape(NCH, P).T)
    d.cw1 = [give(f"c{i}_w1", raw(f"{g}c{i}_w1")) for i in (1, 2)]
    d.cb1 = [give(f"c{i}_b1", raw(f"{g}c{i}_b1")[None]) for i in (1, 2)]
    d.cw2 = [give(f"c{i}_w2", raw(f"{g}c{i}_w2")) for i in (1, 2)]
    d.cvecs = [[give(n, channels(raw(g + n))) for n in (f"c{i}_b2", f"c{i}_g", f"c{i}_b", f"bn{i}_g", f"bn{i}_b")] for i in (1, 2)]
    d.w_qkv = give("w_qkv", raw("L0_mix_w_qkv"))
    d.w_qT = give("w_qT", raw("L0_mix_w_qkv")[:, 0:INNER].T)
    d.w_out = give("w_out", raw("L0_mix_w_out"))
    d.b_out = give("b_out", raw("L0_mix_b_out")[None])
    d.Wr = give("Wr", raw("L0_ffn_Wr"))
    d.br = give("br", raw("L0_ffn_br")[None])
    d.ln_g = give("ln_g", np.moveaxis(channels(raw("L0_ffn_ln_g")), 1, 2))
    d.ln_b = give("ln_b", np.moveaxis(channels(raw("L0_ffn_ln_b")), 1, 2))
    d.W1 = give("W1", raw("L0_ffn_W1"))
    d.b1 = give("b1", np.moveaxis(channels(raw("L0_ffn_b1")), 1, 2))
    d.W2 = give("W2", raw("L0_ffn_W2"))
    d.b2 = give("b2", raw("L0_ffn_b2"))
    d.out = nc.dram_tensor("out", (N, C), F32, kind="ExternalOutput").ap()
    d.spans = nc.dram_tensor("spans", (2, NGP), I32, kind="Internal").ap()
    d.h = nc.dram_tensor("h", (NP, C), F32, kind="Internal").ap()
    d.x2 = nc.dram_tensor("x2", (N, C), F32, kind="Internal").ap()
    d.routed = nc.dram_tensor("routed", (ROWS, C), F32, kind="Internal").ap()
    d.expert_out = nc.dram_tensor("expert_out", (ROWS, C), F32, kind="Internal").ap()
    build(nc, d)
    r = run_bass_kernel_spmd(nc, [arrays], core_ids=[0])
    return r.results[0]["out"]
```

```python
import numpy as np
from contextlib import ExitStack

import concourse.bass as bass
from concourse import mybir

F32, F32R, BF16 = mybir.dt.float32, mybir.dt.float32r, mybir.dt.bfloat16
I32, U32 = mybir.dt.int32, mybir.dt.uint32
ALU = mybir.AluOpType
ACT = mybir.ActivationFunctionType
AX = mybir.AxisListType.X

P = 128
N, C = 6250, 256
CB = C // P
NT = -(-N // P)
NP = NT * P
TAIL = N - (NT - 1) * P
EPS = 1e-5

E = 206250
GC = 4
GE = GC * P
NG = -(-E // GE)
NGP = -(-NG // 4) * 4
NCH = NGP * GC
SLOTS = 4
W = 64
AGW = -(-(N + W) // P) * P

HEADS, DH = 8, 64
INNER = HEADS * DH
NX = 8
HID = 1024
HB = HID // P
TOK = 256
MAX_TILES = 2 * N // TOK + NX
ROWS = (MAX_TILES + 2) * TOK
ZEROS = 2 * C
HPB = 512 // TOK
NODE_CHUNK = 512
NODE_CHUNKS = [(a, min(NODE_CHUNK, N - a)) for a in range(0, N, NODE_CHUNK)]
FULL_CHUNKS = N // NODE_CHUNK
BNS = 6


class Named:
    pass


def make_tools(nc, ctx, stage=""):
    def sb(name, shape, dt=F32):
        return ctx.enter_context(nc.sbuf_tensor(f"sb_{stage}{name}", shape, dt))

    def ps(name, shape, dt=F32):
        return ctx.enter_context(nc.psum_tensor(f"ps_{stage}{name}", shape, dt))

    def sem(name):
        return ctx.enter_context(nc.semaphore(f"{stage}{name}"))

    return sb, ps, sem


class Steps:

    def __init__(self, eng, sem):
        self.eng, self.sem, self.n = eng, sem, 0

    def __call__(self, instruction):
        instruction.then_inc(self.sem, 1)
        self.n += 1
        self.eng.wait_ge(self.sem, self.n)


def tiles(eng, body, slots=2, peel=False):
    if peel:
        for s in range(slots):
            body(s, s)
    with eng.Fori(1 if peel else 0, NT // slots) as i:
        for s in range(slots):
            body(i * slots + s, s)
    for t in range(NT // slots * slots, NT):
        body(t, t % slots)


def visits(slots, s):
    return (NT - 1 - s) // slots + 1


def is_last(t):
    return isinstance(t, int) and t == NT - 1


def is_first(t, slots=2):
    return isinstance(t, int) and t < slots


def load_stage(nc, d, m):
    with ExitStack() as ctx:
        sb, ps, sem = make_tools(nc, ctx)
        dst_rows = sb("dst_rows", [NGP // 4, 4, GE], I32)
        span = sb("span", [NGP // 4, 2, 4], F32)
        span_i = sb("span_i", [NGP // 4, 2, 4], I32)
        base_bc = sb("base_bc", [P, NGP], I32)
        base_f = sb("base_f", [P, NGP])
        dst_cols = sb("dst_cols", [P, NCH], I32)
        lasts = sb("lasts", [1, NGP], I32)
        extra_f = sb("extra_f", [1, NGP])
        zeros = sb("zeros", [1, NGP])
        stats = sb("stats", [P, NT, BNS])
        tmp = sb("tmp", [P, NT, 4])
        head_mean = sb("head_mean", [P, CB * 2 * HEADS])
        x_loaded, dst_loaded, const_loaded = sem("x_loaded"), sem("dst_loaded"), sem("const_loaded")
        tables_back, span_stored, span_ready = sem("tables_back"), sem("span_stored"), sem("span_ready")
        x_cleared, dve_done, stats_done, root_done = sem("x_cleared"), sem("dve_done"), sem("stats_done"), sem("root_done")
        ident_step = sem("ident_step")
        var_ready, root_step = sem("var_ready"), sem("root_step")
        block = ctx.enter_context(nc.Block())

        @block.sync
        def _(sp):
            sp.wait_ge(x_cleared, 1)
            sp.dma_start(m.x[:, 0:NT - 1, :], d.x[0:(NT - 1) * P, :].rearrange("(t p) c -> p t c", p=P)).then_inc(x_loaded, 16)
            sp.dma_start(m.x[0:TAIL, NT - 1, :], d.x[(NT - 1) * P:N, :]).then_inc(x_loaded, 16)
            sp.wait_ge(span_ready, 1)
            sp.dma_start(d.spans[:, :].rearrange("k (p g) -> p k g", g=4), span_i[:, :, :]).then_inc(span_stored, 16)
            sp.wait_ge(span_stored, 16)
            sp.dma_start(base_bc[:, :], d.spans[0:1, :].to_broadcast([P, NGP])).then_inc(tables_back, 16)
            sp.dma_start(m.base[:, :], d.spans[0:1, :]).then_inc(tables_back, 16)
            sp.dma_start(lasts[:, :], d.spans[1:2, :]).then_inc(tables_back, 16)

        @block.scalar
        def _(act):
            act.dma_start(dst_rows[:, :, :], d.dst_rows).then_inc(dst_loaded, 16)
            act.dma_start(dst_cols[:, :], d.dst_cols).then_inc(const_loaded, 16)
            act.dma_start(m.src[:, :], d.src_cols).then_inc(const_loaded, 16)
            act.dma_start(m.ew[:, :], d.ew_cols).then_inc(const_loaded, 16)
            for to, frm in m.weight_loads:
                act.dma_start(to, frm).then_inc(const_loaded, 16)
            act.wait_ge(const_loaded, 16 * (3 + len(m.weight_loads)))
            act.wait_ge(var_ready, 1)
            act.activation(tmp[:, :, 3], tmp[:, :, 2], ACT.Sqrt).then_inc(root_done, 1)

        @block.gpsimd
        def _(pool):
            step = Steps(pool, ident_step)
            step(pool.memset(m.ident[:, :], 0.0))
            step(pool.affine_select(out=m.ident[:, :], in_=m.ident[:, :], compare_op=ALU.not_equal, fill=1.0,
                                    base=0, pattern=[[-1, P]], channel_multiplier=1))
            step(pool.iota(m.iota_i[:, :], [[1, W]], base=0, channel_multiplier=0))
            step(pool.tensor_copy(m.iota[:, :], m.iota_i[:, :]))
            step(pool.iota(m.offsets_i[:, :], [[W, N // W + 2]], base=0, channel_multiplier=0))
            step(pool.tensor_copy(m.offsets[:, :], m.offsets_i[:, :]))
            step(pool.memset(m.ones[:, :], 1.0))

        @block.vector
        def _(dve):
            nc.vector.memset(m.x[:, NT - 1, :], 0.0).then_inc(x_cleared, 1)
            step = Steps(dve, dve_done)
            dve.wait_ge(dst_loaded, 16)
            step(nc.vector.tensor_reduce(span[:, 0, :], dst_rows[:, :, :], AX, ALU.min))
            step(nc.vector.tensor_reduce(span[:, 1, :], dst_rows[:, :, :], AX, ALU.max))
            nc.vector.tensor_copy(span_i[:, :, :], span[:, :, :]).then_inc(span_ready, 1)
            dve.wait_ge(x_loaded, 32)
            with dve.Fori(0, NT) as t:
                nc.vector.bn_stats(stats[:, bass.ds(t, 1), :].squeeze(1), m.x[:, bass.ds(t, 1), :].squeeze(1)).then_inc(stats_done, 1)
            dve.wait_ge(stats_done, NT)
            merge_stats(nc, step, stats, tmp, m.mean[:, :])
            step(nc.vector.tensor_scalar(tmp[:, :, 2], tmp[:, :, 2], EPS, None, ALU.add))
            step(nc.vector.memset(zeros[:, :], 0.0))
            dve.sem_inc(var_ready, 1)
            dve.wait_ge(tables_back, 48)
            step(nc.vector.tensor_tensor(lasts[:, :], lasts[:, :], m.base[:, :], ALU.subtract))
            step(nc.vector.tensor_scalar(m.extra[:, :], lasts[:, :], W.bit_length() - 1, None, ALU.logical_shift_right))
            step(nc.vector.tensor_copy(extra_f[:, :], m.extra[:, :]))
            step(nc.vector.tensor_tensor_scan(m.extra_sum_f[:, 1:NGP + 1], extra_f[:, :], zeros[:, :], 0.0, ALU.add, ALU.add))
            step(nc.vector.memset(m.extra_sum_f[:, 0:1], 0.0))
            step(nc.vector.tensor_copy(m.extra_sum[:, :], m.extra_sum_f[:, :]))
            step(nc.vector.tensor_copy(base_f[:, :], base_bc[:, :]))
            dve.wait_ge(const_loaded, 16 * (3 + len(m.weight_loads)))
            step(nc.vector.tensor_copy(m.dst[:, :], dst_cols[:, :]))
            heads = m.w_kv[:, :, :].rearrange("p c (h e) -> p (c h) e", e=DH)
            step(nc.vector.tensor_reduce(head_mean[:, :], heads, AX, ALU.add))
            step(nc.vector.tensor_scalar(head_mean[:, :], head_mean[:, :], 1.0 / DH, None, ALU.mult))
            step(nc.vector.tensor_tensor(heads, heads, head_mean[:, :].unsqueeze(2).to_broadcast([P, CB * 2 * HEADS, DH]), ALU.subtract))
            by_group = m.dst[:, :].rearrange("p (g k) -> p g k", k=GC)
            step(nc.vector.tensor_tensor(by_group, by_group, base_f[:, :].unsqueeze(2).to_broadcast([P, NGP, GC]), ALU.subtract))
            dve.wait_ge(root_done, 1)
            step(nc.vector.reciprocal(m.rstd[:, :], tmp[:, :, 3]))


def merge_stats(nc, step, stats, tmp, mean):
    me, mo = stats[:, :, 1], stats[:, :, 4]
    step(nc.vector.tensor_tensor(tmp[:, :, 0], me, mo, ALU.add))
    step(nc.vector.tensor_scalar(mean, tmp[:, :, 0], 0.5, None, ALU.mult))
    step(nc.vector.tensor_tensor(tmp[:, :, 0], me, mo, ALU.subtract))
    step(nc.vector.tensor_tensor(tmp[:, :, 0], tmp[:, :, 0], tmp[:, :, 0], ALU.mult))
    step(nc.vector.tensor_tensor(tmp[:, :, 1], stats[:, :, 2], stats[:, :, 5], ALU.add))
    step(nc.vector.tensor_scalar(tmp[:, :, 1], tmp[:, :, 1], 1.0 / C, None, ALU.mult))
    step(nc.vector.scalar_tensor_tensor(tmp[:, :, 2], tmp[:, :, 0], 0.25, tmp[:, :, 1], ALU.mult, ALU.add))


def norm_stage(nc, m):
    with ExitStack() as ctx:
        sb, ps, sem = make_tools(nc, ctx)
        xn = sb("xn", [P, 2, C])
        turned = ps("turned", [P, 2, NODE_CHUNK])
        normed, turned_ready, turned_used = sem("normed"), sem("turned_ready"), sem("turned_used")
        block = ctx.enter_context(nc.Block())

        @block.vector
        def _(dve):
            dve.sem_inc(turned_ready, 2)

            def body(t, s):
                dve.wait_ge(turned_ready, t + 1)
                nc.vector.tensor_scalar(xn[:, s, :], m.x[:, bass.ds(t, 1), :].squeeze(1), m.mean[:, bass.ds(t, 1)],
                                        m.rstd[:, bass.ds(t, 1)], ALU.subtract, ALU.mult).then_inc(normed, 1)
            tiles(dve, body)

        @block.tensor
        def _(pe):
            def body(t, s):
                pe.wait_ge(normed, t + 1)
                pe.wait_ge(turned_used, t + 1)
                for c in range(CB):
                    last = nc.tensor.transpose(turned[:, s, c * P:(c + 1) * P], xn[:, s, c * P:(c + 1) * P], m.ident[:, :])
                last.then_inc(turned_ready, 1)
            tiles(pe, body)

        @block.scalar
        def _(act):
            act.sem_inc(turned_used, 2)

            def body(t, s):
                act.wait_ge(turned_ready, t + 3)
                act.activation(m.xT[:, :, bass.ds(t * P, P)], turned[:, s, 0:C].rearrange("p (c n) -> p c n", c=CB),
                               ACT.Copy).then_inc(turned_used, 1)
            tiles(act, body)


def hidden_stage(nc, d, m, layer, srcT, w, b):
    with ExitStack() as ctx:
        sb, ps, sem = make_tools(nc, ctx, f"hidden{layer}_")
        a_tile = sb("a_tile", [P, 2, CB, P])
        h_tile = sb("h_tile", [P, 2, C])
        acc = ps("acc", [P, 2, NODE_CHUNK])
        staged, product, relued = sem("staged"), sem("product"), sem("relued")
        stored = [sem("stored_0"), sem("stored_1")]
        block = ctx.enter_context(nc.Block())

        @block.scalar
        def _(act):
            act.sem_inc(product, 2)

            def body(t, s):
                act.wait_ge(product, t + 1)
                act.activation(a_tile[:, s, :, :], srcT[:, :, bass.ds(t * P, P)], ACT.Copy).then_inc(staged, 1)
            tiles(act, body)

        @block.tensor
        def _(pe):
            def body(t, s):
                pe.wait_ge(staged, t + 1)
                pe.wait_ge(relued, t + 1)
                nc.tensor.matmul(acc[:, s, 0:C], m.ones[0:1, :], b, start=True, stop=False)
                for c in range(CB):
                    last = nc.tensor.matmul(acc[:, s, 0:C], a_tile[:, s, c, :], w[:, c, :], start=False, stop=c == CB - 1)
                last.then_inc(product, 1)
            tiles(pe, body)

        @block.vector
        def _(dve):
            dve.sem_inc(relued, 2)

            def body(t, s):
                dve.wait_ge(product, t + 3)
                if not is_first(t):
                    dve.wait_ge(stored[s], 8 * (t - s))
                nc.vector.tensor_scalar(h_tile[:, s, :], acc[:, s, 0:C], 0.0, None, ALU.max).then_inc(relued, 1)
            tiles(dve, body, peel=True)

        @block.sync
        def _(sp):
            def body(t, s):
                sp.wait_ge(relued, t + 3)
                sp.dma_start(d.h[bass.ds(t * P, P), :], h_tile[:, s, :]).then_inc(stored[s], 16)
            tiles(sp, body)
            for s in range(2):
                sp.wait_ge(stored[s], 16 * ((NT + 1 - s) // 2))


def gather_stage(nc, d, m, mix):
    with ExitStack() as ctx:
        sb, ps, sem = make_tools(nc, ctx, "gather_mix_" if mix else "gather_")
        rows = sb("rows", [P, SLOTS, GC, C])
        idx = sb("idx", [P, SLOTS, GC], U32)
        sel = sb("sel", [P, 2, GC, W])
        hit_x = sb("hit_x", [P, GC, W])
        sel_x = sb("sel_x", [P, GC, W])
        parts = [ps(f"part{i}", [P, NODE_CHUNK]) for i in range(3)]
        part = [x[:, 0:CB * W].rearrange("p (b w) -> p b w", b=CB) for x in parts]
        part_x = part[2]
        gathered = [sem(f"gathered{i}") for i in range(SLOTS)]
        idx_ready, sel_ready, summed, added = sem("idx_ready"), sem("sel_ready"), sem("summed"), sem("added")
        cleared = sem("cleared")
        x_hit, x_sel, x_summed, x_added = sem("x_hit"), sem("x_sel"), sem("x_summed"), sem("x_added")
        k = mixer_parts(sb, ps, sem) if mix else None
        if not mix:
            zeros, blanked = sb("zeros", [P, ZEROS]), sem("blanked")
        block = ctx.enter_context(nc.Block())

        first = PER_MIX * NT if mix else 0
        turns = (NG - first) // SLOTS
        rest = first + turns * SLOTS

        def groups(group, eng, hooks=()):
            if mix:
                def some(t, s):
                    for j in range(PER_MIX):
                        group(t * PER_MIX + j, j % SLOTS)
                        if j in hooks:
                            hooks[j](t, s)
                tiles(eng, some)
            with eng.Fori(0, turns) as i:
                for j in range(SLOTS):
                    group(i * SLOTS + (first + j), j)
            for g in range(rest, NG):
                group(g, g % SLOTS)

        if not mix:
            @block.sync
            def _(sp):
                sp.wait_ge(cleared, 1)
                blank = zeros[:, :].unsqueeze(1).to_broadcast([P, ROWS * C // P // ZEROS, ZEROS])
                for to in (d.routed, d.expert_out):
                    sp.dma_start(to.rearrange("(p a) c -> p (a c)", p=P).rearrange("p (b z) -> p b z", z=ZEROS), blank).then_inc(blanked, 16)
                sp.wait_ge(blanked, 32)

        @block.gpsimd
        def _(pool):
            def group(g, s):
                pool.wait_ge(idx_ready, g + 1)
                pool.nop(nofuse=True)
                for c in range(GC):
                    pool.indirect_dma_start(rows[:, s, c, :], None, d.h[:, :],
                                            bass.IndirectOffsetOnAxis(ap=idx[:, s, c:c + 1], axis=0)).then_inc(gathered[s], 16)
            groups(group, pool)

        @block.scalar
        def _(act):
            act.sem_inc(added, SLOTS)
            act.sem_inc(x_added, 1)

            def group(g, s):
                act.wait_ge(added, g + 1)
                nc.scalar.activation(idx[:, s, :], m.src[:, bass.ds(g * GC, GC)], ACT.Copy).then_inc(idx_ready, 1)

            def stage_tile(t, s):
                act.wait_ge(k.dots_done, t + 1)
                nc.scalar.activation(k.x_tile[:, s, :, :], m.xT[:, :, bass.ds(t * P, P)], ACT.Copy).then_inc(k.staged, 1)

            def square(t, s):
                act.wait_ge(k.kv_ready, t + 1)
                kv_psum = k.kv_psum[:, :, :].rearrange("p a n -> p (a n)")
                nc.scalar.activation(k.kv[:, s, :], kv_psum, ACT.Copy).then_inc(k.kv_out, 1)
                act.wait_ge(k.var_out, t + 1)
                act.wait_ge(k.kv_out, t + 2)
                nc.scalar.activation(k.squares[:, :], k.kv[:, s, :], ACT.Square).then_inc(k.squared, 1)

            def root(t, s):
                act.wait_ge(k.var_out, t + 2)
                nc.scalar.activation(k.root[:, s, :], k.var[:, s, :], ACT.Sqrt).then_inc(k.rooted, 1)
            if mix:
                act.sem_inc(k.dots_done, 2)
                act.sem_inc(k.kv_out, 1)
                act.sem_inc(k.var_out, 1)
            groups(group, act, {0: stage_tile, 5: square, 7: root})

        @block.tensor
        def _(pe):
            def group(g, s):
                extra = pe.value_load(m.extra[0:1, bass.ds(g, 1)], min_val=0, max_val=N // W)
                pe.wait_ge(gathered[s], (g - s) * (16 * GC // SLOTS) + 16 * GC)
                pe.wait_ge(sel_ready, g + 1)
                pe.wait_ge(added, g + SLOTS - 1)
                for b in range(CB):
                    for c in range(GC):
                        last = nc.tensor.matmul(part[s % 2][:, b, :], rows[:, s, c, b * P:(b + 1) * P], sel[:, s % 2, c, :],
                                                start=c == 0, stop=c == GC - 1)
                last.then_inc(summed, 1)
                with pe.If(extra > 0):
                    before = pe.value_load(m.extra_sum[0:1, bass.ds(g, 1)], min_val=0, max_val=NG * (N // W))
                    with pe.Fori(0, extra) as j:
                        pe.wait_ge(x_sel, before + j + 1)
                        pe.wait_ge(x_added, before + j + 1)
                        for b in range(CB):
                            for c in range(GC):
                                last = nc.tensor.matmul(part_x[:, b, :], rows[:, s, c, b * P:(b + 1) * P], sel_x[:, c, :],
                                                        start=c == 0, stop=c == GC - 1)
                        last.then_inc(x_summed, 1)
                    pe.nop(nofuse=True)
                with pe.Else():
                    pe.nop(nofuse=True)

            def keys_values(t, s):
                pe.wait_ge(k.staged, t + 1)
                pe.wait_ge(k.kv_out, t + 1)
                for half in range(2):
                    for c in range(CB):
                        last = nc.tensor.matmul(k.kv_psum[:, half, :], k.x_tile[:, s, c, :],
                                                m.w_kv[:, c, half * INNER:(half + 1) * INNER], start=c == 0, stop=c == CB - 1)
                last.then_inc(k.kv_ready, 1)

            def dots(t, s):
                pe.wait_ge(k.scaled, t + 1)
                ends = is_last(t)
                for b in range(INNER // P):
                    last = nc.tensor.matmul(k.dots[:, b * P:(b + 1) * P], k.kv[:, s, INNER + b * P:INNER + (b + 1) * P],
                                            k.kv[:, s, b * P:(b + 1) * P], start=False, stop=ends, skip_group_check=True)
                last.then_inc(k.dots_done, 1)
            if mix:
                pe.wait_ge(cleared, 1)
                nc.tensor.matmul(k.dots[:, :], m.ident[:, :], m.agg[:, 0, 0:INNER], start=True, stop=False, skip_group_check=True)\
                    .then_inc(k.zeroed, 1)
            groups(group, pe, {0: keys_values, 7: dots})

        @block.vector
        def _(dve):
            if not mix:
                nc.vector.memset(zeros[:, :], 0.0)
            nc.vector.memset(m.agg[:, :, :], 0.0).then_inc(cleared, 1)
            dve.wait_ge(cleared, 1)
            if mix:
                dve.wait_ge(k.zeroed, 1)

            def select(g, s):
                for c in range(GC):
                    at = bass.ds(g * GC + c, 1)
                    last = nc.vector.tensor_scalar(sel[:, s % 2, c, :], m.iota[:, :], m.dst[:, at], m.ew[:, at],
                                                   ALU.is_equal, ALU.mult)
                last.then_inc(sel_ready, 1)

            def group(g, s):
                select(g + 1, (s + 1) % SLOTS)
                base = dve.value_load(m.base[0:1, bass.ds(g, 1)], min_val=0, max_val=N - 1)
                extra = dve.value_load(m.extra[0:1, bass.ds(g, 1)], min_val=0, max_val=N // W)
                with dve.If(extra > 0):
                    before = dve.value_load(m.extra_sum[0:1, bass.ds(g, 1)], min_val=0, max_val=NG * (N // W))
                    with dve.Fori(0, extra) as j:
                        for c in range(GC):
                            last = nc.vector.tensor_scalar(hit_x[:, c, :], m.iota[:, :], m.offsets[:, bass.ds(j + 1, 1)],
                                                           m.dst[:, bass.ds(g * GC + c, 1)], ALU.add, ALU.is_equal)
                        last.then_inc(x_hit, 1)
                        dve.wait_ge(x_hit, before + j + 1)
                        for c in range(GC):
                            last = nc.vector.tensor_scalar(sel_x[:, c, :], hit_x[:, c, :], m.ew[:, bass.ds(g * GC + c, 1)],
                                                           None, ALU.mult)
                        last.then_inc(x_sel, 1)
                        dve.wait_ge(x_summed, before + j + 1)
                        dve.wait_ge(added, g + SLOTS)
                        start = nc.s_assert_within(base + (j + 1) * W, 0, N - 1,
                                                   skip_runtime_bounds_check_because="the windows end with the last destination")
                        to = m.agg[:, :, bass.ds(start, W)]
                        nc.vector.tensor_tensor(to, part_x[:, :, :], to, ALU.add).then_inc(x_added, 1)
                    dve.wait_ge(x_added, before + extra + 1)
                    dve.nop(nofuse=True)
                with dve.Else():
                    dve.nop(nofuse=True)
                dve.wait_ge(summed, g + 1)
                dve.wait_ge(added, g + SLOTS)
                to = m.agg[:, :, bass.ds(base, W)]
                nc.vector.tensor_tensor(to, part[s % 2][:, :, :], to, ALU.add).then_inc(added, 1)

            def variance(t, s):
                dve.wait_ge(k.squared, t + 1)
                nc.vector.tensor_reduce(k.sums[:, :], k.squares[:, :].rearrange("p (h e) -> p h e", e=DH), AX, ALU.add).then_inc(k.sum_out, 1)
                dve.wait_ge(k.sum_out, t + 1)
                nc.vector.tensor_scalar(k.var[:, s, :], k.sums[:, :], 1.0 / DH, EPS, ALU.mult, ALU.add).then_inc(k.var_out, 1)

            def scale(t, s):
                dve.wait_ge(k.rooted, t + 1)
                nc.vector.tensor_tensor(k.both[:, :], k.root[:, s, 0:HEADS], k.root[:, s, HEADS:2 * HEADS], ALU.mult).then_inc(k.both_out, 1)
                dve.wait_ge(k.both_out, t + 1)
                nc.vector.reciprocal(k.rstd[:, :], k.both[:, :]).then_inc(k.rstd_out, 1)
                dve.wait_ge(k.rstd_out, t + 1)
                keys = k.kv[:, s, 0:INNER].rearrange("p (h e) -> p h e", e=DH)
                nc.vector.tensor_tensor(keys, keys, k.rstd[:, :].unsqueeze(2).to_broadcast([P, HEADS, DH]), ALU.mult).then_inc(k.scaled, 1)
            select(0, 0)
            groups(group, dve, {3: variance, 5: scale})
            if mix:
                dve.wait_ge(k.dots_done, NT + 2)
                nc.vector.memset(m.dots[:, :, :], 0.0).then_inc(k.final, 1)
                dve.wait_ge(k.final, 1)
                dots = k.dots[:, :].rearrange("p (b n) -> p b n", n=P)
                for a in (0, DH):
                    nc.vector.tensor_copy(m.dots[a:a + DH, :, a:a + DH], dots[a:a + DH, :, a:a + DH]).then_inc(k.final, 1)


PER_MIX = 8


def mixer_parts(sb, ps, sem):
    k = Named()
    k.x_tile = sb("mx_x", [P, 2, CB, P])
    k.kv = sb("mx_kv", [P, 2, 2 * INNER])
    k.squares = sb("mx_squares", [P, 2 * INNER])
    k.sums = sb("mx_sums", [P, 2 * HEADS])
    k.var = sb("mx_var", [P, 2, 2 * HEADS])
    k.root = sb("mx_root", [P, 2, 2 * HEADS])
    k.both = sb("mx_both", [P, HEADS])
    k.rstd = sb("mx_rstd", [P, HEADS])
    k.kv_psum = ps("mx_kv_psum", [P, 2, INNER])
    k.dots = ps("mx_dots", [P, INNER])
    k.staged, k.kv_ready, k.kv_out, k.squared = sem("mx_staged"), sem("mx_kv_ready"), sem("mx_kv_out"), sem("mx_squared")
    k.sum_out, k.var_out, k.rooted, k.both_out = sem("mx_sum_out"), sem("mx_var_out"), sem("mx_rooted"), sem("mx_both_out")
    k.rstd_out, k.scaled, k.dots_done = sem("mx_rstd_out"), sem("mx_scaled"), sem("mx_dots_done")
    k.zeroed, k.final = sem("mx_zeroed"), sem("mx_final")
    return k


def batch_norm_stage(nc, d, m, layer, last_layer):
    with ExitStack() as ctx:
        sb, ps, sem = make_tools(nc, ctx, f"norm{layer}_")
        stats = sb("bn_stats", [P, CB, len(NODE_CHUNKS), BNS])
        mv = sb("bn_mv", [P, CB, 2])
        root = sb("bn_root", [P, CB])
        scale = sb("bn_scale", [P, CB])
        shift = sb("bn_shift", [P, CB])
        acc = ps("bn_acc", [P, 2, CB, NODE_CHUNK])
        product, biased, steps, var_ready, rooted, scaled, applied, counted, part_done = (
            sem("bn_" + x) for x in "product biased steps var_ready rooted scaled applied counted part_done".split())
        mixing = layer == 0
        if mixing:
            mid_psum = ps("mid_psum", [P, 2, NODE_CHUNK])
            mid = sb("mid", [P, INNER // P, C])
            mid_ready, mid_out, mix_ready, mix_out = (sem(x) for x in "mid_ready mid_out mix_ready mix_out".split())
        block = ctx.enter_context(nc.Block())
        w2, b2 = m.w2[layer], m.b2[layer]
        gains = m.gains[layer]
        nchunk = len(NODE_CHUNKS)

        def chunks(eng, body):
            with eng.Fori(0, FULL_CHUNKS // 2) as i:
                body(i * 2, 0, bass.ds(i * (2 * NODE_CHUNK), NODE_CHUNK), NODE_CHUNK)
                body(i * 2 + 1, 1, bass.ds(i * (2 * NODE_CHUNK) + NODE_CHUNK, NODE_CHUNK), NODE_CHUNK)
            for i in range(FULL_CHUNKS // 2 * 2, nchunk):
                a, n = NODE_CHUNKS[i]
                body(i, i % 2, slice(a, a + n), n)

        @block.tensor
        def _(pe):
            def body(i, s, cols, n):
                pe.wait_ge(biased, i + 1)
                for b in range(CB):
                    for c in range(CB):
                        last = nc.tensor.matmul(acc[:, s, b, 0:n], w2[:, c, b * P:(b + 1) * P], m.agg[:, c, cols],
                                                start=c == 0, stop=c == CB - 1)
                last.then_inc(product, 1)
            chunks(pe, body)
            if mixing:
                for b in range(INNER // P):
                    if b >= 2:
                        pe.wait_ge(mid_out, b - 1)
                    nc.tensor.matmul(mid_psum[:, b % 2, 0:C], m.dots[:, b, :], m.w_out[:, b, :], start=True, stop=True).then_inc(mid_ready, 1)
                pe.wait_ge(mid_out, INNER // P)
                for c in range(CB):
                    for b in range(INNER // P):
                        last = nc.tensor.matmul(mid_psum[:, c, 0:C], m.w_q[:, b, c * P:(c + 1) * P], mid[:, b, :],
                                                start=b == 0, stop=b == INNER // P - 1)
                    last.then_inc(mix_ready, 1)

        @block.scalar
        def _(act):
            act.sem_inc(biased, 2)

            def body(i, s, cols, n):
                act.wait_ge(product, i + 1)
                for b in range(CB):
                    ins = nc.scalar.activation(m.agg[:, b, cols], acc[:, s, b, 0:n], ACT.Identity, bias=b2[:, b:b + 1])
                ins.then_inc(biased, 1)
            chunks(act, body)
            if mixing:
                for b in range(INNER // P):
                    act.wait_ge(mid_ready, b + 1)
                    nc.scalar.activation(mid[:, b, :], mid_psum[:, b % 2, 0:C], ACT.Copy).then_inc(mid_out, 1)
                for c in range(CB):
                    act.wait_ge(mix_ready, c + 1)
                    nc.scalar.activation(m.w_mix[:, c, :], mid_psum[:, c, 0:C], ACT.Copy, scale=1.0 / N).then_inc(mix_out, 1)
            for norm in range(2):
                act.wait_ge(var_ready, norm + 1)
                nc.scalar.activation(root[:, :], mv[:, :, 1], ACT.Sqrt).then_inc(rooted, 1)
                act.wait_ge(scaled, norm + 1)
                ends = norm == 1 and last_layer

                def apply(i, s, cols, n):
                    if ends:
                        act.wait_ge(part_done, i + 1)
                        for b in range(CB):
                            ins = nc.scalar.activation(m.agg[:, b, cols], m.agg[:, b, cols], ACT.Relu, bias=shift[:, b:b + 1])
                    else:
                        for b in range(CB):
                            ins = nc.scalar.activation(m.agg[:, b, cols], m.agg[:, b, cols], ACT.Relu, bias=shift[:, b:b + 1],
                                                       scale=scale[:, b:b + 1])
                    ins.then_inc(applied, 1)
                chunks(act, apply)

        @block.vector
        def _(dve):
            step = Steps(dve, steps)
            for norm in range(2):
                def count(i, s, cols, n):
                    if norm:
                        dve.wait_ge(applied, i + 1)
                    else:
                        dve.wait_ge(biased, i + 3)
                    at = bass.ds(i, 1)
                    for b in range(CB):
                        ins = nc.vector.bn_stats(stats[:, b, at, :].squeeze(1), m.agg[:, b, cols])
                    ins.then_inc(counted, 1)
                chunks(dve, count)
                dve.wait_ge(counted, nchunk * (norm + 1))
                for b in range(CB):
                    step(nc.vector.bn_aggr(mv[:, b, :], stats[:, b, :, :].rearrange("p a b -> p (a b)")))
                step(nc.vector.tensor_scalar(mv[:, :, 1], mv[:, :, 1], EPS, None, ALU.add))
                dve.sem_inc(var_ready, 1)
                dve.wait_ge(rooted, norm + 1)
                step(nc.vector.reciprocal(scale[:, :], root[:, :]))
                step(nc.vector.tensor_tensor(scale[:, :], scale[:, :], gains[norm][0], ALU.mult))
                step(nc.vector.tensor_tensor(shift[:, :], scale[:, :], mv[:, :, 0], ALU.mult))
                step(nc.vector.tensor_tensor(shift[:, :], gains[norm][1], shift[:, :], ALU.subtract))
                dve.sem_inc(scaled, 1)
            if last_layer:
                def residual(i, s, cols, n):
                    for b in range(CB):
                        ins = nc.vector.scalar_tensor_tensor(m.agg[:, b, cols], m.agg[:, b, cols], scale[:, b:b + 1],
                                                             m.xT[:, b, cols], ALU.mult, ALU.add)
                    ins.then_inc(part_done, 1)
                chunks(dve, residual)
            dve.wait_ge(applied, nchunk * 2)


def join_stage(nc, d, m):
    with ExitStack() as ctx:
        sb, ps, sem = make_tools(nc, ctx)
        x_tile = sb("jn_x", [P, 2, C])
        xT_tile = sb("jn_xT", [P, 2, CB, P])
        gT_tile = sb("jn_gT", [P, 2, CB, P])
        stats = sb("jn_stats", [P, NT, BNS])
        tmp = sb("jn_tmp", [P, NT, 4])
        acc = ps("jn_acc", [P, 2, NODE_CHUNK])
        staged, product, joined, counted, steps, var_ready, rooted, cleared = (
            sem("jn_" + x) for x in "staged product joined counted steps var_ready rooted cleared".split())
        loaded = [sem("jn_loaded0"), sem("jn_loaded1")]
        stored = sem("jn_stored")
        block = ctx.enter_context(nc.Block())

        @block.sync
        def _(sp):
            sp.wait_ge(cleared, 1)

            def body(t, s):
                sp.wait_ge(joined, t + 1)
                if is_last(t):
                    sp.dma_start(x_tile[0:TAIL, s, :], d.x[(NT - 1) * P:N, :]).then_inc(loaded[s], 16)
                else:
                    sp.dma_start(x_tile[:, s, :], d.x[bass.ds(t * P, P), :]).then_inc(loaded[s], 16)
            tiles(sp, body)
            sp.wait_ge(joined, NT + 2)
            sp.dma_start(d.x2[0:N - TAIL, :].rearrange("(t p) c -> p t c", p=P), m.tok[:, 0:NT - 1, :]).then_inc(stored, 16)
            sp.dma_start(d.x2[N - TAIL:N, :], m.tok[0:TAIL, NT - 1, :]).then_inc(stored, 16)
            sp.wait_ge(stored, 32)

        @block.scalar
        def _(act):
            act.sem_inc(product, 2)

            def body(t, s):
                act.wait_ge(product, t + 1)
                at = bass.ds(t * P, P)
                nc.scalar.activation(xT_tile[:, s, :, :], m.xT[:, :, at], ACT.Copy)
                nc.scalar.activation(gT_tile[:, s, :, :], m.agg[:, :, at], ACT.Copy).then_inc(staged, 1)
            tiles(act, body)
            act.wait_ge(var_ready, 1)
            nc.scalar.activation(tmp[:, :, 3], tmp[:, :, 2], ACT.Sqrt).then_inc(rooted, 1)

        @block.tensor
        def _(pe):
            def body(t, s):
                pe.wait_ge(staged, t + 1)
                pe.wait_ge(joined, t + 1)
                nc.tensor.matmul(acc[:, s, 0:C], m.ones[0:1, :], m.b_out[0:1, :], start=True, stop=False)
                for c in range(CB):
                    nc.tensor.matmul(acc[:, s, c * P:(c + 1) * P], gT_tile[:, s, c, :], m.ident[:, :], start=False, stop=False,
                                     skip_group_check=True)
                for c in range(CB):
                    last = nc.tensor.matmul(acc[:, s, 0:C], xT_tile[:, s, c, :], m.w_mix[:, c, :], start=False, stop=c == CB - 1)
                last.then_inc(product, 1)
            tiles(pe, body)

        @block.vector
        def _(dve):
            dve.sem_inc(joined, 2)
            step = Steps(dve, steps)
            step(nc.vector.memset(x_tile[:, :, :], 0.0))
            dve.sem_inc(cleared, 1)

            def body(t, s):
                dve.wait_ge(product, t + 3)
                dve.wait_ge(loaded[s], 8 * (t - s) + 16)
                at = bass.ds(t, 1)
                nc.vector.tensor_tensor(m.tok[:, at, :].squeeze(1), acc[:, s, 0:C], x_tile[:, s, :], ALU.add).then_inc(joined, 1)
                dve.wait_ge(joined, t + 3)
                nc.vector.bn_stats(stats[:, at, :].squeeze(1), m.tok[:, at, :].squeeze(1)).then_inc(counted, 1)
            tiles(dve, body)
            dve.wait_ge(counted, NT)
            merge_stats(nc, step, stats, tmp, m.mean[:, :])
            step(nc.vector.tensor_scalar(tmp[:, :, 2], tmp[:, :, 2], EPS, None, ALU.add))
            dve.sem_inc(var_ready, 1)
            dve.wait_ge(rooted, 1)
            step(nc.vector.reciprocal(m.rstd[:, :], tmp[:, :, 3]))


def router_stage(nc, d, m):
    with ExitStack() as ctx:
        sb, ps, sem = make_tools(nc, ctx)
        turned_tile = sb("rt_turned", [P, 2, CB, P])
        stats = sb("rt_stats", [P, NT, BNS])
        tmp = sb("rt_tmp", [P, NT, 4])
        big = {n: sb("rt_" + n, [P, NT, NX]) for n in "p eq where oh1 oh2 place a".split()}
        one = {n: sb("rt_" + n, [P, NT]) for n in "max1 max2 id1 id2 sum".split()}
        valid, node = sb("rt_valid", [P, NT]), sb("rt_node", [P, NT], I32)
        expert, expert_i = sb("rt_expert", [P, NX]), sb("rt_expert_i", [P, NX], I32)
        picked = sb("rt_picked", [P, NT * NX], BF16)
        earlier, all_ones = sb("rt_earlier", [P, P], BF16), sb("rt_all_ones", [P, P], BF16)
        zeros = sb("rt_zeros", [P, NT])
        tile_i, tile = sb("rt_tile_i", [1, MAX_TILES + 2], I32), sb("rt_tile", [1, MAX_TILES + 2])
        begun, last_expert = sb("rt_begun", [1, MAX_TILES + 2, NX]), sb("rt_last_expert", [1, MAX_TILES + 2])
        tiles_f, tiles_i = sb("rt_tiles_f", [P, 2, NX]), sb("rt_tiles_i", [P, NX], I32)
        turned = ps("rt_turned_psum", [P, 2, NODE_CHUNK])
        logits = ps("rt_logits", [P, NODE_CHUNK])
        counts = ps("rt_counts", [P, 2, NODE_CHUNK])
        normed, turned_ready, turned_used, logit_ready, counted, steps, var_ready, rooted, pool_steps, shifted, exped, pick_ready, count_ready = (
            sem("rt_" + x) for x in ("normed turned_ready turned_used logit_ready counted steps var_ready rooted pool_steps "
                                     "shifted exped pick_ready count_ready").split())
        block = ctx.enter_context(nc.Block())

        @block.gpsimd
        def _(pool):
            step = Steps(pool, pool_steps)
            step(pool.iota(node[:, :], [[P, NT]], base=0, channel_multiplier=1))
            step(pool.tensor_copy(valid[:, :], node[:, :]))
            step(pool.tensor_scalar(valid[:, :], valid[:, :], float(N), None, ALU.is_lt))
            step(pool.iota(expert_i[:, :], [[1, NX]], base=0, channel_multiplier=0))
            step(pool.tensor_copy(expert[:, :], expert_i[:, :]))
            step(pool.memset(all_ones[:, :], 1.0))
            step(pool.affine_select(out=earlier[:, :], in_=all_ones[:, :], compare_op=ALU.is_gt, fill=0.0,
                                    base=0, pattern=[[1, P]], channel_multiplier=-1))
            step(pool.iota(tile_i[:, :], [[1, MAX_TILES + 2]], base=0, channel_multiplier=0))
            step(pool.tensor_copy(tile[:, :], tile_i[:, :]))

        @block.tensor
        def _(pe):
            def body(t, s):
                pe.wait_ge(normed, t + 1)
                pe.wait_ge(turned_used, t + 1)
                for c in range(CB):
                    last = nc.tensor.transpose(turned[:, s, c * P:(c + 1) * P], m.tok_tile[:, s, c * P:(c + 1) * P], m.ident[:, :])
                last.then_inc(turned_ready, 1)
                pe.wait_ge(turned_used, t + 3)
                out = logits[:, bass.ds(t * NX, NX)]
                nc.tensor.matmul(out, m.ones[0:1, :], m.br[0:1, :], start=True, stop=False)
                for c in range(CB):
                    last = nc.tensor.matmul(out, turned_tile[:, s, c, :], m.wr[:, c, :], start=False, stop=c == CB - 1)
                last.then_inc(logit_ready, 1)
            tiles(pe, body)
            pe.wait_ge(pick_ready, 1)
            pe.wait_ge(pool_steps, 7)
            nc.tensor.matmul(counts[:, 0, 0:NT * NX], earlier[:, :], picked[:, :], start=True, stop=True)
            nc.tensor.matmul(counts[:, 1, 0:NT * NX], all_ones[:, :], picked[:, :], start=True, stop=True).then_inc(count_ready, 1)

        @block.scalar
        def _(act):
            act.sem_inc(turned_used, 2)

            def body(t, s):
                act.wait_ge(turned_ready, t + 3)
                nc.scalar.activation(turned_tile[:, s, :, :], turned[:, s, 0:C].rearrange("p (c n) -> p c n", c=CB),
                                     ACT.Copy).then_inc(turned_used, 1)
            tiles(act, body)
            act.wait_ge(var_ready, 1)
            nc.scalar.activation(tmp[:, :, 3], tmp[:, :, 2], ACT.Sqrt).then_inc(rooted, 1)
            act.wait_ge(shifted, 1)
            nc.scalar.activation(big["p"][:, :, :], big["p"][:, :, :], ACT.Exp).then_inc(exped, 1)

        @block.vector
        def _(dve):
            dve.sem_inc(turned_ready, 2)
            step = Steps(dve, steps)

            def body(t, s):
                dve.wait_ge(turned_ready, t + 1)
                at = bass.ds(t, 1)
                nc.vector.tensor_scalar(m.tok_tile[:, s, :], m.tok[:, at, :].squeeze(1), m.mean[:, at], m.rstd[:, at],
                                        ALU.subtract, ALU.mult).then_inc(normed, 1)
                dve.wait_ge(normed, t + 1)
                nc.vector.bn_stats(stats[:, at, :].squeeze(1), m.tok_tile[:, s, :])
                nc.vector.tensor_copy(m.tok[:, at, :].squeeze(1), m.tok_tile[:, s, :]).then_inc(counted, 1)
            tiles(dve, body)
            dve.wait_ge(counted, NT)
            merge_stats(nc, step, stats, tmp, m.mean[:, :])
            step(nc.vector.tensor_scalar(tmp[:, :, 2], tmp[:, :, 2], EPS, None, ALU.add))
            dve.sem_inc(var_ready, 1)
            dve.wait_ge(rooted, 1)
            step(nc.vector.reciprocal(m.rstd[:, :], tmp[:, :, 3]))

            def bc(x):
                return x.unsqueeze(2).to_broadcast([P, NT, NX])
            tt, ts = nc.vector.tensor_tensor, nc.vector.tensor_scalar
            p, eq, where, oh1, oh2, place, a = (big[n][:, :, :] for n in "p eq where oh1 oh2 place a".split())
            max1, max2, id1, id2, total = (one[n][:, :] for n in "max1 max2 id1 id2 sum".split())
            dve.wait_ge(logit_ready, NT)
            lg = logits[:, 0:NT * NX].rearrange("p (t e) -> p t e", e=NX)
            step(nc.vector.tensor_reduce(max1, lg, AX, ALU.max))
            step(tt(p, lg, bc(max1), ALU.subtract))
            dve.sem_inc(shifted, 1)
            dve.wait_ge(exped, 1)
            step(nc.vector.tensor_reduce(total, p, AX, ALU.add))
            step(nc.vector.reciprocal(total, total))
            step(tt(p, p, bc(total), ALU.mult))
            dve.wait_ge(pool_steps, 9)
            e_bc = expert[:, :].unsqueeze(1).to_broadcast([P, NT, NX])
            for oh, mx, ident in ((oh1, max1, id1), (oh2, max2, id2)):
                step(nc.vector.tensor_reduce(mx, p, AX, ALU.max))
                step(tt(eq, p, bc(mx), ALU.is_equal))
                step(nc.vector.scalar_tensor_tensor(where, eq, -float(NX), e_bc, ALU.mult, ALU.add))
                step(nc.vector.tensor_reduce(ident, where, AX, ALU.min))
                step(tt(oh, where, bc(ident), ALU.is_equal))
                step(nc.vector.scalar_tensor_tensor(p, oh, -2.0, p, ALU.mult, ALU.add))
            step(tt(total, max1, max2, ALU.add))
            step(nc.vector.reciprocal(total, total))
            step(tt(m.weight[:, 0, :], max1, total, ALU.mult))
            step(tt(m.weight[:, 1, :], max2, total, ALU.mult))
            step(tt(a, oh1, oh2, ALU.add))
            step(tt(picked[:, :].rearrange("p (t e) -> p t e", e=NX), a, bc(valid[:, :]), ALU.mult))
            dve.sem_inc(pick_ready, 1)
            step(nc.vector.memset(zeros[:, :], 0.0))
            dve.wait_ge(count_ready, 1)
            step(nc.vector.tensor_copy(a, counts[:, 1, 0:NT * NX].rearrange("p (t e) -> p t e", e=NX)))
            for e in range(NX):
                step(nc.vector.tensor_tensor_scan(where[:, :, e], a[:, :, e], zeros[:, :], 0.0, ALU.add, ALU.add))
            step(tt(place, where, a, ALU.subtract))
            step(tt(place, place, counts[:, 0, 0:NT * NX].rearrange("p (t e) -> p t e", e=NX), ALU.add))
            total_e = where[:, NT - 1, :]
            step(ts(tiles_f[:, 0, :], total_e, float(TOK - 1), None, ALU.add))
            step(nc.vector.tensor_copy(tiles_i[:, :], tiles_f[:, 0, :]))
            step(ts(tiles_i[:, :], tiles_i[:, :], TOK.bit_length() - 1, None, ALU.logical_shift_right))
            step(nc.vector.tensor_copy(tiles_f[:, 0, :], tiles_i[:, :]))
            step(ts(tiles_f[:, 0, :], tiles_f[:, 0, :], 1.0, None, ALU.max))
            step(nc.vector.tensor_tensor_scan(tiles_f[:, 1, :], tiles_f[:, 0, :], zeros[:, 0:NX], 0.0, ALU.add, ALU.add))
            step(tt(tiles_f[:, 1, :], tiles_f[:, 1, :], tiles_f[:, 0, :], ALU.subtract))
            step(nc.vector.tensor_copy(m.expert_i[:, :, :], tiles_f[0:1, :, :]))
            step(tt(m.tile_total[:, :], tiles_f[0:1, 0, NX - 1:NX], tiles_f[0:1, 1, NX - 1:NX], ALU.add))
            shape = [1, MAX_TILES + 2, NX]
            step(tt(begun[:, :, :], tile[:, :].unsqueeze(2).to_broadcast(shape), tiles_f[0:1, 1, :].unsqueeze(1).to_broadcast(shape), ALU.is_ge))
            step(nc.vector.tensor_reduce(last_expert[:, :], begun[:, :, :], AX, ALU.add))
            step(ts(m.tile_expert[:, :], last_expert[:, :], -1.0, None, ALU.add))
            step(ts(expert[:, :], tiles_f[:, 1, :], float(TOK), None, ALU.mult))
            step(tt(place, place, e_bc, ALU.add))
            for i, oh in enumerate((oh1, oh2)):
                step(tt(eq, oh, place, ALU.mult))
                step(nc.vector.tensor_reduce(max1, eq, AX, ALU.add))
                step(nc.vector.tensor_copy(m.row[:, i, :], max1))


def scatter_stage(nc, d, m):
    with ExitStack() as ctx:
        sb, ps, sem = make_tools(nc, ctx)
        idx = sb("sc_idx", [P, 2, 2], U32)
        ready, idx_ready = sem("sc_ready"), sem("sc_idx_ready")
        sent = [sem("sc_sent0"), sem("sc_sent1")]
        block = ctx.enter_context(nc.Block())

        @block.vector
        def _(dve):
            def body(t, s):
                if not is_first(t):
                    dve.wait_ge(sent[s], 16 * (t - s))
                    dve.nop(nofuse=True)
                at = bass.ds(t, 1)
                nc.vector.tensor_copy(idx[:, s, :].unsqueeze(2), m.row[:, :, at]).then_inc(idx_ready, 1)
                nc.vector.tensor_scalar(m.tok_tile[:, s, :], m.tok[:, at, :].squeeze(1), m.mean[:, at], m.rstd[:, at],
                                        ALU.subtract, ALU.mult).then_inc(ready, 1)
            tiles(dve, body, peel=True)

        @block.gpsimd
        def _(pool):
            def body(t, s):
                pool.wait_ge(idx_ready, t + 1)
                pool.wait_ge(ready, t + 1)
                pool.nop(nofuse=True)
                n = TAIL if is_last(t) else P
                for i in range(2):
                    pool.indirect_dma_start(d.routed[:, :], bass.IndirectOffsetOnAxis(ap=idx[0:n, s, i:i + 1], axis=0),
                                            m.tok_tile[0:n, s, :], None).then_inc(sent[s], 16)
            tiles(pool, body)

        @block.sync
        def _(sp):
            for s in range(2):
                sp.wait_ge(sent[s], 32 * ((NT + 1 - s) // 2))


def expert_weights(sb):
    x = Named()
    x.w1, x.w2 = ([[sb(f"ex_{name}_{part}{s}", [P, k, n], F32R)[:, :, :] for part in ("high", "low")] for s in range(2)]
                  for name, k, n in (("w1", CB, HID), ("w2", HB, C)))
    x.raw1, x.raw2 = sb("ex_raw1", [P, CB, HID])[:, :, :], sb("ex_raw2", [P, HB, C])[:, :, :]
    x.b2 = sb("ex_b2", [P, NX, C])[:, :, :]
    return x


def split_weights(pool, d, m, e, s, before=None):
    x = m.experts
    pool.dma_start(x.raw1, d.W1[bass.ds(e, 1), :, :].squeeze(0).rearrange("(c p) h -> p c h", p=P)).then_inc(m.raw_loaded, 16)
    pool.dma_start(x.raw2, d.W2[bass.ds(e, 1), :, :].squeeze(0).rearrange("(k p) c -> p k c", p=P)).then_inc(m.raw_loaded, 16)
    if before is not None:
        pool.wait_ge(m.y_ready, before)
    pool.wait_ge(m.raw_loaded, e * 32 + 32)
    pool.nop(nofuse=True)
    pool.tensor_copy(x.w1[s][0], x.raw1).then_inc(m.w_high, 1)
    pool.tensor_copy(x.w2[s][0], x.raw2).then_inc(m.w_high, 1)
    pool.wait_ge(m.w_high, e * 2 + 2)
    pool.nop(nofuse=True)
    pool.tensor_tensor(x.w1[s][1], x.raw1, x.w1[s][0].bitcast(F32), ALU.subtract).then_inc(m.w_ready[s], 1)
    pool.tensor_tensor(x.w2[s][1], x.raw2, x.w2[s][0].bitcast(F32), ALU.subtract).then_inc(m.w_ready[s], 1)
    pool.wait_ge(m.w_ready[s], e - s + 2)
    pool.nop(nofuse=True)


def expert_stage(nc, d, m):
    with ExitStack() as ctx:
        sb, ps, sem = make_tools(nc, ctx)
        x = sb("ex_x", [P, TOK // P, C])
        x_full, hidden_full = sb("ex_x_full", [P, CB, TOK]), sb("ex_hidden_full", [P, HB, TOK])
        xT = [sb("ex_xT_" + part, [P, CB, TOK], F32R) for part in ("high", "low")]
        hT = [sb("ex_hT_" + part, [P, HB, TOK], F32R) for part in ("high", "low")]
        y = sb("ex_y", [P, TOK // P, C])
        turned = ps("ex_turned", [P, CB, TOK])
        hidden = ps("ex_hidden", [P, HB, TOK])
        out = ps("ex_out", [P, TOK // P, C])
        x_loaded, turned_ready, x_gained, x_high, x_ready, h_ready, h_out, h_high, h_split, y_out, y_stored, y_free = (
            sem("ex_" + n) for n in ("x_loaded turned_ready x_gained x_high x_ready h_ready h_out h_high h_split y_out "
                                     "y_stored y_free").split())
        b2_loaded = sem("ex_b2_loaded")
        block = ctx.enter_context(nc.Block())
        PARTS = ((0, 0), (0, 1), (1, 0))
        BANKS = HB // HPB

        def all_tiles(eng):
            return eng.value_load(m.tile_total[0:1, 0:1], min_val=NX, max_val=MAX_TILES)

        def expert_of(eng, tile):
            return eng.value_load(m.tile_expert[0:1, bass.ds(tile, 1)], min_val=0, max_val=NX - 1)

        @block.gpsimd
        def _(pool):
            for e in range(2):
                split_weights(pool, d, m, e, e)
            with pool.Fori(1, NX // 2) as i:
                for s in range(2):
                    before = pool.value_load(m.expert_i[0:1, 1:2, bass.ds(i * 2 + (s - 1), 1)].squeeze(1), min_val=1, max_val=MAX_TILES)
                    split_weights(pool, d, m, i * 2 + s, s, before)

        @block.sync
        def _(sp):
            def row(tile):
                return nc.s_assert_within(tile * TOK, 0, ROWS - TOK,
                                          skip_runtime_bounds_check_because="the experts' tiles are at most MAX_TILES")

            def load(g):
                sp.dma_start(x[:, :, :], d.routed[bass.ds(row(g), TOK), :].rearrange("(a p) c -> p a c", p=P)).then_inc(x_loaded, 16)
            sp.sem_inc(y_free, 1)
            load(0)
            sp.dma_start(m.experts.b2, d.b2.unsqueeze(0).to_broadcast([P, NX, C])).then_inc(b2_loaded, 16)
            sp.wait_ge(turned_ready, 1)
            load(1)
            with sp.Fori(0, all_tiles(sp)) as g:
                sp.wait_ge(turned_ready, g + 2)
                load(g + 2)
                sp.wait_ge(y_out, g + 2)
                sp.dma_start(d.expert_out[bass.ds(row(g), TOK), :].rearrange("(a p) c -> p a c", p=P), y[:, :, :])\
                    .then_inc(y_stored, 16)
                sp.wait_ge(y_stored, g * 16 + 16)
                sp.sem_inc(y_free, 1)
            sp.wait_ge(x_loaded, all_tiles(sp) * 16 + 32)
            sp.nop(nofuse=True)

        @block.tensor
        def _(pe):
            def turn(g):
                pe.wait_ge(x_loaded, g * 16 + 16)
                for c in range(CB):
                    for a in range(TOK // P):
                        last = nc.tensor.transpose(turned[:, c, a * P:(a + 1) * P], x[:, a, c * P:(c + 1) * P], m.ident[:, :])
                last.then_inc(turned_ready, 1)
            turn(0)
            with pe.Fori(0, NX // 2) as i:
                for s in range(2):
                    at = bass.ds(i * 2 + s, 1)
                    n = pe.value_load(m.expert_i[0:1, 0:1, at].squeeze(1), min_val=1, max_val=-(-N // TOK))
                    before = pe.value_load(m.expert_i[0:1, 1:2, at].squeeze(1), min_val=0, max_val=MAX_TILES)
                    w1, w2 = m.experts.w1[s], m.experts.w2[s]
                    pe.wait_ge(m.w_ready[s], i * 2 + 2)
                    pe.nop(nofuse=True)
                    with pe.Fori(0, n) as j:
                        pe.wait_ge(x_ready, before + j + 1)
                        for h in range(HB):
                            for c in range(CB):
                                for k, (still, moving) in enumerate(PARTS):
                                    last = nc.tensor.matmul(hidden[:, h, :], w1[still][:, c, h * P:(h + 1) * P], xT[moving][:, c, :],
                                                            start=c == 0 and k == 0, stop=c == CB - 1 and k == len(PARTS) - 1)
                            if h % HPB == HPB - 1:
                                last.then_inc(h_ready, 1)
                        turn(before + j + 1)
                        pe.wait_ge(y_out, before + j + 1)
                        for a in range(TOK // P):
                            for h in range(HB):
                                if a == 0 and h % HPB == 0:
                                    pe.wait_ge(h_split, (before + j) * BANKS + (h // HPB + 1))
                                for k, (still, moving) in enumerate(PARTS):
                                    last = nc.tensor.matmul(out[:, a, :], hT[still][:, h, a * P:(a + 1) * P], w2[moving][:, h, :],
                                                            start=h == 0 and k == 0, stop=h == HB - 1 and k == len(PARTS) - 1)
                        last.then_inc(m.y_ready, 1)

        @block.scalar
        def _(act):
            with act.Fori(0, all_tiles(act)) as g:
                e = expert_of(act, g)
                for h in range(HB):
                    if h % HPB == 0:
                        act.wait_ge(h_ready, g * BANKS + (h // HPB + 1))
                    last = nc.scalar.activation(hidden_full[:, h, :], hidden[:, h, :], ACT.Gelu,
                                                bias=m.b1[:, h:h + 1, bass.ds(e, 1)].squeeze(1))
                    if h % HPB == HPB - 1:
                        last.then_inc(h_out, 1)

        @block.vector
        def _(dve):
            def gain(g):
                e = expert_of(dve, g)
                dve.wait_ge(turned_ready, g + 1)
                for c in range(CB):
                    last = nc.vector.tensor_scalar(x_full[:, c, :], turned[:, c, :], m.ln_g[:, c:c + 1, bass.ds(e, 1)].squeeze(1),
                                                   m.ln_b[:, c:c + 1, bass.ds(e, 1)].squeeze(1), ALU.mult, ALU.add)
                last.then_inc(x_gained, 1)
                dve.wait_ge(x_gained, g + 1)
                nc.vector.tensor_copy(xT[0][:, :, :], x_full[:, :, :]).then_inc(x_high, 1)
                dve.wait_ge(x_high, g + 1)
                nc.vector.tensor_tensor(xT[1][:, :, :], x_full[:, :, :], xT[0][:, :, :].bitcast(F32), ALU.subtract).then_inc(x_ready, 1)
            dve.sem_inc(y_out, 1)
            gain(0)
            dve.wait_ge(b2_loaded, 16)
            dve.nop(nofuse=True)
            with dve.Fori(0, all_tiles(dve)) as g:
                for b in range(BANKS):
                    at = slice(b * HPB, (b + 1) * HPB)
                    dve.wait_ge(h_out, g * BANKS + (b + 1))
                    nc.vector.tensor_copy(hT[0][:, at, :], hidden_full[:, at, :]).then_inc(h_high, 1)
                    dve.wait_ge(h_high, g * BANKS + (b + 1))
                    nc.vector.tensor_tensor(hT[1][:, at, :], hidden_full[:, at, :], hT[0][:, at, :].bitcast(F32), ALU.subtract)\
                        .then_inc(h_split, 1)
                gain(g + 1)
                e = expert_of(dve, g)
                dve.wait_ge(m.y_ready, g + 1)
                dve.wait_ge(y_free, g + 1)
                nc.vector.tensor_tensor(y[:, :, :], out[:, :, :], m.experts.b2[:, bass.ds(e, 1), :].to_broadcast([P, TOK // P, C]),
                                        ALU.add).then_inc(y_out, 1)


def combine_stage(nc, d, m):
    with ExitStack() as ctx:
        sb, ps, sem = make_tools(nc, ctx)
        slots = 4
        idx = sb("cb_idx", [P, slots, 2], U32)
        rows = sb("cb_rows", [P, slots, 2, C])
        x2 = sb("cb_x2", [P, slots, C])
        res = sb("cb_res", [P, slots, C])
        idx_ready, half, done = sem("cb_idx_ready"), sem("cb_half"), sem("cb_done")
        got, x2_loaded, stored = ([sem(f"cb_{name}{s}") for s in range(slots)] for name in ("got", "x2_loaded", "stored"))
        block = ctx.enter_context(nc.Block())

        @block.scalar
        def _(act):
            act.sem_inc(done, slots)

            def body(t, s):
                act.wait_ge(done, t + 1)
                nc.scalar.activation(idx[:, s, :].unsqueeze(2), m.row[:, :, bass.ds(t, 1)], ACT.Copy).then_inc(idx_ready, 1)
            tiles(act, body, slots)

        @block.gpsimd
        def _(pool):
            def body(t, s):
                pool.wait_ge(idx_ready, t + 1)
                pool.nop(nofuse=True)
                n = TAIL if is_last(t) else P
                for i in range(2):
                    pool.indirect_dma_start(rows[0:n, s, i, :], None, d.expert_out[:, :],
                                            bass.IndirectOffsetOnAxis(ap=idx[0:n, s, i:i + 1], axis=0)).then_inc(got[s], 16)
            tiles(pool, body, slots)

        @block.vector
        def _(dve):
            def body(t, s):
                n = TAIL if is_last(t) else P
                dve.wait_ge(got[s], (t - s) * (32 // slots) + 32)
                dve.wait_ge(x2_loaded[s], (t - s) * (16 // slots) + 16)
                if not is_first(t, slots):
                    dve.wait_ge(stored[s], (t - s) * (16 // slots))
                at = bass.ds(t, 1)
                nc.vector.scalar_tensor_tensor(res[0:n, s, :], rows[0:n, s, 0, :], m.weight[0:n, 0, at], x2[0:n, s, :],
                                               ALU.mult, ALU.add).then_inc(half, 1)
                dve.wait_ge(half, t + 1)
                nc.vector.scalar_tensor_tensor(res[0:n, s, :], rows[0:n, s, 1, :], m.weight[0:n, 1, at], res[0:n, s, :],
                                               ALU.mult, ALU.add).then_inc(done, 1)
            tiles(dve, body, slots, peel=True)

        @block.sync
        def _(sp):
            def store(t, s):
                if is_last(t):
                    sp.dma_start(d.out[(NT - 1) * P:N, :], res[0:TAIL, s, :]).then_inc(stored[s], 16)
                else:
                    sp.dma_start(d.out[bass.ds(t * P, P), :], res[:, s, :]).then_inc(stored[s], 16)

            def body(t, s):
                sp.wait_ge(done, t + 1)
                if not is_first(t, slots):
                    store(t - slots, s)
                if is_last(t):
                    sp.dma_start(x2[0:TAIL, s, :], d.x2[(NT - 1) * P:N, :]).then_inc(x2_loaded[s], 16)
                else:
                    sp.dma_start(x2[:, s, :], d.x2[bass.ds(t * P, P), :]).then_inc(x2_loaded[s], 16)
            tiles(sp, body, slots, peel=True)
            for t in range(NT - slots, NT):
                sp.wait_ge(done, slots + t + 1)
                store(t, t % slots)
            for s in range(slots):
                sp.wait_ge(stored[s], 16 * visits(slots, s))


def build(nc, d):
    with ExitStack() as ctx:
        sb, ps, sem = make_tools(nc, ctx)
        m = Named()
        m.ident = sb("ident", [P, P])
        m.iota_i, m.iota = sb("iota_i", [P, W], I32), sb("iota", [P, W])
        m.offsets_i, m.offsets = sb("offsets_i", [P, N // W + 2], I32), sb("offsets", [P, N // W + 2])
        m.ones = sb("ones", [1, P])
        m.mean, m.rstd = sb("mean", [P, NT]), sb("rstd", [P, NT])
        m.weight = sb("weight", [P, 2, NT])
        m.row = sb("row", [P, 2, NT], U32)
        m.expert_i = sb("expert_i", [1, 2, NX], I32)
        m.tile_total, m.tile_expert = sb("tile_total", [1, 1], I32), sb("tile_expert", [1, MAX_TILES + 2], I32)
        m.raw_loaded, m.w_high, m.y_ready = sem("ex_raw_loaded"), sem("ex_w_high"), sem("ex_y_ready")
        m.w_ready = [sem("ex_w_ready0"), sem("ex_w_ready1")]
        m.w_mix = sb("w_mix", [P, CB, C])
        m.wr, m.br = sb("wr", [P, CB, NX]), sb("br", [1, NX])
        m.ln_g, m.ln_b = sb("ln_g", [P, CB, NX]), sb("ln_b", [P, CB, NX])
        m.b1 = sb("b1", [P, HB, NX])
        m.b_out = sb("b_out", [1, C])
        loads = [(m.wr[:, :, :], d.Wr.rearrange("(c p) e -> p c e", p=P)), (m.br[:, :], d.br),
                 (m.ln_g[:, :, :], d.ln_g), (m.ln_b[:, :, :], d.ln_b), (m.b1[:, :, :], d.b1), (m.b_out[:, :], d.b_out)]
        with ExitStack() as early:
            esb, _, _ = make_tools(nc, early)
            m.xT = esb("xT", [P, CB, NP])
            m.agg = esb("agg", [P, CB, AGW])
            with ExitStack() as convs:
                csb, _, _ = make_tools(nc, convs)
                m.src = csb("src", [P, NCH], U32)
                m.dst, m.ew = csb("dst", [P, NCH]), csb("ew", [P, NCH])
                m.base, m.extra = csb("base", [1, NGP], I32), csb("extra", [1, NGP], I32)
                m.extra_sum_f, m.extra_sum = csb("extra_sum_f", [1, NGP + 1]), csb("extra_sum", [1, NGP + 1], I32)
                m.w_kv = csb("w_kv", [P, CB, 2 * INNER])
                m.w_q = csb("w_q", [P, INNER // P, C])
                m.w_out = csb("w_out", [P, INNER // P, C])
                m.dots = csb("dots", [P, INNER // P, P])
                m.w1 = [csb(f"w1_{i}", [P, CB, C]) for i in range(2)]
                m.b1c = [csb(f"b1_{i}", [1, C]) for i in range(2)]
                m.w2 = [csb(f"w2_{i}", [P, CB, C]) for i in range(2)]
                vecs = csb("vecs", [P, 2, 5, CB])
                m.b2 = [vecs[:, i, 0, :] for i in range(2)]
                m.gains = [[(vecs[:, i, 1 + 2 * n, :], vecs[:, i, 2 + 2 * n, :]) for n in range(2)] for i in range(2)]
                m.x = m.agg[:, :, :].rearrange("p b n -> p (b n)")[:, 0:NT * C].rearrange("p (t c) -> p t c", c=C)
                m.weight_loads = loads + [
                    (m.w_kv[:, :, :], d.w_qkv[:, INNER:3 * INNER].rearrange("(c p) n -> p c n", p=P)),
                    (m.w_q[:, :, :], d.w_qT.rearrange("(b p) c -> p b c", p=P)),
                    (m.w_out[:, :, :], d.w_out.rearrange("(b p) c -> p b c", p=P))]
                for i in range(2):
                    m.weight_loads += [(m.w1[i][:, :, :], d.cw1[i].rearrange("(c p) n -> p c n", p=P)), (m.b1c[i][:, :], d.cb1[i]),
                                       (m.w2[i][:, :, :], d.cw2[i].rearrange("(c p) n -> p c n", p=P))]
                    for n, v in enumerate(d.cvecs[i]):
                        m.weight_loads.append((vecs[:, i, n, :], v))
                load_stage(nc, d, m)
                norm_stage(nc, m)
                for layer in range(2):
                    hidden_stage(nc, d, m, layer, m.agg if layer else m.xT, m.w1[layer], m.b1c[layer][0:1, :])
                    gather_stage(nc, d, m, mix=layer == 0)
                    batch_norm_stage(nc, d, m, layer, layer == 1)
            with ExitStack() as tokens:
                tsb, _, _ = make_tools(nc, tokens)
                m.tok = tsb("tok", [P, NT, C])
                m.tok_tile = tsb("tok_tile", [P, 2, C])
                join_stage(nc, d, m)
                router_stage(nc, d, m)
                scatter_stage(nc, d, m)
        with ExitStack() as late:
            lsb, _, _ = make_tools(nc, late)
            m.experts = expert_weights(lsb)
            expert_stage(nc, d, m)
            combine_stage(nc, d, m)


def kernel(**inputs):
    from concourse import bacc
    from concourse.bass_utils import run_bass_kernel_spmd

    nc = bacc.Bacc("TRN2", target_bir_lowering=False, num_devices=1)
    g = "L0_gnn_"
    arrays = {}
    d = Named()

    def give(name, array):
        array = np.ascontiguousarray(array)
        arrays[name] = array
        return nc.dram_tensor(name, array.shape, mybir.dt.from_np(array.dtype), kind="ExternalInput").ap()

    def raw(name):
        return np.asarray(inputs[name])

    def edges(name, mode):
        return np.pad(raw(name), (0, NCH * P - E), mode=mode)

    def channels(array):
        return np.moveaxis(array.reshape(array.shape[:-1] + (array.shape[-1] // P, P)), -1, 0)

    d.x = give("x", raw("x"))
    dst = edges("dst", "edge")
    d.dst_rows = give("dst_rows", dst.reshape(NGP // 4, 4, GE))
    d.dst_cols = give("dst_cols", dst.reshape(NCH, P).T)
    d.src_cols = give("src_cols", edges("src", "edge").reshape(NCH, P).T.view(np.uint32))
    d.ew_cols = give("ew_cols", edges("edge_weight", "constant").reshape(NCH, P).T)
    d.cw1 = [give(f"c{i}_w1", raw(f"{g}c{i}_w1")) for i in (1, 2)]
    d.cb1 = [give(f"c{i}_b1", raw(f"{g}c{i}_b1")[None]) for i in (1, 2)]
    d.cw2 = [give(f"c{i}_w2", raw(f"{g}c{i}_w2")) for i in (1, 2)]
    d.cvecs = [[give(n, channels(raw(g + n))) for n in (f"c{i}_b2", f"c{i}_g", f"c{i}_b", f"bn{i}_g", f"bn{i}_b")] for i in (1, 2)]
    d.w_qkv = give("w_qkv", raw("L0_mix_w_qkv"))
    d.w_qT = give("w_qT", raw("L0_mix_w_qkv")[:, 0:INNER].T)
    d.w_out = give("w_out", raw("L0_mix_w_out"))
    d.b_out = give("b_out", raw("L0_mix_b_out")[None])
    d.Wr = give("Wr", raw("L0_ffn_Wr"))
    d.br = give("br", raw("L0_ffn_br")[None])
    d.ln_g = give("ln_g", np.moveaxis(channels(raw("L0_ffn_ln_g")), 1, 2))
    d.ln_b = give("ln_b", np.moveaxis(channels(raw("L0_ffn_ln_b")), 1, 2))
    d.W1 = give("W1", raw("L0_ffn_W1"))
    d.b1 = give("b1", np.moveaxis(channels(raw("L0_ffn_b1")), 1, 2))
    d.W2 = give("W2", raw("L0_ffn_W2"))
    d.b2 = give("b2", raw("L0_ffn_b2"))
    d.out = nc.dram_tensor("out", (N, C), F32, kind="ExternalOutput").ap()
    d.spans = nc.dram_tensor("spans", (2, NGP), I32, kind="Internal").ap()
    d.h = nc.dram_tensor("h", (NP, C), F32, kind="Internal").ap()
    d.x2 = nc.dram_tensor("x2", (N, C), F32, kind="Internal").ap()
    d.routed = nc.dram_tensor("routed", (ROWS, C), F32, kind="Internal").ap()
    d.expert_out = nc.dram_tensor("expert_out", (ROWS, C), F32, kind="Internal").ap()
    build(nc, d)
    r = run_bass_kernel_spmd(nc, [arrays], core_ids=[0])
    return r.results[0]["out"]
```

```python
import numpy as np
from contextlib import ExitStack

import concourse.bass as bass
from concourse import mybir

F32, F32R, BF16 = mybir.dt.float32, mybir.dt.float32r, mybir.dt.bfloat16
I32, U32 = mybir.dt.int32, mybir.dt.uint32
ALU = mybir.AluOpType
ACT = mybir.ActivationFunctionType
AX = mybir.AxisListType.X

P = 128
N, C = 6250, 256
CB = C // P
NT = -(-N // P)
NP = NT * P
TAIL = N - (NT - 1) * P
EPS = 1e-5

E = 206250
GC = 4
GE = GC * P
NG = -(-E // GE)
NGP = -(-NG // 4) * 4
NCH = NGP * GC
SLOTS = 4
W = 64
AGW = -(-(N + W) // P) * P

HEADS, DH = 8, 64
INNER = HEADS * DH
NX = 8
HID = 1024
HB = HID // P
TOK = 256
MAX_TILES = 2 * N // TOK + NX
CAP = N + TOK
ROWS = MAX_TILES * TOK
BT = 7
NBLK = NT // BT
assert NT % BT == 0
ZEROS = TOK * C // P
HPB = 512 // TOK
NODE_CHUNK = 512
NODE_CHUNKS = [(a, min(NODE_CHUNK, N - a)) for a in range(0, N, NODE_CHUNK)]
FULL_CHUNKS = N // NODE_CHUNK
BNS = 6


class Named:
    pass


def make_tools(nc, ctx, stage=""):
    def sb(name, shape, dt=F32):
        return ctx.enter_context(nc.sbuf_tensor(f"sb_{stage}{name}", shape, dt))

    def ps(name, shape, dt=F32):
        return ctx.enter_context(nc.psum_tensor(f"ps_{stage}{name}", shape, dt))

    def sem(name):
        return ctx.enter_context(nc.semaphore(f"{stage}{name}"))

    return sb, ps, sem


class Steps:

    def __init__(self, eng, sem, base=0):
        self.eng, self.sem, self.base, self.n = eng, sem, base, 0

    def __call__(self, instruction):
        self.go(instruction)
        self.eng.wait_ge(self.sem, self.base + self.n)

    def go(self, instruction):
        instruction.then_inc(self.sem, 1)
        self.n += 1


def tiles(eng, body, slots=2, peel=False, count=NT):
    if peel:
        for s in range(slots):
            body(s, s)
    with eng.Fori(1 if peel else 0, count // slots) as i:
        for s in range(slots):
            body(i * slots + s, s)
    for t in range(count // slots * slots, count):
        body(t, t % slots)


def visits(slots, s, count=NT):
    return (count - 1 - s) // slots + 1


def is_last(t):
    return isinstance(t, int) and t == NT - 1


def is_first(t, slots=2):
    return isinstance(t, int) and t < slots


def start_stage(nc, d, m):
    with ExitStack() as ctx:
        sb, ps, sem = make_tools(nc, ctx)
        dst_rows = sb("dst_rows", [NGP // 4, 4, GE], I32)
        span = sb("span", [NGP // 4, 2, 4], F32)
        span_i = sb("span_i", [NGP // 4, 2, 4], I32)
        base_bc = sb("base_bc", [P, NGP], I32)
        base_f = sb("base_f", [P, NGP])
        dst_cols = sb("dst_cols", [P, NCH], I32)
        lasts = sb("lasts", [1, NGP], I32)
        extra_f = sb("extra_f", [1, NGP])
        zeros = sb("zeros", [1, NGP])
        stats = sb("stats", [P, NT, BNS])
        tmp = sb("tmp", [P, NT, 4])
        head_mean = sb("head_mean", [P, CB * 2 * HEADS])
        ahead = 4
        xn = sb("xn", [P, ahead, C])
        a_tile = sb("a_tile", [P, 2, CB, P])
        h_tile = sb("h_tile", [P, ahead, C])
        turned = ps("turned", [P, 2, NODE_CHUNK])
        acc = ps("acc", [P, 2, NODE_CHUNK])
        x_loaded = [sem("x_loaded0"), sem("x_loaded1")]
        stored = [sem(f"stored{n}") for n in range(ahead)]
        dst_loaded, const_loaded, spans_moved = sem("dst_loaded"), sem("const_loaded"), sem("spans_moved")
        x_cleared, dve_done, stats_done, root_done = sem("x_cleared"), sem("dve_done"), sem("stats_done"), sem("root_done")
        pool_step = sem("pool_step")
        normed, turned_ready, turned_used, product, summed, h_ready = (
            sem(name) for name in "normed turned_ready turned_used product summed h_ready".split())
        block = ctx.enter_context(nc.Block())
        HALF = NT // BT // 2 * BT
        mark = Named()

        @block.vector
        def _(dve):
            nc.vector.memset(m.x[:, NT - 1, :], 0.0).then_inc(x_cleared, 1)
            step = Steps(dve, dve_done)
            dve.wait_ge(dst_loaded, 16)
            step(nc.vector.tensor_reduce(span[:, 0, :], dst_rows[:, :, :], AX, ALU.min))
            step(nc.vector.tensor_reduce(span[:, 1, :], dst_rows[:, :, :], AX, ALU.max))
            step(nc.vector.tensor_copy(span_i[:, :, :], span[:, :, :]))
            mark.spans = step.n
            for part, (a, b) in enumerate(((0, HALF), (HALF, NT))):
                dve.wait_ge(x_loaded[part], 32 if part else 16)
                with dve.Fori(a // BT, b // BT) as i:
                    for j in range(BT):
                        at = bass.ds(i * BT + j, 1)
                        nc.vector.bn_stats(stats[:, at, :].squeeze(1), m.x[:, at, :].squeeze(1)).then_inc(stats_done, 1)
            dve.wait_ge(stats_done, NT)
            merge_stats(nc, step, stats, tmp, m.mean[:, :])
            step(nc.vector.tensor_scalar(tmp[:, :, 2], tmp[:, :, 2], EPS, None, ALU.add))
            mark.variance = step.n
            step(nc.vector.memset(zeros[:, :], 0.0))
            dve.wait_ge(root_done, 1)
            step(nc.vector.reciprocal(m.rstd[:, :], tmp[:, :, 3]))
            dve.wait_ge(const_loaded, 16 * (3 + len(m.weight_loads)))

            def norm(t, s):
                nc.vector.tensor_scalar(xn[:, s, :], m.x[:, bass.ds(t, 1), :].squeeze(1), m.mean[:, bass.ds(t, 1)],
                                        m.rstd[:, bass.ds(t, 1)], ALU.subtract, ALU.mult).then_inc(normed, 1)

            def body(t, n):
                s = n % 2
                if not isinstance(t, int) or t < NT - ahead:
                    dve.wait_ge(turned_ready, t + 1)
                    norm(t + ahead, n)
                dve.wait_ge(product, t + 1)
                if not is_first(t, ahead):
                    dve.wait_ge(stored[n], (t - n) * (16 // ahead))
                nc.vector.tensor_tensor(h_tile[:, n, :], acc[:, s, 0:C], m.b1c[0][:, :], ALU.add).then_inc(summed, 1)
                dve.wait_ge(summed, t + 3)
                nc.vector.tensor_scalar(h_tile[:, n, :], h_tile[:, n, :], 0.0, None, ALU.max).then_inc(h_ready, 1)
            dve.sem_inc(summed, 2)
            for t in range(ahead):
                norm(t, t)
            dve.wait_ge(spans_moved, 64)
            step(nc.vector.tensor_copy(base_f[:, :], base_bc[:, :]))
            mark.bases = step.n
            heads = m.w_kv[:, :, :].rearrange("p c (h e) -> p (c h) e", e=DH)
            step(nc.vector.tensor_reduce(head_mean[:, :], heads, AX, ALU.add))
            step(nc.vector.tensor_scalar(head_mean[:, :], head_mean[:, :], 1.0 / DH, None, ALU.mult))
            mark.head_means = step.n
            tiles(dve, body, ahead, peel=True, count=NT - ahead)
            for t in range(NT - ahead, NT):
                body(t, t % ahead)
            step(nc.vector.tensor_tensor(lasts[:, :], lasts[:, :], m.base[:, :], ALU.subtract))
            step(nc.vector.tensor_scalar(m.extra[:, :], lasts[:, :], W.bit_length() - 1, None, ALU.logical_shift_right))
            step(nc.vector.tensor_copy(extra_f[:, :], m.extra[:, :]))
            step(nc.vector.tensor_tensor_scan(m.extra_sum_f[:, 1:NGP + 1], extra_f[:, :], zeros[:, :], 0.0, ALU.add, ALU.add))
            step(nc.vector.memset(m.extra_sum_f[:, 0:1], 0.0))
            step(nc.vector.tensor_copy(m.extra_sum[:, :], m.extra_sum_f[:, :]))

        @block.sync
        def _(sp):
            sp.dma_start(m.x[:, 0:HALF, :], d.x[0:HALF * P, :].rearrange("(t p) c -> p t c", p=P)).then_inc(x_loaded[0], 16)
            sp.dma_start(m.x[:, HALF:NT - 1, :], d.x[HALF * P:(NT - 1) * P, :].rearrange("(t p) c -> p t c", p=P))\
                .then_inc(x_loaded[1], 16)
            sp.wait_ge(x_cleared, 1)
            sp.dma_start(m.x[0:TAIL, NT - 1, :], d.x[(NT - 1) * P:N, :]).then_inc(x_loaded[1], 16)
            sp.wait_ge(dve_done, mark.spans)
            sp.dma_start(d.spans[:, :].rearrange("k (p g) -> p k g", g=4), span_i[:, :, :]).then_inc(spans_moved, 16)
            sp.wait_ge(spans_moved, 16)
            sp.dma_start(base_bc[:, :], d.spans[0:1, :].to_broadcast([P, NGP])).then_inc(spans_moved, 16)
            sp.dma_start(m.base[:, :], d.spans[0:1, :]).then_inc(spans_moved, 16)
            sp.dma_start(lasts[:, :], d.spans[1:2, :]).then_inc(spans_moved, 16)

            def body(t, n):
                sp.wait_ge(h_ready, t + 1)
                sp.dma_start(d.h[bass.ds(t * P, P), :], h_tile[:, n, :]).then_inc(stored[n], 16)
            tiles(sp, body, ahead)
            for n in range(ahead):
                sp.wait_ge(stored[n], 16 * visits(ahead, n))

        @block.scalar
        def _(act):
            act.dma_start(dst_rows[:, :, :], d.dst_rows).then_inc(dst_loaded, 16)
            act.dma_start(dst_cols[:, :], d.dst_cols).then_inc(const_loaded, 16)
            act.dma_start(m.src[:, :], d.src_cols).then_inc(const_loaded, 16)
            act.dma_start(m.ew[:, :], d.ew_cols).then_inc(const_loaded, 16)
            for to, frm in m.weight_loads:
                act.dma_start(to, frm).then_inc(const_loaded, 16)
            act.wait_ge(dve_done, mark.variance)
            act.activation(tmp[:, :, 3], tmp[:, :, 2], ACT.Sqrt).then_inc(root_done, 1)
            act.sem_inc(turned_used, 2)

            def body(t, s):
                act.wait_ge(turned_ready, t + 1)
                tile = turned[:, s, 0:C].rearrange("p (c n) -> p c n", c=CB)
                act.activation(a_tile[:, s, :, :], tile, ACT.Copy)
                act.activation(m.xT[:, :, bass.ds(t * P, P)], tile, ACT.Copy).then_inc(turned_used, 1)
            tiles(act, body)

        @block.gpsimd
        def _(pool):
            step = Steps(pool, pool_step)
            step(pool.memset(m.ident[:, :], 0.0))
            step(pool.affine_select(out=m.ident[:, :], in_=m.ident[:, :], compare_op=ALU.not_equal, fill=1.0,
                                    base=0, pattern=[[-1, P]], channel_multiplier=1))
            mark.ident = step.n
            step(pool.iota(m.iota_i[:, :], [[1, W]], base=0, channel_multiplier=0))
            step(pool.tensor_copy(m.iota[:, :], m.iota_i[:, :]))
            step(pool.iota(m.offsets_i[:, :], [[W, N // W + 2]], base=0, channel_multiplier=0))
            step(pool.tensor_copy(m.offsets[:, :], m.offsets_i[:, :]))
            step(pool.memset(m.ones[:, :], 1.0))
            pool.wait_ge(const_loaded, 16 * (3 + len(m.weight_loads)))
            step(pool.tensor_copy(m.dst[:, :], dst_cols[:, :]))
            pool.wait_ge(dve_done, mark.bases)
            by_group = m.dst[:, :].rearrange("p (g k) -> p g k", k=GC)
            step(pool.tensor_tensor(by_group, by_group, base_f[:, :].unsqueeze(2).to_broadcast([P, NGP, GC]), ALU.subtract))
            pool.wait_ge(dve_done, mark.head_means)
            heads = m.w_kv[:, :, :].rearrange("p c (h e) -> p (c h) e", e=DH)
            step(pool.tensor_tensor(heads, heads, head_mean[:, :].unsqueeze(2).to_broadcast([P, CB * 2 * HEADS, DH]), ALU.subtract))

        @block.tensor
        def _(pe):
            pe.wait_ge(pool_step, mark.ident)
            pe.wait_ge(const_loaded, 16 * (3 + len(m.weight_loads)))

            def turn(t, n):
                s = n % 2
                pe.wait_ge(normed, t + 1)
                pe.wait_ge(turned_used, t + 1)
                for c in range(CB):
                    last = nc.tensor.transpose(turned[:, s, c * P:(c + 1) * P], xn[:, n, c * P:(c + 1) * P], m.ident[:, :])
                last.then_inc(turned_ready, 1)

            def body(t, n):
                s = n % 2
                if not is_last(t):
                    turn(t + 1, (n + 1) % ahead)
                pe.wait_ge(turned_used, t + 3)
                pe.wait_ge(summed, t + 1)
                for c in range(CB):
                    last = nc.tensor.matmul(acc[:, s, 0:C], a_tile[:, s, c, :], m.w1[0][:, c, :], start=c == 0, stop=c == CB - 1)
                last.then_inc(product, 1)
            turn(0, 0)
            tiles(pe, body, ahead)


def merge_stats(nc, step, stats, tmp, mean):
    me, mo = stats[:, :, 1], stats[:, :, 4]
    step.go(nc.vector.tensor_tensor(mean, me, mo, ALU.add))
    step.go(nc.vector.tensor_tensor(tmp[:, :, 0], me, mo, ALU.subtract))
    step(nc.vector.tensor_tensor(tmp[:, :, 1], stats[:, :, 2], stats[:, :, 5], ALU.add))
    step.go(nc.vector.tensor_scalar(mean, mean, 0.5, None, ALU.mult))
    step.go(nc.vector.tensor_tensor(tmp[:, :, 0], tmp[:, :, 0], tmp[:, :, 0], ALU.mult))
    step(nc.vector.tensor_scalar(tmp[:, :, 1], tmp[:, :, 1], 1.0 / C, None, ALU.mult))
    step(nc.vector.scalar_tensor_tensor(tmp[:, :, 2], tmp[:, :, 0], 0.25, tmp[:, :, 1], ALU.mult, ALU.add))


def hidden_stage(nc, d, m, w, b):
    with ExitStack() as ctx:
        sb, ps, sem = make_tools(nc, ctx, "hidden_")
        a_tile = sb("a_tile", [P, 2, CB, P])
        slots = 4
        h_tile = sb("h_tile", [P, slots, C])
        acc = ps("acc", [P, 2, NODE_CHUNK])
        staged, product, summed, h_ready = sem("staged"), sem("product"), sem("summed"), sem("h_ready")
        stored = [sem(f"stored_{n}") for n in range(slots)]
        block = ctx.enter_context(nc.Block())

        @block.scalar
        def _(act):
            act.sem_inc(product, 2)

            def body(t, s):
                act.wait_ge(product, t + 1)
                for b in range(CB):
                    last = act.activation(a_tile[:, s, b, :], m.agg[:, b, bass.ds(t * P, P)], ACT.Relu, bias=m.bn_shift[:, b:b + 1],
                                          scale=m.bn_scale[:, b:b + 1])
                last.then_inc(staged, 1)
            tiles(act, body)

        @block.tensor
        def _(pe):
            def body(t, s):
                pe.wait_ge(staged, t + 1)
                pe.wait_ge(summed, t + 1)
                for c in range(CB):
                    last = nc.tensor.matmul(acc[:, s, 0:C], a_tile[:, s, c, :], w[:, c, :], start=c == 0, stop=c == CB - 1)
                last.then_inc(product, 1)
            tiles(pe, body)

        @block.vector
        def _(dve):
            dve.sem_inc(summed, 2)

            def body(t, n):
                dve.wait_ge(product, t + 3)
                if not is_first(t, slots):
                    dve.wait_ge(stored[n], (t - n) * (16 // slots))
                nc.vector.tensor_tensor(h_tile[:, n, :], acc[:, n % 2, 0:C], b[:, :], ALU.add).then_inc(summed, 1)
                dve.wait_ge(summed, t + 3)
                nc.vector.tensor_scalar(h_tile[:, n, :], h_tile[:, n, :], 0.0, None, ALU.max).then_inc(h_ready, 1)
            tiles(dve, body, slots, peel=True)

        @block.sync
        def _(sp):
            def body(t, n):
                sp.wait_ge(h_ready, t + 1)
                sp.dma_start(d.h[bass.ds(t * P, P), :], h_tile[:, n, :]).then_inc(stored[n], 16)
            tiles(sp, body, slots)
            for n in range(slots):
                sp.wait_ge(stored[n], 16 * visits(slots, n))


def gather_stage(nc, d, m, mix):
    with ExitStack() as ctx:
        sb, ps, sem = make_tools(nc, ctx, "gather_mix_" if mix else "gather_")
        rows = sb("rows", [P, SLOTS, GC, C])
        idx = sb("idx", [P, SLOTS, GC], U32)
        sel = sb("sel", [P, 2, GC, W])
        hit_x = sb("hit_x", [P, GC, W])
        sel_x = sb("sel_x", [P, GC, W])
        parts = [ps(f"part{i}", [P, NODE_CHUNK]) for i in range(3)]
        part = [x[:, 0:CB * W].rearrange("p (b w) -> p b w", b=CB) for x in parts]
        part_x = part[2]
        gathered = [sem(f"gathered{i}") for i in range(SLOTS)]
        idx_ready, sel_ready, summed, added = sem("idx_ready"), sem("sel_ready"), sem("summed"), sem("added")
        cleared = sem("cleared")
        x_hit, x_sel, x_summed, x_added = sem("x_hit"), sem("x_sel"), sem("x_summed"), sem("x_added")
        k = mixer_parts(sb, ps, sem) if mix else mixed_parts(sb, ps, sem)
        block = ctx.enter_context(nc.Block())

        first = PER_MIX * NT
        turns = (NG - first) // SLOTS
        rest = first + turns * SLOTS

        def groups(group, eng, hooks=()):
            def some(t, s):
                for j in range(PER_MIX):
                    group(t * PER_MIX + j, j % SLOTS)
                    if j in hooks:
                        hooks[j](t, s)
            tiles(eng, some)
            with eng.Fori(0, turns) as i:
                for j in range(SLOTS):
                    group(i * SLOTS + (first + j), j)
            for g in range(rest, NG):
                group(g, g % SLOTS)

        if not mix:
            @block.sync
            def _(sp):
                sp.wait_ge(cleared, 1)

                def blank(tile):
                    sp.dma_start(d.expert_out[bass.ds(tile * TOK, TOK), :].rearrange("(p a) c -> p (a c)", p=P), k.zeros[:, :])\
                        .then_inc(k.blanked, 16)

                def load(t, s):
                    n = TAIL if is_last(t) else P
                    sp.dma_start(k.x[0:n, s, :], d.x[bass.ds(t * P, n), :]).then_inc(k.x_loaded[s], 16)

                def store(t, s):
                    sp.wait_ge(k.summed, t + 3)
                    n = TAIL if is_last(t) else P
                    sp.dma_start(d.x_mixed[bass.ds(t * P, n), :], k.x[0:n, s, :]).then_inc(k.stored, 16)

                def turn(t, s):
                    store(t, s)
                    sp.wait_ge(k.stored, t * 16 + 16)
                    load(t + 2, s)
                    blank(t)
                load(0, 0)
                load(1, 1)
                tiles(sp, turn, count=NT - 2)
                for tile in range(NT - 2, MAX_TILES):
                    blank(tile)
                for t in (NT - 2, NT - 1):
                    store(t, t % 2)
                sp.wait_ge(k.stored, 16 * NT)
                sp.wait_ge(k.blanked, 16 * MAX_TILES)

        @block.gpsimd
        def _(pool):
            def group(g, s):
                pool.wait_ge(idx_ready, g + 1)
                pool.nop(nofuse=True)
                for c in range(GC):
                    pool.indirect_dma_start(rows[:, s, c, :], None, d.h[:, :],
                                            bass.IndirectOffsetOnAxis(ap=idx[:, s, c:c + 1], axis=0)).then_inc(gathered[s], 16)
            groups(group, pool)

        @block.scalar
        def _(act):
            act.sem_inc(added, SLOTS)
            act.sem_inc(x_added, 1)

            def group(g, s):
                act.wait_ge(added, g + 1)
                nc.scalar.activation(idx[:, s, :], m.src[:, bass.ds(g * GC, GC)], ACT.Copy).then_inc(idx_ready, 1)

            def stage_tile(t, s):
                act.wait_ge(k.dots_done if mix else k.product, t + 1)
                nc.scalar.activation(k.x_tile[:, s, :, :], m.xT[:, :, bass.ds(t * P, P)], ACT.Copy).then_inc(k.staged, 1)

            def square(t, s):
                act.wait_ge(k.kv_ready, t + 1)
                kv_psum = k.kv_psum[:, :, :].rearrange("p a n -> p (a n)")
                nc.scalar.activation(k.kv[:, s, :], kv_psum, ACT.Copy).then_inc(k.kv_out, 1)
                act.wait_ge(k.var_out, t + 1)
                act.wait_ge(k.kv_out, t + 2)
                nc.scalar.activation(k.squares[:, :], k.kv[:, s, :], ACT.Square).then_inc(k.squared, 1)

            def root(t, s):
                act.wait_ge(k.var_out, t + 2)
                nc.scalar.activation(k.root[:, s, :], k.var[:, s, :], ACT.Sqrt).then_inc(k.rooted, 1)
            if mix:
                act.sem_inc(k.dots_done, 2)
                act.sem_inc(k.kv_out, 1)
                act.sem_inc(k.var_out, 1)
            else:
                act.sem_inc(k.product, 2)
            groups(group, act, {0: stage_tile, 5: square, 7: root} if mix else {0: stage_tile})

        @block.tensor
        def _(pe):
            def group(g, s):
                extra = pe.value_load(m.extra[0:1, bass.ds(g, 1)], min_val=0, max_val=N // W)
                pe.wait_ge(gathered[s], (g - s) * (16 * GC // SLOTS) + 16 * GC)
                pe.wait_ge(sel_ready, g + 1)
                pe.wait_ge(added, g + SLOTS - 1)
                for b in range(CB):
                    for c in range(GC):
                        last = nc.tensor.matmul(part[s % 2][:, b, :], rows[:, s, c, b * P:(b + 1) * P], sel[:, s % 2, c, :],
                                                start=c == 0, stop=c == GC - 1)
                last.then_inc(summed, 1)
                with pe.If(extra > 0):
                    before = pe.value_load(m.extra_sum[0:1, bass.ds(g, 1)], min_val=0, max_val=NG * (N // W))
                    with pe.Fori(0, extra) as j:
                        pe.wait_ge(x_sel, before + j + 1)
                        pe.wait_ge(x_added, before + j + 1)
                        for b in range(CB):
                            for c in range(GC):
                                last = nc.tensor.matmul(part_x[:, b, :], rows[:, s, c, b * P:(b + 1) * P], sel_x[:, c, :],
                                                        start=c == 0, stop=c == GC - 1)
                        last.then_inc(x_summed, 1)
                    pe.nop(nofuse=True)
                with pe.Else():
                    pe.nop(nofuse=True)

            def keys_values(t, s):
                pe.wait_ge(k.staged, t + 1)
                pe.wait_ge(k.kv_out, t + 1)
                for half in range(2):
                    for c in range(CB):
                        last = nc.tensor.matmul(k.kv_psum[:, half, :], k.x_tile[:, s, c, :],
                                                m.w_kv[:, c, half * INNER:(half + 1) * INNER], start=c == 0, stop=c == CB - 1)
                last.then_inc(k.kv_ready, 1)

            def dots(t, s):
                pe.wait_ge(k.scaled, t + 1)
                ends = is_last(t)
                for b in range(INNER // P):
                    last = nc.tensor.matmul(k.dots[:, b * P:(b + 1) * P], k.kv[:, s, INNER + b * P:INNER + (b + 1) * P],
                                            k.kv[:, s, b * P:(b + 1) * P], start=False, stop=ends, skip_group_check=True)
                last.then_inc(k.dots_done, 1)
            if mix:
                pe.wait_ge(cleared, 1)
                nc.tensor.matmul(k.dots[:, :], m.ident[:, :], m.agg[:, 0, 0:INNER], start=True, stop=False, skip_group_check=True)\
                    .then_inc(k.zeroed, 1)

            def mixed(t, s):
                pe.wait_ge(k.staged, t + 1)
                pe.wait_ge(k.summed, t + 1)
                nc.tensor.matmul(k.acc[:, s, 0:C], m.ones[0:1, :], m.b_out[0:1, :], start=True, stop=False)
                for c in range(CB):
                    last = nc.tensor.matmul(k.acc[:, s, 0:C], k.x_tile[:, s, c, :], m.w_mix[:, c, :], start=False, stop=c == CB - 1)
                last.then_inc(k.product, 1)
            groups(group, pe, {0: keys_values, 7: dots} if mix else {0: mixed})

        @block.vector
        def _(dve):
            if not mix:
                dve.sem_inc(k.summed, 2)
                nc.vector.memset(k.zeros[:, :], 0.0)
            nc.vector.memset(m.agg[:, :, :], 0.0).then_inc(cleared, 1)
            dve.wait_ge(cleared, 1)
            if mix:
                dve.wait_ge(k.zeroed, 1)

            def select(g, s):
                for c in range(GC):
                    at = bass.ds(g * GC + c, 1)
                    last = nc.vector.tensor_scalar(sel[:, s % 2, c, :], m.iota[:, :], m.dst[:, at], m.ew[:, at],
                                                   ALU.is_equal, ALU.mult)
                last.then_inc(sel_ready, 1)

            def group(g, s):
                select(g + 1, (s + 1) % SLOTS)
                base = dve.value_load(m.base[0:1, bass.ds(g, 1)], min_val=0, max_val=N - 1)
                extra = dve.value_load(m.extra[0:1, bass.ds(g, 1)], min_val=0, max_val=N // W)
                with dve.If(extra > 0):
                    before = dve.value_load(m.extra_sum[0:1, bass.ds(g, 1)], min_val=0, max_val=NG * (N // W))
                    with dve.Fori(0, extra) as j:
                        for c in range(GC):
                            last = nc.vector.tensor_scalar(hit_x[:, c, :], m.iota[:, :], m.offsets[:, bass.ds(j + 1, 1)],
                                                           m.dst[:, bass.ds(g * GC + c, 1)], ALU.add, ALU.is_equal)
                        last.then_inc(x_hit, 1)
                        dve.wait_ge(x_hit, before + j + 1)
                        for c in range(GC):
                            last = nc.vector.tensor_scalar(sel_x[:, c, :], hit_x[:, c, :], m.ew[:, bass.ds(g * GC + c, 1)],
                                                           None, ALU.mult)
                        last.then_inc(x_sel, 1)
                        dve.wait_ge(x_summed, before + j + 1)
                        dve.wait_ge(added, g + SLOTS)
                        start = nc.s_assert_within(base + (j + 1) * W, 0, N - 1,
                                                   skip_runtime_bounds_check_because="the windows end with the last destination")
                        to = m.agg[:, :, bass.ds(start, W)]
                        nc.vector.tensor_tensor(to, part_x[:, :, :], to, ALU.add).then_inc(x_added, 1)
                    dve.wait_ge(x_added, before + extra + 1)
                    dve.nop(nofuse=True)
                with dve.Else():
                    dve.nop(nofuse=True)
                dve.wait_ge(summed, g + 1)
                dve.wait_ge(added, g + SLOTS)
                to = m.agg[:, :, bass.ds(base, W)]
                nc.vector.tensor_tensor(to, part[s % 2][:, :, :], to, ALU.add).then_inc(added, 1)

            def variance(t, s):
                dve.wait_ge(k.squared, t + 1)
                nc.vector.tensor_reduce(k.sums[:, :], k.squares[:, :].rearrange("p (h e) -> p h e", e=DH), AX, ALU.add).then_inc(k.steps, 1)
                dve.wait_ge(k.steps, t * 3 + 1)
                nc.vector.tensor_scalar(k.var[:, s, :], k.sums[:, :], 1.0 / DH, EPS, ALU.mult, ALU.add).then_inc(k.var_out, 1)

            def scale(t, s):
                dve.wait_ge(k.rooted, t + 1)
                nc.vector.tensor_tensor(k.both[:, :], k.root[:, s, 0:HEADS], k.root[:, s, HEADS:2 * HEADS], ALU.mult).then_inc(k.steps, 1)
                dve.wait_ge(k.steps, t * 3 + 2)
                nc.vector.reciprocal(k.rstd[:, :], k.both[:, :]).then_inc(k.steps, 1)
                dve.wait_ge(k.steps, t * 3 + 3)
                keys = k.kv[:, s, 0:INNER].rearrange("p (h e) -> p h e", e=DH)
                nc.vector.tensor_tensor(keys, keys, k.rstd[:, :].unsqueeze(2).to_broadcast([P, HEADS, DH]), ALU.mult).then_inc(k.scaled, 1)

            def add_x(t, s):
                dve.wait_ge(k.product, t + 3)
                dve.wait_ge(k.x_loaded[s], (t - s) * 8 + 16)
                nc.vector.tensor_tensor(k.x[:, s, :], k.acc[:, s, 0:C], k.x[:, s, :], ALU.add).then_inc(k.summed, 1)
            select(0, 0)
            groups(group, dve, {3: variance, 5: scale} if mix else {5: add_x})
            if mix:
                dve.wait_ge(k.dots_done, NT + 2)
                nc.vector.memset(m.dots[:, :, :], 0.0).then_inc(k.final, 1)
                dve.wait_ge(k.final, 1)
                dots = k.dots[:, :].rearrange("p (b n) -> p b n", n=P)
                for a in (0, DH):
                    nc.vector.tensor_copy(m.dots[a:a + DH, :, a:a + DH], dots[a:a + DH, :, a:a + DH]).then_inc(k.final, 1)


PER_MIX = 8


def mixer_parts(sb, ps, sem):
    k = Named()
    k.x_tile = sb("mx_x", [P, 2, CB, P])
    k.kv = sb("mx_kv", [P, 2, 2 * INNER])
    k.squares = sb("mx_squares", [P, 2 * INNER])
    k.sums = sb("mx_sums", [P, 2 * HEADS])
    k.var = sb("mx_var", [P, 2, 2 * HEADS])
    k.root = sb("mx_root", [P, 2, 2 * HEADS])
    k.both = sb("mx_both", [P, HEADS])
    k.rstd = sb("mx_rstd", [P, HEADS])
    k.kv_psum = ps("mx_kv_psum", [P, 2, INNER])
    k.dots = ps("mx_dots", [P, INNER])
    k.staged, k.kv_ready, k.kv_out, k.squared = sem("mx_staged"), sem("mx_kv_ready"), sem("mx_kv_out"), sem("mx_squared")
    k.steps, k.var_out, k.rooted = sem("mx_steps"), sem("mx_var_out"), sem("mx_rooted")
    k.scaled, k.dots_done = sem("mx_scaled"), sem("mx_dots_done")
    k.zeroed, k.final = sem("mx_zeroed"), sem("mx_final")
    return k


def mixed_parts(sb, ps, sem):
    k = Named()
    k.x_tile = sb("xm_x_tile", [P, 2, CB, P])
    k.x = sb("xm_x", [P, 2, C])
    k.zeros = sb("xm_zeros", [P, ZEROS])
    k.acc = ps("xm_acc", [P, 2, NODE_CHUNK])
    k.staged, k.product, k.summed, k.stored, k.blanked = (sem("xm_" + n) for n in "staged product summed stored blanked".split())
    k.x_loaded = [sem("xm_x_loaded0"), sem("xm_x_loaded1")]
    return k


def batch_norm_stage(nc, d, m, layer, last_layer):
    with ExitStack() as ctx:
        sb, ps, sem = make_tools(nc, ctx, f"norm{layer}_")
        stats = sb("bn_stats", [P, CB, len(NODE_CHUNKS), BNS])
        mv = sb("bn_mv", [P, CB, 2])
        root = sb("bn_root", [P, CB])
        scale, shift = m.bn_scale, m.bn_shift
        acc = ps("bn_acc", [P, 2, CB, NODE_CHUNK])
        product, biased, steps, var_ready, rooted, scaled, applied, counted, part_done = (
            sem("bn_" + x) for x in "product biased steps var_ready rooted scaled applied counted part_done".split())
        mixing = layer == 0
        if mixing:
            mid_psum = ps("mid_psum", [P, 2, NODE_CHUNK])
            mid = sb("mid", [P, INNER // P, C])
            mid_ready, mid_out, mix_ready, mix_out = (sem(x) for x in "mid_ready mid_out mix_ready mix_out".split())
        block = ctx.enter_context(nc.Block())
        w2, b2 = m.w2[layer], m.b2[layer]
        gains = m.gains[layer]
        nchunk = len(NODE_CHUNKS)

        def chunks(eng, body):
            with eng.Fori(0, FULL_CHUNKS // 2) as i:
                body(i * 2, 0, bass.ds(i * (2 * NODE_CHUNK), NODE_CHUNK), NODE_CHUNK)
                body(i * 2 + 1, 1, bass.ds(i * (2 * NODE_CHUNK) + NODE_CHUNK, NODE_CHUNK), NODE_CHUNK)
            for i in range(FULL_CHUNKS // 2 * 2, nchunk):
                a, n = NODE_CHUNKS[i]
                body(i, i % 2, slice(a, a + n), n)

        @block.tensor
        def _(pe):
            def body(i, s, cols, n):
                pe.wait_ge(biased, i + 1)
                for b in range(CB):
                    for c in range(CB):
                        last = nc.tensor.matmul(acc[:, s, b, 0:n], w2[:, c, b * P:(b + 1) * P], m.agg[:, c, cols],
                                                start=c == 0, stop=c == CB - 1)
                last.then_inc(product, 1)
            chunks(pe, body)
            if mixing:
                for b in range(INNER // P):
                    if b >= 2:
                        pe.wait_ge(mid_out, b - 1)
                    nc.tensor.matmul(mid_psum[:, b % 2, 0:C], m.dots[:, b, :], m.w_out[:, b, :], start=True, stop=True).then_inc(mid_ready, 1)
                pe.wait_ge(mid_out, INNER // P)
                for c in range(CB):
                    for b in range(INNER // P):
                        last = nc.tensor.matmul(mid_psum[:, c, 0:C], m.w_q[:, b, c * P:(c + 1) * P], mid[:, b, :],
                                                start=b == 0, stop=b == INNER // P - 1)
                    last.then_inc(mix_ready, 1)

        @block.scalar
        def _(act):
            act.sem_inc(biased, 2)

            def body(i, s, cols, n):
                act.wait_ge(product, i + 1)
                for b in range(CB):
                    ins = nc.scalar.activation(m.agg[:, b, cols], acc[:, s, b, 0:n], ACT.Identity, bias=b2[:, b:b + 1])
                ins.then_inc(biased, 1)
            chunks(act, body)
            if mixing:
                for b in range(INNER // P):
                    act.wait_ge(mid_ready, b + 1)
                    nc.scalar.activation(mid[:, b, :], mid_psum[:, b % 2, 0:C], ACT.Copy).then_inc(mid_out, 1)
                for c in range(CB):
                    act.wait_ge(mix_ready, c + 1)
                    nc.scalar.activation(m.w_mix[:, c, :], mid_psum[:, c, 0:C], ACT.Copy, scale=1.0 / N).then_inc(mix_out, 1)
            for norm in range(2):
                act.wait_ge(var_ready, norm + 1)
                nc.scalar.activation(root[:, :], mv[:, :, 1], ACT.Sqrt).then_inc(rooted, 1)
                if norm == 1 and not last_layer:
                    continue
                act.wait_ge(scaled, norm + 1)
                ends = norm == 1 and last_layer

                def apply(i, s, cols, n):
                    if ends:
                        act.wait_ge(part_done, i + 1)
                        for b in range(CB):
                            ins = nc.scalar.activation(m.agg[:, b, cols], m.agg[:, b, cols], ACT.Relu, bias=shift[:, b:b + 1])
                    else:
                        for b in range(CB):
                            ins = nc.scalar.activation(m.agg[:, b, cols], m.agg[:, b, cols], ACT.Relu, bias=shift[:, b:b + 1],
                                                       scale=scale[:, b:b + 1])
                    ins.then_inc(applied, 1)
                chunks(act, apply)

        @block.vector
        def _(dve):
            step = Steps(dve, steps)
            for norm in range(2):
                def count(i, s, cols, n):
                    if norm:
                        dve.wait_ge(applied, i + 1)
                    else:
                        dve.wait_ge(biased, i + 3)
                    at = bass.ds(i, 1)
                    for b in range(CB):
                        ins = nc.vector.bn_stats(stats[:, b, at, :].squeeze(1), m.agg[:, b, cols])
                    ins.then_inc(counted, 1)
                chunks(dve, count)
                dve.wait_ge(counted, nchunk * (norm + 1))
                for b in range(CB):
                    step(nc.vector.bn_aggr(mv[:, b, :], stats[:, b, :, :].rearrange("p a b -> p (a b)")))
                step(nc.vector.tensor_scalar(mv[:, :, 1], mv[:, :, 1], EPS, None, ALU.add))
                dve.sem_inc(var_ready, 1)
                dve.wait_ge(rooted, norm + 1)
                step(nc.vector.reciprocal(scale[:, :], root[:, :]))
                step(nc.vector.tensor_tensor(scale[:, :], scale[:, :], gains[norm][0], ALU.mult))
                step(nc.vector.tensor_tensor(shift[:, :], scale[:, :], mv[:, :, 0], ALU.mult))
                step(nc.vector.tensor_tensor(shift[:, :], gains[norm][1], shift[:, :], ALU.subtract))
                dve.sem_inc(scaled, 1)
            if last_layer:
                def residual(i, s, cols, n):
                    for b in range(CB):
                        ins = nc.vector.scalar_tensor_tensor(m.agg[:, b, cols], m.agg[:, b, cols], scale[:, b:b + 1],
                                                             m.xT[:, b, cols], ALU.mult, ALU.add)
                    ins.then_inc(part_done, 1)
                chunks(dve, residual)
            dve.wait_ge(applied, nchunk * (2 if last_layer else 1))


def route_stage(nc, d, m):
    with ExitStack() as ctx:
        sb, ps, sem = make_tools(nc, ctx, "rt_")
        gT_tile = sb("gT_tile", [P, BT, CB, P])
        x = sb("x", [P, 2, BT, C])
        xn = sb("xn", [P, 2, BT, C])
        turned_tile = sb("turned_tile", [P, 2, CB, P])
        stats, tmp = ([sb(f"{name}{i}", [P, BT, width]) for i in range(2)] for name, width in (("stats", BNS), ("tmp", 4)))
        mean, rstd = ([sb(f"{name}{i}", [P, BT])[:, :] for i in range(2)] for name in ("mean", "rstd"))
        shift = sb("shift", [P, BT])
        p, eq, where, place, both = (sb(name, [P, BT, NX])[:, :, :] for name in ("p", "eq", "where", "place", "both"))
        oh, placed = sb("oh", [P, 2, BT, NX]), sb("placed", [P, 2, BT, NX])
        best = sb("best", [P, 2, BT])
        ident, total = sb("ident", [P, BT])[:, :], sb("total", [P, BT])[:, :]
        row = sb("row", [P, 2, BT])
        idx = sb("idx", [P, 2, 2, BT], U32)
        scan_in, scan_out, scan_keep = (sb(name, [P, NX, BT + 1])[:, :, :] for name in ("scan_in", "scan_out", "scan_keep"))
        valid, node = sb("valid", [P, NT]), sb("node", [P, NT], I32)
        expert, region, expert_i = sb("expert", [P, NX])[:, :], sb("region", [P, NX])[:, :], sb("expert_i", [P, NX], I32)
        picked = sb("picked", [P, BT, NX], BF16)
        earlier, all_ones = sb("earlier", [P, P], BF16), sb("all_ones", [P, P], BF16)
        zeros = sb("zeros", [P, TOK // P, C])
        G = MAX_TILES + 2
        oh_all, row_all = sb("oh_all", [P, 2, NT, NX]), sb("row_all", [P, 2, NT])
        own_tiles, before, offset = (sb(name, [P, NX])[:, :] for name in ("own_tiles", "before", "offset"))
        own_i, fill_i, offset_step = sb("own_i", [P, NX], I32), sb("fill_i", [1, NX], I32), sb("offset_step", [1, NX])
        ordered, by_order = sb("ordered", [P, 2, NT]), sb("by_order", [P, 2, NT])
        tile_i, tile = sb("tile_i", [1, G], I32), sb("tile", [1, G])
        begun, begun_off = sb("begun", [1, G, NX]), sb("begun_off", [1, G, NX])
        last_expert, tile_row = sb("last_expert", [1, G]), sb("tile_row", [1, G])

        acc = ps("acc", [P, -(-BT // 2), 2, C])
        turned = ps("turned", [P, 2, NODE_CHUNK])
        logits = ps("logits", [P, NODE_CHUNK])
        counts = ps("counts", [P, NODE_CHUNK])
        (staged, gnn_turned, joined, x2_counted, join_steps, var1_ready, rooted1, xn_ready, xn_counted, steps, var2_ready,
         rooted2, scaled2, turned_ready, turned_used, logit_ready, shifted, exped, pick_ready, count_ready, idx_ready,
         normed, x2_stored, pool_steps, end_steps, fill_ready) = (
            sem(name) for name in ("staged gnn_turned joined x2_counted join_steps var1_ready rooted1 xn_ready xn_counted steps "
                                   "var2_ready rooted2 scaled2 turned_ready turned_used logit_ready shifted exped pick_ready "
                                   "count_ready idx_ready normed x2_stored pool_steps end_steps fill_ready").split())
        x_loaded, sent = [sem("x_loaded0"), sem("x_loaded1")], [sem("sent0"), sem("sent1")]
        block = ctx.enter_context(nc.Block())
        JOIN_STEPS, BLOCK_STEPS = 8, 37
        POOL_STEPS = 13

        def bank_end(j):
            return min(j // 2 * 2 + 2, BT)

        def turned_slot(s, j):
            return (s * BT + j) % 2

        @block.sync
        def _(sp):
            def load(k, s):
                sp.dma_start(x[:, s, 0:BT - 1, :], d.x_mixed[bass.ds(k * (BT * P), (BT - 1) * P), :].rearrange("(t p) c -> p t c", p=P))\
                    .then_inc(x_loaded[s], 16)
                n = TAIL if isinstance(k, int) and k == NBLK - 1 else P
                sp.dma_start(x[0:n, s, BT - 1, :], d.x_mixed[bass.ds(k * (BT * P) + (BT - 1) * P, n), :]).then_inc(x_loaded[s], 16)

            def store(k, s):
                sp.wait_ge(xn_ready, k * BT + BT)
                if isinstance(k, int) and k == NBLK - 1:
                    sp.dma_start(d.x2[k * BT * P:(NT - 1) * P, :].rearrange("(t p) c -> p t c", p=P), x[:, s, 0:BT - 1, :])\
                        .then_inc(x2_stored, 16)
                    sp.dma_start(d.x2[(NT - 1) * P:N, :], x[0:TAIL, s, BT - 1, :]).then_inc(x2_stored, 16)
                else:
                    sp.dma_start(d.x2[bass.ds(k * (BT * P), BT * P), :].rearrange("(t p) c -> p t c", p=P), x[:, s, :, :])\
                        .then_inc(x2_stored, 16)

            def turn(k, s):
                store(k, s)
                sp.wait_ge(x2_stored, k * 16 + 16)
                load(k + 2, s)
            load(0, 0)
            load(1, 1)
            tiles(sp, turn, count=NBLK - 3)
            turn(NBLK - 3, (NBLK - 3) % 2)
            store(NBLK - 2, (NBLK - 2) % 2)
            store(NBLK - 1, (NBLK - 1) % 2)
            sp.wait_ge(fill_ready, 1)
            sp.nop(nofuse=True)
            with sp.Fori(0, NX) as e:
                at = sp.value_load(fill_i[0:1, bass.ds(e, 1)], min_val=0, max_val=NX * CAP - TOK)
                sp.dma_start(d.routed[bass.ds(at, TOK), :].rearrange("(p a) c -> p a c", p=P), zeros[:, :, :]).then_inc(x2_stored, 16)
            sp.wait_ge(x2_stored, 16 * (NBLK + 1) + 16 * NX)
            for s in range(2):
                blocks = visits(2, s, NBLK)
                sp.wait_ge(sent[s], 2 * BT * 16 * blocks)

        @block.gpsimd
        def _(pool):
            step = Steps(pool, pool_steps)
            step(pool.iota(node[:, :], [[P, NT]], base=0, channel_multiplier=1))
            step(pool.tensor_copy(valid[:, :], node[:, :]))
            step(pool.tensor_scalar(valid[:, :], valid[:, :], float(N), None, ALU.is_lt))
            step(pool.iota(expert_i[:, :], [[1, NX]], base=0, channel_multiplier=0))
            step(pool.tensor_copy(expert, expert_i[:, :]))
            step(pool.tensor_scalar(region, expert, float(CAP), None, ALU.mult))
            step(pool.memset(all_ones[:, :], 1.0))
            step(pool.affine_select(out=earlier[:, :], in_=all_ones[:, :], compare_op=ALU.is_gt, fill=0.0,
                                    base=0, pattern=[[1, P]], channel_multiplier=-1))
            step(pool.memset(scan_keep, 1.0))
            step(pool.memset(scan_keep[:, :, 0], 0.0))
            step(pool.memset(zeros[:, :, :], 0.0))
            step(pool.iota(tile_i[:, :], [[1, G]], base=0, channel_multiplier=0))
            step(pool.tensor_copy(tile[:, :], tile_i[:, :]))
            assert step.n == POOL_STEPS

            def scatter(k, s):
                pool.wait_ge(idx_ready, k + 1)
                for j in range(BT):
                    pool.wait_ge(normed, k * BT + j + 1)
                    pool.nop(nofuse=True)
                    n = TAIL if is_last(k * BT + j) else P
                    for i in range(2):
                        pool.indirect_dma_start(d.routed[:, :], bass.IndirectOffsetOnAxis(ap=idx[0:n, s, i, j:j + 1], axis=0),
                                                xn[0:n, s, j, :], None).then_inc(sent[s], 16)
            tiles(pool, scatter, count=NBLK)

        @block.tensor
        def _(pe):
            def turn_gnn(k):
                for j in range(BT):
                    pe.wait_ge(staged, k * BT + j + 1)
                    pe.wait_ge(joined, k * BT + bank_end(j))
                    out = acc[:, j // 2, j % 2, :]
                    for c in range(CB):
                        last = nc.tensor.transpose(out[:, c * P:(c + 1) * P], gT_tile[:, j, c, :], m.ident[:, :])
                    last.then_inc(gnn_turned, 1)

            def route(k, s):
                def turn(j):
                    pe.wait_ge(xn_ready, k * BT + j + 1)
                    pe.wait_ge(turned_used, k * BT + j + 1)
                    for c in range(CB):
                        last = nc.tensor.transpose(turned[:, turned_slot(s, j), c * P:(c + 1) * P], xn[:, s, j, c * P:(c + 1) * P],
                                                   m.ident[:, :])
                    last.then_inc(turned_ready, 1)
                more = not (isinstance(k, int) and k == NBLK - 1)
                if more:
                    turn_gnn(k + 1)
                turn(0)
                for j in range(BT):
                    if j < BT - 1:
                        turn(j + 1)
                    pe.wait_ge(turned_used, k * BT + j + 3)
                    out = logits[:, j * NX:(j + 1) * NX]
                    nc.tensor.matmul(out, m.ones[0:1, :], m.br[0:1, :], start=True, stop=False)
                    for c in range(CB):
                        last = nc.tensor.matmul(out, turned_tile[:, turned_slot(s, j), c, :], m.wr[:, c, :], start=False, stop=c == CB - 1)
                last.then_inc(logit_ready, 1)
                pe.wait_ge(pick_ready, k + 1)
                both_picked = picked[:, :, :].rearrange("p t e -> p (t e)")
                nc.tensor.matmul(counts[:, 0:BT * NX], earlier[:, :], both_picked, start=True, stop=True)
                nc.tensor.matmul(counts[:, BT * NX:2 * BT * NX], all_ones[:, :], both_picked, start=True, stop=True).then_inc(count_ready, 1)
            turn_gnn(0)
            tiles(pe, route, count=NBLK)

        @block.scalar
        def _(act):
            act.sem_inc(gnn_turned, BT)
            act.sem_inc(turned_used, 2)

            def stage(k):
                for j in range(BT):
                    act.wait_ge(gnn_turned, k * BT + j + 1)
                    at = bass.ds(k * (BT * P) + j * P, P)
                    nc.scalar.activation(gT_tile[:, j, :, :], m.agg[:, :, at], ACT.Copy).then_inc(staged, 1)

            def root(ready, count, i, to):
                act.wait_ge(ready, count)
                nc.scalar.activation(tmp[i][:, :, 3], tmp[i][:, :, 2], ACT.Sqrt).then_inc(to, 1)

            def route(k, s):
                more = not (isinstance(k, int) and k == NBLK - 1)
                if more:
                    stage(k + 1)
                for j in range(BT):
                    act.wait_ge(turned_ready, k * BT + j + 1)
                    slot = turned_slot(s, j)
                    nc.scalar.activation(turned_tile[:, slot, :, :], turned[:, slot, 0:C].rearrange("p (c n) -> p c n", c=CB),
                                         ACT.Copy).then_inc(turned_used, 1)
                root(var2_ready, k + 1, 1, rooted2)
                if more:
                    root(var1_ready, k + 2, 0, rooted1)
                act.wait_ge(shifted, k + 1)
                nc.scalar.activation(p, p, ACT.Exp).then_inc(exped, 1)
                act.wait_ge(scaled2, k + 1)
                for j in range(BT):
                    nc.scalar.activation(xn[:, s, j, :], xn[:, s, j, :], ACT.Identity, bias=shift[:, j:j + 1],
                                         scale=rstd[1][:, j:j + 1]).then_inc(normed, 1)
            stage(0)
            root(var1_ready, 1, 0, rooted1)
            tiles(act, route, count=NBLK)

        @block.vector
        def _(dve):
            tt, ts, stt = nc.vector.tensor_tensor, nc.vector.tensor_scalar, nc.vector.scalar_tensor_tensor

            def bc(v):
                return v.unsqueeze(2).to_broadcast([P, BT, NX])

            def over_tiles(v):
                return v.unsqueeze(1).to_broadcast([P, BT, NX])

            def join(k, s):
                dve.wait_ge(x_loaded[s], (k - s) * 16 + 32)
                for j in range(BT):
                    dve.wait_ge(gnn_turned, k * BT + (BT + bank_end(j)))
                    tt(x[:, s, j, :], acc[:, j // 2, j % 2, :], x[:, s, j, :], ALU.add).then_inc(joined, 1)
                for j in range(BT):
                    dve.wait_ge(joined, k * BT + (BT + j + 1))
                    nc.vector.bn_stats(stats[0][:, j, :], x[:, s, j, :]).then_inc(x2_counted, 1)
                dve.wait_ge(x2_counted, k * BT + BT)
                step = Steps(dve, join_steps, k * JOIN_STEPS)
                merge_stats(nc, step, stats[0], tmp[0], mean[0])
                step(ts(tmp[0][:, :, 2], tmp[0][:, :, 2], EPS, None, ALU.add))
                assert step.n == JOIN_STEPS
                dve.sem_inc(var1_ready, 1)

            def route(k, s):
                step = Steps(dve, steps, k * BLOCK_STEPS)
                dve.wait_ge(rooted1, k + 1)
                step(nc.vector.reciprocal(rstd[0], tmp[0][:, :, 3]))
                if not is_first(k):
                    dve.wait_ge(sent[s], (k - s) * (BT * 16))
                    dve.nop(nofuse=True)
                for j in range(BT):
                    ts(xn[:, s, j, :], x[:, s, j, :], mean[0][:, j:j + 1], rstd[0][:, j:j + 1], ALU.subtract, ALU.mult)\
                        .then_inc(xn_ready, 1)
                for j in range(BT):
                    dve.wait_ge(xn_ready, k * BT + j + 1)
                    nc.vector.bn_stats(stats[1][:, j, :], xn[:, s, j, :]).then_inc(xn_counted, 1)
                dve.wait_ge(xn_counted, k * BT + BT)
                merge_stats(nc, step, stats[1], tmp[1], mean[1])
                step(ts(tmp[1][:, :, 2], tmp[1][:, :, 2], EPS, None, ALU.add))
                dve.sem_inc(var2_ready, 1)
                if not (isinstance(k, int) and k == NBLK - 1):
                    join(k + 1, 1 - s)
                dve.wait_ge(logit_ready, k + 1)
                lg = logits[:, 0:BT * NX].rearrange("p (t e) -> p t e", e=NX)
                step(nc.vector.tensor_reduce(total, lg, AX, ALU.max))
                step(tt(p, lg, bc(total), ALU.subtract))
                dve.sem_inc(shifted, 1)
                dve.wait_ge(rooted2, k + 1)
                step(nc.vector.reciprocal(rstd[1], tmp[1][:, :, 3]))
                step(stt(shift[:, :], mean[1], -1.0, rstd[1], ALU.mult, ALU.mult))
                dve.sem_inc(scaled2, 1)
                dve.wait_ge(exped, k + 1)
                step(nc.vector.tensor_reduce(total, p, AX, ALU.add))
                step(nc.vector.reciprocal(total, total))
                step(tt(p, p, bc(total), ALU.mult))
                for i in range(2):
                    step(nc.vector.tensor_reduce(best[:, i, :], p, AX, ALU.max))
                    step(tt(eq, p, bc(best[:, i, :]), ALU.is_equal))
                    step(stt(where, eq, -float(NX), over_tiles(expert), ALU.mult, ALU.add))
                    step(nc.vector.tensor_reduce(ident, where, AX, ALU.min))
                    step(tt(oh[:, i, :, :], where, bc(ident), ALU.is_equal))
                    if i == 0:
                        step(stt(p, oh[:, i, :, :], -2.0, p, ALU.mult, ALU.add))
                step(tt(both, oh[:, 0, :, :], oh[:, 1, :, :], ALU.add))
                tt(picked[:, :, :], both, bc(valid[:, bass.ds(k * BT, BT)]), ALU.mult).then_inc(pick_ready, 1)
                step(tt(total, best[:, 0, :], best[:, 1, :], ALU.add))
                step(nc.vector.reciprocal(total, total))
                tt(m.weight[:, :, bass.ds(k * BT, BT)], best[:, :, :], total.unsqueeze(1).to_broadcast([P, 2, BT]), ALU.mult)
                dve.wait_ge(count_ready, k + 1)
                step(nc.vector.tensor_copy(scan_in[:, :, 1:BT + 1], counts[:, BT * NX:2 * BT * NX].rearrange("p (t e) -> p e t", e=NX)))
                step(nc.vector.tensor_tensor_scan(scan_out.rearrange("p e t -> p (e t)"), scan_keep.rearrange("p e t -> p (e t)"),
                                                  scan_in.rearrange("p e t -> p (e t)"), 0.0, ALU.mult, ALU.add))
                step.go(nc.vector.tensor_copy(scan_in[:, :, 0], scan_out[:, :, BT]))
                step(tt(place, scan_out[:, :, 0:BT].rearrange("p e t -> p t e"), over_tiles(region), ALU.add))
                step(tt(place, place, counts[:, 0:BT * NX].rearrange("p (t e) -> p t e", e=NX), ALU.add))
                step(tt(placed[:, :, :, :], oh[:, :, :, :], place.unsqueeze(1).to_broadcast([P, 2, BT, NX]), ALU.mult))
                step(nc.vector.tensor_reduce(row[:, :, :], placed[:, :, :, :], AX, ALU.add))
                nc.vector.tensor_copy(idx[:, s, :, :], row[:, :, :]).then_inc(idx_ready, 1)
                dve.nop(nofuse=True)
                at = bass.ds(k * BT, BT)
                ts(row_all[:, :, at], row[:, :, :], 0.0, None, ALU.add)
                ts(oh_all[:, :, at, :], oh[:, :, :, :], 0.0, None, ALU.add)
                assert step.n == BLOCK_STEPS, step.n
            dve.sem_inc(joined, BT)
            nc.vector.memset(scan_in, 0.0)
            join(0, 0)
            dve.wait_ge(pool_steps, POOL_STEPS)
            tiles(dve, route, peel=True, count=NBLK)

            step = Steps(dve, end_steps)
            total_e = scan_out[:, :, BT]
            step(tt(fill_i[:, :], total_e[0:1], region[0:1], ALU.add))
            dve.sem_inc(fill_ready, 1)
            step(ts(own_tiles, total_e, float(TOK - 1), None, ALU.add))
            step(nc.vector.tensor_copy(own_i[:, :], own_tiles))
            step(ts(own_i[:, :], own_i[:, :], TOK.bit_length() - 1, None, ALU.logical_shift_right))
            step(nc.vector.tensor_copy(own_tiles, own_i[:, :]))
            step(ts(own_tiles, own_tiles, 1.0, None, ALU.max))
            step(nc.vector.tensor_tensor_scan(before, own_tiles, zeros[:, 0, 0:NX], 0.0, ALU.add, ALU.add))
            step(tt(before, before, own_tiles, ALU.subtract))
            step(stt(offset, before, -float(TOK), region, ALU.mult, ALU.add))
            step(nc.vector.tensor_copy(m.expert_i[:, 0, :], own_tiles[0:1]))
            step(nc.vector.tensor_copy(m.expert_i[:, 1, :], before[0:1]))
            step(tt(m.tile_total[:, :], own_tiles[0:1, NX - 1:NX], before[0:1, NX - 1:NX], ALU.add))
            shape = [1, G, NX]
            tile_bc = tile[:, :].unsqueeze(2).to_broadcast(shape)
            step(nc.vector.tensor_copy(offset_step[:, 0:1], offset[0:1, 0:1]))
            step(tt(offset_step[:, 1:NX], offset[0:1, 1:NX], offset[0:1, 0:NX - 1], ALU.subtract))
            step(tt(begun[:, :, :], tile_bc, before[0:1].unsqueeze(1).to_broadcast(shape), ALU.is_ge))
            step(nc.vector.tensor_reduce(last_expert[:, :], begun[:, :, :], AX, ALU.add))
            step(ts(m.tile_expert[:, :], last_expert[:, :], -1.0, None, ALU.add))
            step(tt(begun_off[:, :, :], begun[:, :, :], offset_step[:, :].unsqueeze(1).to_broadcast(shape), ALU.mult))
            step(nc.vector.tensor_reduce(tile_row[:, :], begun_off[:, :, :], AX, ALU.add))
            step(stt(tile_row[:, :], tile[:, :], float(TOK), tile_row[:, :], ALU.mult, ALU.add))
            step(tt(own_tiles[0:1, 0:1], own_tiles[0:1, NX - 1:NX], before[0:1, NX - 1:NX], ALU.add))
            step(ts(tile[:, :], tile[:, :], own_tiles[0:1, 0:1], None, ALU.is_lt))
            step(tt(m.tile_row[:, :], tile_row[:, :], tile[:, :], ALU.mult))
            step(tt(oh_all[:, :, :, :].rearrange("p i t e -> p (i t) e"), oh_all[:, :, :, :].rearrange("p i t e -> p (i t) e"),
                    offset.unsqueeze(1).to_broadcast([P, 2 * NT, NX]), ALU.mult))
            step(nc.vector.tensor_reduce(m.row_f[:, :, :], oh_all[:, :, :, :], AX, ALU.add))
            step(tt(row_all[:, :, :], row_all[:, :, :], m.row_f[:, :, :], ALU.subtract))
            first, second = row_all[:, 0, :], row_all[:, 1, :]
            step(tt(m.row[:, 0, :], first, second, ALU.min))
            step(tt(m.row[:, 1, :], first, second, ALU.max))
            step(tt(ordered[:, 0, :], first, second, ALU.is_lt))
            step(tt(ordered[:, 1, :], first, second, ALU.is_gt))
            for i in range(2):
                step(tt(m.row_f[:, :, :], m.weight[:, :, :], ordered[:, :, :] if i == 0 else ordered[:, ::-1, :], ALU.mult))
                step(tt(by_order[:, i, :], m.row_f[:, 0, :], m.row_f[:, 1, :], ALU.add))
            step(nc.vector.tensor_copy(m.weight[:, :, :], by_order[:, :, :]))


def expert_weights(sb):
    x = Named()
    x.w1, x.w2 = ([[sb(f"ex_{name}_{part}{s}", [P, k, n], F32R)[:, :, :] for part in ("high", "low")] for s in range(2)]
                  for name, k, n in (("w1", CB, HID), ("w2", HB, C)))
    x.b2 = sb("ex_b2", [P, NX, C])[:, :, :]
    return x


def load_weights(eng, d, m, e, loaded):
    eng.dma_start(m.raw1, d.W1[bass.ds(e, 1), :, :].squeeze(0).rearrange("(c p) h -> p c h", p=P)).then_inc(loaded, 16)
    eng.dma_start(m.raw2, d.W2[bass.ds(e, 1), :, :].squeeze(0).rearrange("(k p) c -> p k c", p=P)).then_inc(loaded, 16)


def split_weights(pool, d, m, e, s, before=None):
    x = m.experts
    load_weights(pool, d, m, e, m.raw_loaded)
    if before is not None:
        pool.wait_ge(m.y_ready, before)
    pool.wait_ge(m.raw_loaded, e * 32)
    pool.nop(nofuse=True)
    pool.tensor_copy(x.w1[s][0], m.raw1).then_inc(m.w_high, 1)
    pool.tensor_copy(x.w2[s][0], m.raw2).then_inc(m.w_high, 1)
    pool.wait_ge(m.w_high, e * 2 + 2)
    pool.nop(nofuse=True)
    pool.tensor_tensor(x.w1[s][1], m.raw1, x.w1[s][0].bitcast(F32), ALU.subtract).then_inc(m.w_ready[s], 1)
    pool.tensor_tensor(x.w2[s][1], m.raw2, x.w2[s][0].bitcast(F32), ALU.subtract).then_inc(m.w_ready[s], 1)
    pool.wait_ge(m.w_ready[s], e - s + 2)
    pool.nop(nofuse=True)


def expert_stage(nc, d, m):
    with ExitStack() as ctx:
        sb, ps, sem = make_tools(nc, ctx)
        x = sb("ex_x", [P, TOK // P, C])
        x_full, hidden_full = sb("ex_x_full", [P, CB, TOK]), sb("ex_hidden_full", [P, HB, TOK])
        xT = [sb("ex_xT_" + part, [P, CB, TOK], F32R) for part in ("high", "low")]
        hT = [sb("ex_hT_" + part, [P, HB, TOK], F32R) for part in ("high", "low")]
        y = sb("ex_y", [P, TOK // P, C])
        turned = ps("ex_turned", [P, CB, TOK])
        hidden = ps("ex_hidden", [P, HB, TOK])
        out = ps("ex_out", [P, TOK // P, C])
        x_loaded, turned_ready, x_steps, x_ready, h_ready, h_out, h_high, h_split, y_out, y_stored, y_free = (
            sem("ex_" + n) for n in ("x_loaded turned_ready x_steps x_ready h_ready h_out h_high h_split y_out "
                                     "y_stored y_free").split())
        first_loaded = sem("ex_first_loaded")
        block = ctx.enter_context(nc.Block())
        PARTS = ((0, 0), (0, 1), (1, 0))
        BANKS = HB // HPB

        def all_tiles(eng):
            return eng.value_load(m.tile_total[0:1, 0:1], min_val=NX, max_val=MAX_TILES)

        def expert_of(eng, tile):
            return eng.value_load(m.tile_expert[0:1, bass.ds(tile, 1)], min_val=0, max_val=NX - 1)

        @block.gpsimd
        def _(pool):
            pool.wait_ge(m.w_ready[0], 2)
            pool.nop(nofuse=True)
            split_weights(pool, d, m, 1, 1)
            with pool.Fori(1, NX // 2) as i:
                for s in range(2):
                    before = pool.value_load(m.expert_i[0:1, 1:2, bass.ds(i * 2 + (s - 1), 1)].squeeze(1), min_val=1, max_val=MAX_TILES)
                    split_weights(pool, d, m, i * 2 + s, s, before)
            before = pool.value_load(m.expert_i[0:1, 1:2, NX - 1:NX].squeeze(1), min_val=1, max_val=MAX_TILES)
            pool.wait_ge(y_free, before + 1)
            pool.nop(nofuse=True)
            for t in range(NT):
                n = TAIL if is_last(t) else P
                pool.indirect_dma_start(m.lower[0:n, t, :], None, d.expert_out[:, :],
                                        bass.IndirectOffsetOnAxis(ap=m.row[0:n, 0, t:t + 1], axis=0)).then_inc(m.lower_got, 16)

        @block.sync
        def _(sp):
            def load(g):
                row = sp.value_load(m.tile_row[0:1, bass.ds(g, 1)], min_val=0, max_val=NX * CAP - TOK)
                sp.dma_start(x[:, :, :], d.routed[bass.ds(row, TOK), :].rearrange("(a p) c -> p a c", p=P)).then_inc(x_loaded, 16)
            sp.sem_inc(y_free, 1)
            load(0)
            load_weights(sp, d, m, 0, first_loaded)
            sp.dma_start(m.experts.b2, d.b2.unsqueeze(0).to_broadcast([P, NX, C])).then_inc(first_loaded, 16)
            sp.wait_ge(turned_ready, 1)
            load(1)
            with sp.Fori(0, all_tiles(sp)) as g:
                sp.wait_ge(turned_ready, g + 2)
                load(g + 2)
                sp.wait_ge(y_out, g + 2)
                row = nc.s_assert_within(g * TOK, 0, ROWS - TOK,
                                         skip_runtime_bounds_check_because="the experts' tiles are at most MAX_TILES")
                sp.dma_start(d.expert_out[bass.ds(row, TOK), :].rearrange("(a p) c -> p a c", p=P), y[:, :, :])\
                    .then_inc(y_stored, 16)
                sp.wait_ge(y_stored, g * 16 + 16)
                sp.sem_inc(y_free, 1)
            sp.wait_ge(x_loaded, all_tiles(sp) * 16 + 32)
            sp.nop(nofuse=True)
            sp.wait_ge(m.lower_got, 16 * NT)

        @block.tensor
        def _(pe):
            def turn(g):
                pe.wait_ge(x_loaded, g * 16 + 16)
                for c in range(CB):
                    for a in range(TOK // P):
                        last = nc.tensor.transpose(turned[:, c, a * P:(a + 1) * P], x[:, a, c * P:(c + 1) * P], m.ident[:, :])
                last.then_inc(turned_ready, 1)
            turn(0)
            with pe.Fori(0, NX // 2) as i:
                for s in range(2):
                    at = bass.ds(i * 2 + s, 1)
                    n = pe.value_load(m.expert_i[0:1, 0:1, at].squeeze(1), min_val=1, max_val=-(-N // TOK))
                    before = pe.value_load(m.expert_i[0:1, 1:2, at].squeeze(1), min_val=0, max_val=MAX_TILES)
                    w1, w2 = m.experts.w1[s], m.experts.w2[s]
                    pe.wait_ge(m.w_ready[s], i * 2 + 2)
                    pe.nop(nofuse=True)
                    with pe.Fori(0, n) as j:
                        pe.wait_ge(x_ready, before + j + 1)
                        for h in range(HB):
                            for c in range(CB):
                                for k, (still, moving) in enumerate(PARTS):
                                    last = nc.tensor.matmul(hidden[:, h, :], w1[still][:, c, h * P:(h + 1) * P], xT[moving][:, c, :],
                                                            start=c == 0 and k == 0, stop=c == CB - 1 and k == len(PARTS) - 1)
                            if h % HPB == HPB - 1:
                                last.then_inc(h_ready, 1)
                        turn(before + j + 1)
                        pe.wait_ge(y_out, before + j + 1)
                        for a in range(TOK // P):
                            for h in range(HB):
                                if a == 0 and h % HPB == 0:
                                    pe.wait_ge(h_split, (before + j) * BANKS + (h // HPB + 1))
                                for k, (still, moving) in enumerate(PARTS):
                                    last = nc.tensor.matmul(out[:, a, :], hT[still][:, h, a * P:(a + 1) * P], w2[moving][:, h, :],
                                                            start=h == 0 and k == 0, stop=h == HB - 1 and k == len(PARTS) - 1)
                        last.then_inc(m.y_ready, 1)

        @block.scalar
        def _(act):
            act.wait_ge(first_loaded, 48)
            for to, frm in ((m.experts.w1[0][0], m.raw1), (m.experts.w2[0][0], m.raw2)):
                nc.scalar.activation(to, frm, ACT.Copy).then_inc(m.w_high, 1)
            with act.Fori(0, all_tiles(act)) as g:
                e = expert_of(act, g)
                for h in range(HB):
                    if h % HPB == 0:
                        act.wait_ge(h_ready, g * BANKS + (h // HPB + 1))
                    last = nc.scalar.activation(hidden_full[:, h, :], hidden[:, h, :], ACT.Gelu,
                                                bias=m.b1[:, h:h + 1, bass.ds(e, 1)].squeeze(1))
                    if h % HPB == HPB - 1:
                        last.then_inc(h_out, 1)

        @block.vector
        def _(dve):
            def gain(g):
                e = expert_of(dve, g)
                dve.wait_ge(turned_ready, g + 1)
                for c in range(CB):
                    last = nc.vector.tensor_scalar(x_full[:, c, :], turned[:, c, :], m.ln_g[:, c:c + 1, bass.ds(e, 1)].squeeze(1),
                                                   m.ln_b[:, c:c + 1, bass.ds(e, 1)].squeeze(1), ALU.mult, ALU.add)
                last.then_inc(x_steps, 1)
                dve.wait_ge(x_steps, g * 2 + 1)
                nc.vector.tensor_copy(xT[0][:, :, :], x_full[:, :, :]).then_inc(x_steps, 1)
                dve.wait_ge(x_steps, g * 2 + 2)
                nc.vector.tensor_tensor(xT[1][:, :, :], x_full[:, :, :], xT[0][:, :, :].bitcast(F32), ALU.subtract).then_inc(x_ready, 1)
            dve.sem_inc(y_out, 1)
            gain(0)
            for i, (w, raw) in enumerate(((m.experts.w1[0], m.raw1), (m.experts.w2[0], m.raw2))):
                dve.wait_ge(m.w_high, i + 1)
                nc.vector.tensor_tensor(w[1], raw, w[0].bitcast(F32), ALU.subtract).then_inc(m.w_ready[0], 1)
            dve.wait_ge(first_loaded, 48)
            dve.nop(nofuse=True)
            with dve.Fori(0, all_tiles(dve)) as g:
                for b in range(BANKS):
                    at = slice(b * HPB, (b + 1) * HPB)
                    dve.wait_ge(h_out, g * BANKS + (b + 1))
                    nc.vector.tensor_copy(hT[0][:, at, :], hidden_full[:, at, :]).then_inc(h_high, 1)
                    dve.wait_ge(h_high, g * BANKS + (b + 1))
                    nc.vector.tensor_tensor(hT[1][:, at, :], hidden_full[:, at, :], hT[0][:, at, :].bitcast(F32), ALU.subtract)\
                        .then_inc(h_split, 1)
                gain(g + 1)
                e = expert_of(dve, g)
                dve.wait_ge(m.y_ready, g + 1)
                dve.wait_ge(y_free, g + 1)
                nc.vector.tensor_tensor(y[:, :, :], out[:, :, :], m.experts.b2[:, bass.ds(e, 1), :].to_broadcast([P, TOK // P, C]),
                                        ALU.add).then_inc(y_out, 1)


def combine_stage(nc, d, m):
    with ExitStack() as ctx:
        sb, ps, sem = make_tools(nc, ctx)
        slots = 4
        idx = sb("cb_idx", [P, slots], U32)
        rows = sb("cb_rows", [P, slots, C])
        x2 = sb("cb_x2", [P, slots, C])
        res = sb("cb_res", [P, slots, C])
        idx_ready, half, done = sem("cb_idx_ready"), sem("cb_half"), sem("cb_done")
        got, x2_loaded, stored = ([sem(f"cb_{name}{s}") for s in range(slots)] for name in ("got", "x2_loaded", "stored"))
        block = ctx.enter_context(nc.Block())

        @block.scalar
        def _(act):
            act.sem_inc(done, slots)

            def body(t, s):
                act.wait_ge(done, t + 1)
                nc.scalar.activation(idx[:, s:s + 1], m.row[:, 1:2, bass.ds(t, 1)].squeeze(1), ACT.Copy).then_inc(idx_ready, 1)
            tiles(act, body, slots)

        @block.gpsimd
        def _(pool):
            def body(t, s):
                pool.wait_ge(idx_ready, t + 1)
                pool.nop(nofuse=True)
                n = TAIL if is_last(t) else P
                pool.indirect_dma_start(rows[0:n, s, :], None, d.expert_out[:, :],
                                        bass.IndirectOffsetOnAxis(ap=idx[0:n, s:s + 1], axis=0)).then_inc(got[s], 16)
            tiles(pool, body, slots)

        @block.vector
        def _(dve):
            def body(t, s):
                n = TAIL if is_last(t) else P
                dve.wait_ge(got[s], (t - s) * (16 // slots) + 16)
                dve.wait_ge(x2_loaded[s], (t - s) * (16 // slots) + 16)
                if not is_first(t, slots):
                    dve.wait_ge(stored[s], (t - s) * (16 // slots))
                at = bass.ds(t, 1)
                nc.vector.scalar_tensor_tensor(res[0:n, s, :], m.lower[0:n, at, :].squeeze(1), m.weight[0:n, 0, at], x2[0:n, s, :],
                                               ALU.mult, ALU.add).then_inc(half, 1)
                dve.wait_ge(half, t + 1)
                nc.vector.scalar_tensor_tensor(res[0:n, s, :], rows[0:n, s, :], m.weight[0:n, 1, at], res[0:n, s, :],
                                               ALU.mult, ALU.add).then_inc(done, 1)
            tiles(dve, body, slots, peel=True)

        @block.sync
        def _(sp):
            def store(t, s):
                if is_last(t):
                    sp.dma_start(d.out[(NT - 1) * P:N, :], res[0:TAIL, s, :]).then_inc(stored[s], 16)
                else:
                    sp.dma_start(d.out[bass.ds(t * P, P), :], res[:, s, :]).then_inc(stored[s], 16)

            def body(t, s):
                sp.wait_ge(done, t + 1)
                if not is_first(t, slots):
                    store(t - slots, s)
                if is_last(t):
                    sp.dma_start(x2[0:TAIL, s, :], d.x2[(NT - 1) * P:N, :]).then_inc(x2_loaded[s], 16)
                else:
                    sp.dma_start(x2[:, s, :], d.x2[bass.ds(t * P, P), :]).then_inc(x2_loaded[s], 16)
            tiles(sp, body, slots, peel=True)
            for t in range(NT - slots, NT):
                sp.wait_ge(done, slots + t + 1)
                store(t, t % slots)
            for s in range(slots):
                sp.wait_ge(stored[s], 16 * visits(slots, s))


def build(nc, d):
    with ExitStack() as ctx:
        sb, ps, sem = make_tools(nc, ctx)
        m = Named()
        m.ident = sb("ident", [P, P])
        m.iota_i, m.iota = sb("iota_i", [P, W], I32), sb("iota", [P, W])
        m.offsets_i, m.offsets = sb("offsets_i", [P, N // W + 2], I32), sb("offsets", [P, N // W + 2])
        m.ones = sb("ones", [1, P])
        m.mean, m.rstd = sb("mean", [P, NT]), sb("rstd", [P, NT])
        m.weight = sb("weight", [P, 2, NT])
        m.row = sb("row", [P, 2, NT], U32)
        m.expert_i = sb("expert_i", [1, 2, NX], I32)
        m.tile_total, m.tile_expert = sb("tile_total", [1, 1], I32), sb("tile_expert", [1, MAX_TILES + 2], I32)
        m.tile_row, m.row_f = sb("tile_row", [1, MAX_TILES + 2], I32), sb("row_f", [P, 2, NT])
        m.raw_loaded, m.w_high, m.y_ready = sem("ex_raw_loaded"), sem("ex_w_high"), sem("ex_y_ready")
        m.lower_got = sem("ex_lower_got")
        m.w_ready = [sem("ex_w_ready0"), sem("ex_w_ready1")]
        m.bn_scale, m.bn_shift = sb("bn_scale", [P, CB]), sb("bn_shift", [P, CB])
        m.w_mix = sb("w_mix", [P, CB, C])
        m.wr, m.br = sb("wr", [P, CB, NX]), sb("br", [1, NX])
        m.ln_g, m.ln_b = sb("ln_g", [P, CB, NX]), sb("ln_b", [P, CB, NX])
        m.b1 = sb("b1", [P, HB, NX])
        m.b_out = sb("b_out", [1, C])
        loads = [(m.wr[:, :, :], d.Wr.rearrange("(c p) e -> p c e", p=P)), (m.br[:, :], d.br),
                 (m.ln_g[:, :, :], d.ln_g), (m.ln_b[:, :, :], d.ln_b), (m.b1[:, :, :], d.b1), (m.b_out[:, :], d.b_out)]
        with ExitStack() as early:
            esb, _, _ = make_tools(nc, early)
            m.xT = esb("xT", [P, CB, NP])
            m.agg = esb("agg", [P, CB, AGW])
            with ExitStack() as convs:
                csb, _, _ = make_tools(nc, convs)
                m.src = csb("src", [P, NCH], U32)
                m.dst, m.ew = csb("dst", [P, NCH]), csb("ew", [P, NCH])
                m.base, m.extra = csb("base", [1, NGP], I32), csb("extra", [1, NGP], I32)
                m.extra_sum_f, m.extra_sum = csb("extra_sum_f", [1, NGP + 1]), csb("extra_sum", [1, NGP + 1], I32)
                m.w_kv = csb("w_kv", [P, CB, 2 * INNER])
                m.w_q = csb("w_q", [P, INNER // P, C])
                m.w_out = csb("w_out", [P, INNER // P, C])
                m.dots = csb("dots", [P, INNER // P, P])
                m.w1 = [csb(f"w1_{i}", [P, CB, C]) for i in range(2)]
                m.b1c = [csb(f"b1_{i}", [P, C]) for i in range(2)]
                m.w2 = [csb(f"w2_{i}", [P, CB, C]) for i in range(2)]
                vecs = csb("vecs", [P, 2, 5, CB])
                m.b2 = [vecs[:, i, 0, :] for i in range(2)]
                m.gains = [[(vecs[:, i, 1 + 2 * n, :], vecs[:, i, 2 + 2 * n, :]) for n in range(2)] for i in range(2)]
                m.x = m.agg[:, :, :].rearrange("p b n -> p (b n)")[:, 0:NT * C].rearrange("p (t c) -> p t c", c=C)
                m.weight_loads = loads + [
                    (m.w_kv[:, :, :], d.w_qkv[:, INNER:3 * INNER].rearrange("(c p) n -> p c n", p=P)),
                    (m.w_q[:, :, :], d.w_qT.rearrange("(b p) c -> p b c", p=P)),
                    (m.w_out[:, :, :], d.w_out.rearrange("(b p) c -> p b c", p=P))]
                for i in range(2):
                    m.weight_loads += [(m.w1[i][:, :, :], d.cw1[i].rearrange("(c p) n -> p c n", p=P)), (m.b1c[i][:, :], d.cb1[i].to_broadcast([P, C])),
                                       (m.w2[i][:, :, :], d.cw2[i].rearrange("(c p) n -> p c n", p=P))]
                    for n, v in enumerate(d.cvecs[i]):
                        m.weight_loads.append((vecs[:, i, n, :], v))
                start_stage(nc, d, m)
                for layer in range(2):
                    if layer:
                        hidden_stage(nc, d, m, m.w1[layer], m.b1c[layer])
                    gather_stage(nc, d, m, mix=layer == 0)
                    batch_norm_stage(nc, d, m, layer, layer == 1)
            route_stage(nc, d, m)
        with ExitStack() as late:
            lsb, _, _ = make_tools(nc, late)
            m.experts = expert_weights(lsb)
            m.raw1, m.raw2 = lsb("raw1", [P, CB, HID])[:, :, :], lsb("raw2", [P, HB, C])[:, :, :]
            m.lower = lsb("lower", [P, NT, C])
            expert_stage(nc, d, m)
            combine_stage(nc, d, m)


def kernel(**inputs):
    from concourse import bacc
    from concourse.bass_utils import run_bass_kernel_spmd

    nc = bacc.Bacc("TRN2", target_bir_lowering=False, num_devices=1)
    g = "L0_gnn_"
    arrays = {}
    d = Named()

    def give(name, array):
        array = np.ascontiguousarray(array)
        arrays[name] = array
        return nc.dram_tensor(name, array.shape, mybir.dt.from_np(array.dtype), kind="ExternalInput").ap()

    def raw(name):
        return np.asarray(inputs[name])

    def edges(name, mode):
        return np.pad(raw(name), (0, NCH * P - E), mode=mode)

    def channels(array):
        return np.moveaxis(array.reshape(array.shape[:-1] + (array.shape[-1] // P, P)), -1, 0)

    d.x = give("x", raw("x"))
    dst = edges("dst", "edge")
    d.dst_rows = give("dst_rows", dst.reshape(NGP // 4, 4, GE))
    d.dst_cols = give("dst_cols", dst.reshape(NCH, P).T)
    d.src_cols = give("src_cols", edges("src", "edge").reshape(NCH, P).T.view(np.uint32))
    d.ew_cols = give("ew_cols", edges("edge_weight", "constant").reshape(NCH, P).T)
    d.cw1 = [give(f"c{i}_w1", raw(f"{g}c{i}_w1")) for i in (1, 2)]
    d.cb1 = [give(f"c{i}_b1", raw(f"{g}c{i}_b1")[None]) for i in (1, 2)]
    d.cw2 = [give(f"c{i}_w2", raw(f"{g}c{i}_w2")) for i in (1, 2)]
    d.cvecs = [[give(n, channels(raw(g + n))) for n in (f"c{i}_b2", f"c{i}_g", f"c{i}_b", f"bn{i}_g", f"bn{i}_b")] for i in (1, 2)]
    d.w_qkv = give("w_qkv", raw("L0_mix_w_qkv"))
    d.w_qT = give("w_qT", raw("L0_mix_w_qkv")[:, 0:INNER].T)
    d.w_out = give("w_out", raw("L0_mix_w_out"))
    d.b_out = give("b_out", raw("L0_mix_b_out")[None])
    d.Wr = give("Wr", raw("L0_ffn_Wr"))
    d.br = give("br", raw("L0_ffn_br")[None])
    d.ln_g = give("ln_g", np.moveaxis(channels(raw("L0_ffn_ln_g")), 1, 2))
    d.ln_b = give("ln_b", np.moveaxis(channels(raw("L0_ffn_ln_b")), 1, 2))
    d.W1 = give("W1", raw("L0_ffn_W1"))
    d.b1 = give("b1", np.moveaxis(channels(raw("L0_ffn_b1")), 1, 2))
    d.W2 = give("W2", raw("L0_ffn_W2"))
    d.b2 = give("b2", raw("L0_ffn_b2"))
    d.out = nc.dram_tensor("out", (N, C), F32, kind="ExternalOutput").ap()
    d.spans = nc.dram_tensor("spans", (2, NGP), I32, kind="Internal").ap()
    d.h = nc.dram_tensor("h", (NP, C), F32, kind="Internal").ap()
    d.x_mixed = nc.dram_tensor("x_mixed", (N, C), F32, kind="Internal").ap()
    d.x2 = nc.dram_tensor("x2", (N, C), F32, kind="Internal").ap()
    d.routed = nc.dram_tensor("routed", (NX * CAP, C), F32, kind="Internal").ap()
    d.expert_out = nc.dram_tensor("expert_out", (ROWS, C), F32, kind="Internal").ap()
    build(nc, d)
    r = run_bass_kernel_spmd(nc, [arrays], core_ids=[0])
    return r.results[0]["out"]
```
